# Optimizing a Trainium2 kernel written in Bass

```python
import numpy as np
import jax
import jax.numpy as jnp

def _softmax(x, axis=-1):
    return jax.nn.softmax(x, axis=axis)

def _gelu(x):
    return jax.nn.gelu(x, approximate=True)

def _silu(x):
    return jax.nn.silu(x)

def _sigmoid(x):
    return jax.nn.sigmoid(x)

def _layernorm(x, axis=-1, eps=1e-05):
    m = jnp.mean(x, axis=axis, keepdims=True)
    v = jnp.var(x, axis=axis, keepdims=True)
    return (x - m) / jnp.sqrt(v + eps)

def _scatter_add(tgt, idx, src, axis=0):
    return tgt.at[idx].add(src)

def _segment_sum(src, seg, n):
    return jax.ops.segment_sum(src, seg, n)
kernel_name = 'mk_gnn_resnorm_d2_gnn_r8_2baa54'

def setup_inputs(seed: int=0):
    np.random.seed(seed)
    _w = jnp.asarray

    def _rec_inputs():
        import jax
        import jax.numpy as jnp
        _gk = jax.random.key(seed)
        x = -0.0003713 + 1 * jax.random.normal(jax.random.fold_in(_gk, 1), (12500, 128), jnp.float32)
        _s = jax.random.randint(jax.random.fold_in(_gk, 2), (200000,), 0, 12500, jnp.int32)
        _d = jax.random.randint(jax.random.fold_in(_gk, 3), (200000,), 0, 12500, jnp.int32)
        _loop = jnp.arange(12500, dtype=jnp.int32)
        src = jnp.concatenate([_s, _d, _loop])
        dst = jnp.concatenate([_d, _s, _loop])
        _o = jnp.argsort(dst, stable=True)
        src = src[_o]
        dst = dst[_o]
        edge_attr_4 = 0.00109026 + 0.999989 * jax.random.normal(jax.random.fold_in(_gk, 12), (412500, 4), jnp.float32)
        edge_attr_64 = 0.000103221 + 1.00003 * jax.random.normal(jax.random.fold_in(_gk, 13), (412500, 64), jnp.float32)
        node_vec1 = jax.random.uniform(jax.random.fold_in(_gk, 15), (12500, 1), jnp.float32, 0.0, 1)
        return (x, src, dst, edge_attr_4, edge_attr_64, node_vec1)
    x, src, dst, edge_attr_4, edge_attr_64, node_vec1 = _rec_inputs()

    def _L0_gnn_setup():
        import jax, jax.numpy as jnp
        import numpy as np
        N = 12500
        E = 200000
        D_IN = 128
        D_H = 128
        PROP_STEP = 2

        def _degree_norms(src, dst):
            ones = jnp.ones((src.shape[0],), dtype=jnp.float32)
            deg_out = jax.ops.segment_sum(ones, src, num_segments=N)
            deg_in = jax.ops.segment_sum(ones, dst, num_segments=N)
            dout = jnp.maximum(deg_out, 1.0) ** (-0.5)
            din = jnp.maximum(deg_in, 1.0) ** (-0.5)
            return (dout, din)

        def _gcn_conv(x, src, dst, dout, din, W, b):
            m = (x * dout[:, None])[src]
            agg = jax.ops.segment_sum(m, dst, num_segments=N)
            return agg * din[:, None] @ W + b
        key = jax.random.key(seed)
        k = jax.random.split(key, 6)
        in_feat = jax.random.normal(k[0], (N, D_IN), dtype=jnp.float32)
        edge_index = jax.random.randint(k[1], (2, E), 0, N, dtype=jnp.int64)
        s1 = 1.0 / np.sqrt(D_IN)
        s2 = 1.0 / np.sqrt(D_H)
        W1 = jax.random.normal(k[2], (D_IN, D_H), dtype=jnp.float32) * s1
        b1 = jnp.zeros((D_H,), dtype=jnp.float32)
        W2 = jax.random.normal(k[3], (D_H, D_H), dtype=jnp.float32) * s2
        b2 = jnp.zeros((D_H,), dtype=jnp.float32)
        return {'in_feat': in_feat, 'edge_index': edge_index, 'W1': W1, 'b1': b1, 'W2': W2, 'b2': b2}
    _L0_gnn_all = _L0_gnn_setup()
    _L0_gnn_in = {k: v for k, v in _L0_gnn_all.items() if k in ('W1', 'b1', 'W2', 'b2')}
    del _L0_gnn_all

    def _L1_gnn_setup():
        import jax, jax.numpy as jnp
        import numpy as np
        MUL = 32
        N_NODES = 6250
        N_EDGES = 100000
        NUM_NEIGHBORS = 16.0
        SQRT3 = 3.0 ** 0.5
        SILU_NORM = 1.679

        def split_irreps(x):
            x0 = x[..., :MUL]
            x1 = x[..., MUL:].reshape(x.shape[:-1] + (MUL, 3))
            return (x0, x1)

        def merge_irreps(x0, x1):
            return jnp.concatenate([x0, x1.reshape(x1.shape[:-2] + (MUL * 3,))], axis=-1)

        def fctp_scalar(x0, x1, a, W0, W1, fan_in):
            s = a / jnp.sqrt(jnp.asarray(fan_in, x0.dtype))
            o0 = x0 @ W0 * s
            o1 = jnp.einsum('nud,uw->nwd', x1, W1) * s[..., None]
            return (o0, o1)
        key = jax.random.key(seed)
        ks = jax.random.split(key, 17)
        inp = dict(node_input=jax.random.normal(ks[0], (N_NODES, 4 * MUL), jnp.float32), node_attr=jnp.ones((N_NODES, 1), jnp.float32), edge_src=jax.random.randint(ks[1], (N_EDGES,), 0, N_NODES), edge_dst=jax.random.randint(ks[2], (N_EDGES,), 0, N_NODES), edge_attr=jax.random.normal(ks[3], (N_EDGES, 4), jnp.float32), edge_scalars=jax.random.normal(ks[4], (N_EDGES, 64), jnp.float32))
        p = lambda k, sh: jax.random.normal(k, sh, jnp.float32)
        inp.update(W_sc0=p(ks[5], (MUL, MUL)), W_sc1=p(ks[6], (MUL, MUL)), W_l1_0=p(ks[7], (MUL, MUL)), W_l1_1=p(ks[8], (MUL, MUL)), W_fc1=p(ks[9], (64, 64)), W_fc2=p(ks[10], (64, 4 * MUL)), W_l2_A0=p(ks[11], (MUL, MUL)), W_l2_B0=p(ks[12], (MUL, MUL)), W_l2_C1=p(ks[13], (MUL, MUL)), W_l2_D1=p(ks[14], (MUL, MUL)), W_l3_A=p(ks[15], (MUL, 1)), W_l3_B=p(ks[16], (MUL, 1)))
        return inp
    _L1_gnn_all = _L1_gnn_setup()
    _L1_gnn_in = {k: v for k, v in _L1_gnn_all.items() if k in ('W_sc0', 'W_sc1', 'W_l1_0', 'W_l1_1', 'W_fc1', 'W_fc2', 'W_l2_A0', 'W_l2_B0', 'W_l2_C1', 'W_l2_D1', 'W_l3_A', 'W_l3_B')}
    del _L1_gnn_all
    return {'x': x, 'src': src, 'dst': dst, 'edge_attr_4': edge_attr_4, 'edge_attr_64': edge_attr_64, 'node_vec1': node_vec1, 'L0_gnn_W1': _L0_gnn_in['W1'], 'L0_gnn_b1': _L0_gnn_in['b1'], 'L0_gnn_W2': _L0_gnn_in['W2'], 'L0_gnn_b2': _L0_gnn_in['b2'], 'L1_gnn_W_sc0': _L1_gnn_in['W_sc0'], 'L1_gnn_W_sc1': _L1_gnn_in['W_sc1'], 'L1_gnn_W_l1_0': _L1_gnn_in['W_l1_0'], 'L1_gnn_W_l1_1': _L1_gnn_in['W_l1_1'], 'L1_gnn_W_fc1': _L1_gnn_in['W_fc1'], 'L1_gnn_W_fc2': _L1_gnn_in['W_fc2'], 'L1_gnn_W_l2_A0': _L1_gnn_in['W_l2_A0'], 'L1_gnn_W_l2_B0': _L1_gnn_in['W_l2_B0'], 'L1_gnn_W_l2_C1': _L1_gnn_in['W_l2_C1'], 'L1_gnn_W_l2_D1': _L1_gnn_in['W_l2_D1'], 'L1_gnn_W_l3_A': _L1_gnn_in['W_l3_A'], 'L1_gnn_W_l3_B': _L1_gnn_in['W_l3_B']}

def reference(x, src, dst, edge_attr_4, edge_attr_64, node_vec1, L0_gnn_W1, L0_gnn_b1, L0_gnn_W2, L0_gnn_b2, L1_gnn_W_sc0, L1_gnn_W_sc1, L1_gnn_W_l1_0, L1_gnn_W_l1_1, L1_gnn_W_fc1, L1_gnn_W_fc2, L1_gnn_W_l2_A0, L1_gnn_W_l2_B0, L1_gnn_W_l2_C1, L1_gnn_W_l2_D1, L1_gnn_W_l3_A, L1_gnn_W_l3_B):
    import jax
    import jax.numpy as jnp

    def _L0_gnn_ref(in_feat, edge_index, W1, b1, W2, b2):
        import jax, jax.numpy as jnp
        import numpy as np
        N = 12500
        E = 200000
        D_IN = 128
        D_H = 128
        PROP_STEP = 2

        def _degree_norms(src, dst):
            ones = jnp.ones((src.shape[0],), dtype=jnp.float32)
            deg_out = jax.ops.segment_sum(ones, src, num_segments=N)
            deg_in = jax.ops.segment_sum(ones, dst, num_segments=N)
            dout = jnp.maximum(deg_out, 1.0) ** (-0.5)
            din = jnp.maximum(deg_in, 1.0) ** (-0.5)
            return (dout, din)

        def _gcn_conv(x, src, dst, dout, din, W, b):
            m = (x * dout[:, None])[src]
            agg = jax.ops.segment_sum(m, dst, num_segments=N)
            return agg * din[:, None] @ W + b
        src, dst = (edge_index[0], edge_index[1])
        dout, din = _degree_norms(src, dst)
        h = _gcn_conv(in_feat, src, dst, dout, din, W1, b1)
        for _ in range(1, PROP_STEP):
            h = _gcn_conv(h, src, dst, dout, din, W2, b2)
        return h

    def _L1_gnn_ref(node_input, node_attr, edge_src, edge_dst, edge_attr, edge_scalars, W_sc0, W_sc1, W_l1_0, W_l1_1, W_fc1, W_fc2, W_l2_A0, W_l2_B0, W_l2_C1, W_l2_D1, W_l3_A, W_l3_B):
        import jax, jax.numpy as jnp
        import numpy as np
        MUL = 32
        N_NODES = 6250
        N_EDGES = 100000
        NUM_NEIGHBORS = 16.0
        SQRT3 = 3.0 ** 0.5
        SILU_NORM = 1.679

        def split_irreps(x):
            x0 = x[..., :MUL]
            x1 = x[..., MUL:].reshape(x.shape[:-1] + (MUL, 3))
            return (x0, x1)

        def merge_irreps(x0, x1):
            return jnp.concatenate([x0, x1.reshape(x1.shape[:-2] + (MUL * 3,))], axis=-1)

        def fctp_scalar(x0, x1, a, W0, W1, fan_in):
            s = a / jnp.sqrt(jnp.asarray(fan_in, x0.dtype))
            o0 = x0 @ W0 * s
            o1 = jnp.einsum('nud,uw->nwd', x1, W1) * s[..., None]
            return (o0, o1)
        n = node_input.shape[0]
        x0, x1 = split_irreps(node_input)
        h = SILU_NORM * jax.nn.silu(edge_scalars @ (W_fc1 / 8.0))
        weight = h @ (W_fc2 / 8.0)
        sc0, sc1 = fctp_scalar(x0, x1, node_attr, W_sc0, W_sc1, MUL)
        f0, f1 = fctp_scalar(x0, x1, node_attr, W_l1_0, W_l1_1, MUL)
        g0 = f0[edge_src]
        g1 = f1[edge_src]
        e0 = edge_attr[:, :1]
        e1 = edge_attr[:, 1:]
        wA, wC, wD, wB = (weight[:, :MUL], weight[:, MUL:2 * MUL], weight[:, 2 * MUL:3 * MUL], weight[:, 3 * MUL:])
        outA = wA * g0 * e0
        outB = wB * jnp.einsum('euk,ek->eu', g1, e1) / SQRT3
        outC = (wC * g0)[..., None] * e1[:, None, :]
        outD = wD[..., None] * g1 * e0[..., None]
        seg = lambda v: jax.ops.segment_sum(v, edge_dst, num_segments=n)
        inv = 1.0 / jnp.sqrt(jnp.asarray(NUM_NEIGHBORS, node_input.dtype))
        mA, mB, mC, mD = (seg(outA) * inv, seg(outB) * inv, seg(outC) * inv, seg(outD) * inv)
        s = node_attr / 8.0
        c0 = (mA @ W_l2_A0 + mB @ W_l2_B0) * s
        c1 = (jnp.einsum('nud,uw->nwd', mC, W_l2_C1) + jnp.einsum('nud,uw->nwd', mD, W_l2_D1)) * s[..., None]
        angle = 0.1 * (mA @ W_l3_A + mB @ W_l3_B) * s
        cos, sin = (jnp.cos(angle), jnp.sin(angle))
        return cos * merge_irreps(sc0, sc1) + sin * merge_irreps(c0, c1)
    edge_index = jnp.stack([src, dst])
    x = _layernorm(x + _L0_gnn_ref(x, edge_index, L0_gnn_W1, L0_gnn_b1, L0_gnn_W2, L0_gnn_b2), axis=-1)
    x = _layernorm(x + _L1_gnn_ref(x, node_vec1, src, dst, edge_attr_4, edge_attr_64, L1_gnn_W_sc0, L1_gnn_W_sc1, L1_gnn_W_l1_0, L1_gnn_W_l1_1, L1_gnn_W_fc1, L1_gnn_W_fc2, L1_gnn_W_l2_A0, L1_gnn_W_l2_B0, L1_gnn_W_l2_C1, L1_gnn_W_l2_D1, L1_gnn_W_l3_A, L1_gnn_W_l3_B), axis=-1)
    return x

_drawn_inputs = setup_inputs


def setup_inputs(seed=0):
    import zlib

    import numpy as np

    out = dict(_drawn_inputs(seed))
    spreads = {'L0_gnn_b1': (0.0, 0.1), 'L0_gnn_b2': (0.0, 0.1)}
    factors = {'edge_attr_4': 2.798,
     'edge_attr_64': 2.788,
     'L1_gnn_W_l1_0': 3.378,
     'L1_gnn_W_l1_1': 3.021,
     'L1_gnn_W_fc1': 2.822,
     'L1_gnn_W_fc2': 2.771,
     'L1_gnn_W_l2_A0': 7.547,
     'L1_gnn_W_l2_B0': 8.0,
     'L1_gnn_W_l2_C1': 4.421,
     'L1_gnn_W_l2_D1': 4.667,
     'L1_gnn_W_l3_A': 4.381,
     'L1_gnn_W_l3_B': 2.967,
     'L1_gnn_W_sc0': 5.346,
     'L1_gnn_W_sc1': 3.109}
    for name, (base, spread) in spreads.items():
        noise = np.random.default_rng([zlib.crc32(name.encode()), seed]).standard_normal(out[name].shape)
        drawn = base * np.exp(spread * noise) if base else spread * noise
        out[name] = jnp.asarray(drawn.astype(out[name].dtype))
    for name, factor in factors.items():
        out[name] = (out[name] * factor).astype(out[name].dtype)
    return out
```

```python
from contextlib import ExitStack

import numpy as np
import concourse.bass as bass
from concourse import mybir
from concourse.alu_op_type import AluOpType as ALU

ACT = mybir.ActivationFunctionType
AX = mybir.AxisListType
F32 = mybir.dt.float32
BF16 = mybir.dt.bfloat16
I32 = mybir.dt.int32

P = 128
N = 12500
E = 412500
D = 128
MUL = 32
ES = 64
NB = -(-N // P)
TAIL = N - (NB - 1) * P
T = 8
GE = P * T
NG = -(-E // GE)
SLOTS = 4
FAR = 1 << 14
HP = 125
HC = E // HP
HT = 22
NCH = HC // HT
TC = -(-NG // P)
QB = 4
NQ = (NB - 1) // QB
EPS = 1e-5
K_MSG = 1.679 / 8.0 / 4.0 / 8.0
K_DOT = K_MSG / 3.0 ** 0.5
K_F = 1.0 / 32.0 ** 0.5
PI = float(np.pi)
ROUND = 1.5 * 2.0 ** 23
TAU_A = 6.28125
TAU_B = float(np.float32(np.floor((2 * np.pi - TAU_A) * 2.0 ** 21) / 2.0 ** 21))
TAU_C = float(np.float32(2 * np.pi - TAU_A - TAU_B))


def split_groups(engine, body):
    rounds = NG // SLOTS
    for g in range(SLOTS):
        body(g, g, 0)
    with engine.Fori(1, rounds) as r:
        for s in range(SLOTS):
            body(r * SLOTS + s, s, r)
    for g in range(rounds * SLOTS, NG):
        body(g, g % SLOTS, rounds)


def node_steps(engine, body):
    full = [P] * QB
    body(0, 0, full)
    body(1, 1, full)
    with engine.Fori(1, NQ // 2) as h:
        for j in range(2):
            body(h * 2 + j, j, full)
    body(NQ, NQ % 2, [P] * (NB - 1 - NQ * QB) + [TAIL])


def rows_of(dram, step, blocks):
    if blocks[-1] == P:
        return [(slice(0, P), slice(0, len(blocks)),
                 dram[bass.ds(step * (QB * P), QB * P), :].rearrange("(s p) d -> p s d", p=P))]
    out = []
    for j, n in enumerate(blocks):
        r0 = (step * QB + j) * P
        out.append((slice(0, n), slice(j, j + 1), dram[r0:r0 + n, :].rearrange("(s p) d -> p s d", s=1)))
    return out


def later(g, n):
    return not isinstance(g, int) or g >= n


def worked_out(engine, reg, value):
    if isinstance(value, int):
        return value
    engine.reg_mov(reg, value)
    return reg


class Bounds:

    def __init__(self, engine, name, c):
        self.engine, self.c = engine, c
        self.pairs = [[engine.alloc_register(f"{name}_{p}{i}") for i in range(4)] for p in "ab"]

    def load(self, g, pair):
        self.engine.load(self.pairs[pair], self.c.bounds[0:1, bass.ds(g * 2, 4)])

    def load_next(self, g, slot):
        if slot % 2 == 1 and (not isinstance(g, int) or g + 1 < NG):
            self.load(g + 1, (slot // 2 + 1) % 2)

    def of(self, slot):
        pair = self.pairs[slot // 2]
        return pair[slot % 2 * 2], pair[slot % 2 * 2 + 1]


def constants(nc, c, w):
    ctx = ExitStack()
    with ctx:
        def sb(name, shape, dt=F32):
            return ctx.enter_context(nc.sbuf_tensor(name, shape, dt))

        def sem(name):
            return ctx.enter_context(nc.semaphore(name))

        iota_i = sb("iota_i", [P, P], I32)
        col_i = sb("col_i", [P, 1], I32)
        col = sb("col", [P, 1])
        vec_i = sb("vec_i", [P, 3, MUL], I32)
        vec_hit = sb("vec_hit", [P, 3, MUL])
        vec_mask = sb("vec_mask", [P, 3])
        quad_i = sb("quad_i", [P, 4], I32)
        quad_ge = sb("quad_ge", [P, 4])
        quad_mask = sb("quad_mask", [P, 4])
        w_f = sb("w_f", [P, MUL])
        w_sc = sb("w_sc", [P, MUL])
        w_ad = sb("w_ad", [P, MUL])
        w_bc = sb("w_bc", [P, MUL])
        l3 = sb("l3", [P, 2])
        loaded = sem("weights_loaded")
        iotas = sem("iotas_made")
        cleared = sem("weights_cleared")
        made = sem("masks_made")
        n_loads = [0]

        with nc.Block() as block:
            @block.gpsimd
            def _(pool):
                pool.iota(iota_i[:], [[1, P]], base=0, channel_multiplier=0).then_inc(iotas, 1)
                pool.iota(col_i[:], [[1, 1]], base=0, channel_multiplier=1).then_inc(iotas, 1)
                pool.iota(vec_i[:], [[1, 3], [3, MUL]], base=MUL, channel_multiplier=-1).then_inc(iotas, 1)
                pool.iota(quad_i[:], [[-MUL, 4]], base=0, channel_multiplier=1).then_inc(iotas, 1)

            @block.sync
            def _(sp):
                def load(dst, src):
                    n_loads[0] += 1
                    sp.dma_start(dst, src).then_inc(loaded, 16)

                load(c.w1[:], w["L0_gnn_W1"])
                load(c.w2[:], w["L0_gnn_W2"])
                load(c.b1[:], w["L0_gnn_b1"].partition_broadcast(P))
                load(c.b2[:], w["L0_gnn_b2"].partition_broadcast(P))
                load(w_f[0:MUL, :], w["L1_gnn_W_l1_0"])
                load(w_sc[0:MUL, :], w["L1_gnn_W_sc0"])
                for dst, name in ((w_f, "L1_gnn_W_l1_1"), (w_sc, "L1_gnn_W_sc1")):
                    src = w[name]
                    load(dst[MUL:P, :], bass.AP(tensor=src.tensor, offset=src.offset,
                                                ap=[[MUL, MUL], [0, 3], [1, MUL]]))
                load(w_ad[0:MUL, :], w["L1_gnn_W_l2_A0"])
                load(w_bc[0:MUL, :], w["L1_gnn_W_l2_B0"])
                for k in range(3):
                    rows = slice(MUL * (k + 1), MUL * (k + 2))
                    load(w_ad[rows, :], w["L1_gnn_W_l2_D1"])
                    load(w_bc[rows, :], w["L1_gnn_W_l2_C1"])
                sp.wait_ge(cleared, 1)
                load(l3[0:MUL, 0:1], w["L1_gnn_W_l3_A"])
                load(l3[0:MUL, 1:2], w["L1_gnn_W_l3_B"])
                for i in range(2):
                    half = slice(ES * i, ES * (i + 1))
                    load(c.w_fc1[half, half], w["L1_gnn_W_fc1"])
                    for to, at in enumerate((0, 2, 1, 3)):
                        load(c.w_fc2[half, P * i + MUL * to:P * i + MUL * (to + 1)],
                             w["L1_gnn_W_fc2"][:, MUL * at:MUL * (at + 1)])

            @block.vector
            def _(dve):
                dve.memset(l3[:], 0.0)
                dve.memset(c.w_fc1[:], 0.0)
                dve.memset(c.w_fc2[:], 0.0).then_inc(cleared, 1)
                dve.memset(c.one_row[:], 1.0)
                dve.wait_ge(iotas, 4)
                dve.tensor_copy(c.iota[:], iota_i[:]).then_inc(made, 1)
                dve.tensor_copy(col[:], col_i[:]).then_inc(made, 1)
                dve.tensor_scalar(vec_hit[:], vec_i[:], 0.0, None, ALU.is_equal).then_inc(made, 1)
                dve.tensor_scalar(quad_ge[:], quad_i[:], 0.0, None, ALU.is_ge).then_inc(made, 1)
                dve.wait_ge(made, 4)
                dve.tensor_scalar(c.ident[:], c.iota[:], col[:, 0:1], None, ALU.is_equal)
                dve.tensor_reduce(vec_mask[:], vec_hit[:], AX.X, ALU.add).then_inc(made, 1)
                dve.scalar_tensor_tensor(quad_mask[:], quad_i[:], float(MUL), quad_ge[:],
                                         ALU.is_lt, ALU.mult).then_inc(made, 1)
                dve.wait_ge(made, 6)
                dve.wait_ge(loaded, 16 * n_loads[0])
                dve.tensor_scalar(c.w_node[:, 0:MUL], w_f[:], quad_mask[:, 0:1], K_F, ALU.mult, ALU.mult)
                dve.tensor_scalar(c.w_node[:, D:D + MUL], w_sc[:], quad_mask[:, 0:1], K_F, ALU.mult, ALU.mult)
                for k in range(3):
                    at = MUL * (k + 1)
                    out = slice(MUL + k, D, 3)
                    dve.tensor_scalar(c.w_node[:, at:at + MUL], w_f[:], vec_mask[:, k:k + 1], K_F,
                                      ALU.mult, ALU.mult)
                    dve.tensor_scalar(c.w_node[:, D + MUL + k:2 * D:3], w_sc[:], vec_mask[:, k:k + 1], K_F,
                                      ALU.mult, ALU.mult)
                    dve.tensor_scalar(c.w_ad[:, out], w_ad[:], quad_mask[:, k + 1:k + 2], K_MSG,
                                      ALU.mult, ALU.mult)
                    dve.tensor_scalar(c.w_bc[:, out], w_bc[:], quad_mask[:, k + 1:k + 2], K_MSG,
                                      ALU.mult, ALU.mult)
                dve.tensor_scalar(c.w_ad[:, 0:MUL], w_ad[:], quad_mask[:, 0:1], K_MSG, ALU.mult, ALU.mult)
                dve.tensor_scalar(c.w_bc[:, 0:MUL], w_bc[:], quad_mask[:, 0:1], K_DOT, ALU.mult, ALU.mult)
                dve.tensor_scalar(c.w_ad[:, D:D + 1], l3[:, 0:1], 0.1 * K_MSG, None, ALU.mult)
                dve.tensor_scalar(c.w_bc[:, D:D + 1], l3[:, 1:2], 0.1 * K_DOT, None, ALU.mult)


def bounds_table(nc, c, dst_groups, bounds_dram, base_dram):
    ctx = ExitStack()
    with ctx:
        def sb(name, shape, dt=F32):
            return ctx.enter_context(nc.sbuf_tensor(name, shape, dt))

        def sem(name):
            return ctx.enter_context(nc.semaphore(name))

        dst = sb("bt_dst", [P, TC, GE], I32)
        least = sb("bt_least", [P, TC], I32)
        most = sb("bt_most", [P, TC], I32)
        most_in = sb("bt_most_in", [P, TC], I32)
        most_block = sb("bt_most_block", [P, TC], I32)
        bounds = sb("bt_bounds", [P, TC, 2], I32)
        base = sb("bt_base", [P, TC])
        landed = sem("bt_landed")
        step = sem("bt_step")
        stored = sem("bt_stored")
        done = sem("bt_back")
        counts = [min(P, NG - P * i) for i in range(TC)]

        with nc.Block() as block:
            @block.sync
            def _(sp):
                for i, n in enumerate(counts):
                    sp.dma_start(dst[0:n, i, :], dst_groups[P * i:P * i + n, :]).then_inc(landed, 16)
                sp.wait_ge(step, 7)
                with nc.allow_non_contiguous_dma(reason="a table of a few numbers per partition"):
                    sp.dma_start(bounds_dram.rearrange("(c p) e -> p c e", p=P), bounds[:]).then_inc(stored, 16)
                    sp.dma_start(base_dram.rearrange("(c p) -> p c", p=P), base[:]).then_inc(stored, 16)
                sp.wait_ge(stored, 32)
                sp.dma_start(c.bounds[:], bounds_dram.rearrange("(a g) e -> a (g e)", a=1)).then_inc(done, 16)
                sp.dma_start(c.base[:], base_dram.partition_broadcast(P)).then_inc(done, 16)
                sp.wait_ge(done, 32)

            @block.vector
            def _(dve):
                dve.memset(least[:], 0)
                dve.memset(most[:], 0).then_inc(step, 1)
                dve.wait_ge(step, 1)
                dve.wait_ge(landed, 16 * TC)
                for i, n in enumerate(counts):
                    dve.tensor_reduce(least[0:n, i:i + 1], dst[0:n, i, :], AX.X, ALU.min)
                    last = dve.tensor_reduce(most[0:n, i:i + 1], dst[0:n, i, :], AX.X, ALU.max)
                last.then_inc(step, 1)
                dve.wait_ge(step, 2)
                dve.tensor_scalar(most_in[:], most[:], float(NB * P - 1), None, ALU.min).then_inc(step, 1)
                dve.tensor_scalar(bounds[:, :, 0], least[:], 7, None, ALU.arith_shift_right).then_inc(step, 1)
                dve.wait_ge(step, 4)
                dve.tensor_scalar(most_block[:], most_in[:], 7, None, ALU.arith_shift_right).then_inc(step, 1)
                dve.wait_ge(step, 5)
                dve.tensor_scalar(bounds[:, :, 1], most_block[:], 1.0, None, ALU.add).then_inc(step, 1)
                dve.tensor_scalar(base[:], bounds[:, :, 0], float(P), None, ALU.mult).then_inc(step, 1)


def source_degrees(nc, c, src, node_vec):
    ctx = ExitStack()
    with ctx:
        def sb(name, shape, dt=F32):
            return ctx.enter_context(nc.sbuf_tensor(name, shape, dt))

        def sem(name):
            return ctx.enter_context(nc.semaphore(name))

        src_i = sb("h_src", [HP, HC], I32)
        part_i = sb("h_part", [HP, HC], I32)
        hi = sb("h_hi", [HP, HC], BF16)
        lo = sb("h_lo", [HP, HC], BF16)
        iota_t = sb("h_iota", [P, P, HT], BF16)
        one_hi = sb("h_one_hi", [HP, 2, NB, HT], BF16)
        one_lo = sb("h_one_lo", [HP, 2, P, HT], BF16)
        count_rows = sb("h_rows", [NB, P])
        vec_rows = sb("h_vec", [NB, P])
        degree = sb("h_degree", [P, NB])
        root = sb("h_root", [P, NB])
        counts = ctx.enter_context(nc.psum_tensor("h_counts", [NB, 512], F32))
        turned = ctx.enter_context(nc.psum_tensor("h_turned", [P, 512], F32))
        landed = sem("h_landed")
        split = sem("h_split")
        hot = sem("h_hot")
        hot_used = sem("h_hot_used")
        rows_ready = sem("h_rows_ready")
        turned_ready = sem("h_turned_ready")
        degree_ready = sem("h_degree_ready")
        root_ready = sem("h_root_ready")

        with nc.Block() as block:
            @block.sync
            def _(sp):
                sp.dma_start(src_i[:], src.rearrange("(p c) -> p c", p=HP)).then_inc(landed, 16)
                sp.wait_ge(split, 1)
                sp.dma_start(vec_rows[0:NB - 1, :],
                             node_vec[0:(NB - 1) * P, :].rearrange("(b p) e -> b (p e)", p=P)).then_inc(landed, 16)
                sp.dma_start(vec_rows[NB - 1:NB, 0:TAIL],
                             node_vec[(NB - 1) * P:N, :].rearrange("(b p) e -> b (p e)", b=1)).then_inc(landed, 16)

            @block.gpsimd
            def _(pool):
                pool.memset(vec_rows[96:NB, :], 0.0).then_inc(split, 1)

            @block.vector
            def _(dve):
                dve.tensor_copy(iota_t[:], c.iota[:, :, None].to_broadcast([P, P, HT]))
                dve.wait_ge(landed, 48)
                dve.tensor_scalar(part_i[:], src_i[:], 7, None, ALU.arith_shift_right).then_inc(split, 1)
                dve.wait_ge(split, 2)
                dve.tensor_copy(hi[:], part_i[:]).then_inc(split, 1)
                dve.wait_ge(split, 3)
                dve.tensor_scalar(part_i[:], src_i[:], P - 1, None, ALU.bitwise_and).then_inc(split, 1)
                dve.wait_ge(split, 4)
                dve.tensor_copy(lo[:], part_i[:]).then_inc(split, 1)
                dve.wait_ge(split, 5)

                def chunk(i, b):
                    dve.tensor_tensor(one_hi[:, b], hi[:, None, bass.ds(i * HT, HT)].to_broadcast([HP, NB, HT]),
                                      iota_t[0:HP, 0:NB, :], ALU.is_equal)
                    dve.tensor_tensor(one_lo[:, b], lo[:, None, bass.ds(i * HT, HT)].to_broadcast([HP, P, HT]),
                                      iota_t[0:HP, :, :], ALU.is_equal).then_inc(hot, 1)

                chunk(0, 0)
                chunk(1, 1)
                with dve.Fori(1, NCH // 2) as h:
                    for b in range(2):
                        dve.wait_ge(hot_used, h * 2 + (b - 1))
                        chunk(h * 2 + b, b)
                dve.wait_ge(hot_used, NCH)
                dve.tensor_copy(count_rows[:], counts[:, 0:P]).then_inc(rows_ready, 1)
                dve.wait_ge(turned_ready, 1)
                dve.tensor_scalar(degree[:], turned[:, 0:NB], 1.0, None, ALU.max).then_inc(degree_ready, 1)
                dve.tensor_copy(c.node_vec[:], turned[:, P:P + NB])
                dve.wait_ge(root_ready, 1)
                dve.reciprocal(c.dout[:], root[:])

            @block.scalar
            def _(act):
                act.wait_ge(degree_ready, 1)
                act.activation(root[:], degree[:], ACT.Sqrt).then_inc(root_ready, 1)

            @block.tensor
            def _(pe):
                def chunk(i, b, first, last):
                    pe.wait_ge(hot, i + 1)
                    for t in range(HT):
                        mm = pe.matmul(counts[:, 0:P], one_hi[:, b, :, t], one_lo[:, b, :, t],
                                       start=first and t == 0, stop=last and t == HT - 1)
                    mm.then_inc(hot_used, 1)

                chunk(0, 0, True, False)
                chunk(1, 1, False, False)
                with pe.Fori(1, NCH // 2 - 1) as h:
                    for b in range(2):
                        chunk(h * 2 + b, b, False, False)
                chunk(NCH - 2, 0, False, False)
                chunk(NCH - 1, 1, False, True)
                pe.wait_ge(rows_ready, 1)
                pe.wait_ge(landed, 48)
                pe.transpose(turned[:, 0:NB], count_rows[:], c.ident[0:NB, 0:NB])
                pe.transpose(turned[:, P:P + NB], vec_rows[:], c.ident[0:NB, 0:NB]).then_inc(turned_ready, 1)


def scaled_table(nc, c, x, table):
    ctx = ExitStack()
    with ctx:
        xin = ctx.enter_context(nc.sbuf_tensor("s_in", [P, 2, QB, D], F32))
        out = ctx.enter_context(nc.sbuf_tensor("s_out", [P, 2, QB, D], F32))
        landed = [ctx.enter_context(nc.semaphore(f"s_landed{i}")) for i in range(2)]
        stored = [ctx.enter_context(nc.semaphore(f"s_stored{i}")) for i in range(2)]
        tail = ctx.enter_context(nc.semaphore("s_tail"))
        scaled = ctx.enter_context(nc.semaphore("s_scaled"))

        with nc.Block() as block:
            @block.sync
            def _(sp):
                def body(i, b, blocks):
                    if later(i, 2):
                        sp.wait_ge(scaled, i - 1)
                    for p, s, rows in rows_of(x, i, blocks):
                        sp.dma_start(xin[p, b, s], rows).then_inc(tail if blocks[-1] < P else landed[b], 16)
                node_steps(sp, body)

            @block.vector
            def _(dve):
                def body(i, b, blocks):
                    if blocks[-1] < P:
                        dve.wait_ge(tail, 16 * len(blocks))
                    else:
                        dve.wait_ge(landed[b], (i - b) * 8 + 16)
                    if later(i, 2):
                        dve.wait_ge(stored[b], (i - b) * 8)
                    for j, n in enumerate(blocks):
                        mul = dve.tensor_scalar(out[0:n, b, j], xin[0:n, b, j],
                                                c.dout[0:n, bass.ds(i * QB + j, 1)], None, ALU.mult)
                    mul.then_inc(scaled, 1)
                node_steps(dve, body)

            @block.scalar
            def _(act):
                def body(i, b, blocks):
                    act.wait_ge(scaled, i + 1)
                    for p, s, rows in rows_of(table, i, blocks):
                        act.dma_start(rows, out[p, b, s]).then_inc(stored[b], 16)
                node_steps(act, body)
                for b in range(2):
                    steps = (NQ + 1 - b) // 2 + (NB - 1 - NQ * QB if NQ % 2 == b else 0) + (NQ % 2 == b)
                    act.wait_ge(stored[b], 16 * steps)


def convolve_edges(nc, c, name, table, edges, acc, degree_row):
    ctx = ExitStack()
    with ctx:
        def sb(n, shape, dt=F32):
            return ctx.enter_context(nc.sbuf_tensor(f"{name}_{n}", shape, dt))

        def ps(n):
            return ctx.enter_context(nc.psum_tensor(f"{name}_{n}", [P, 512], F32))

        def sem(n):
            return ctx.enter_context(nc.semaphore(f"{name}_{n}"))

        ends = sb("ends", [P, SLOTS, 2 * T], I32)
        rows = sb("rows", [P, SLOTS, T, D])
        rel = sb("rel", [P, T])
        hot = sb("hot", [P, T, P])
        iota = ps("iota")
        sums = ps("sums")
        counts = ps("counts")
        ends_landed = [sem(f"ends_landed{i}") for i in range(SLOTS)]
        rows_landed = [sem(f"rows_landed{i}") for i in range(SLOTS)]
        groups_past = sem("groups_past")
        cleared = sem("cleared")
        rel_ready = sem("rel_ready")
        hot_ready = sem("hot_ready")
        sums_ready = sem("sums_ready")
        sums_added = sem("sums_added")

        with nc.Block() as block:
            @block.sync
            def _(sp):
                past_reg, landed_reg = sp.alloc_register(f"{name}_sp_past"), sp.alloc_register(f"{name}_sp_landed")

                def body(g, slot, r):
                    if later(g, SLOTS):
                        past = worked_out(sp, past_reg, g - (SLOTS - 1))
                        landed = worked_out(sp, landed_reg, r * (16 * T))
                        sp.wait_ge(groups_past, past)
                        sp.wait_ge(rows_landed[slot], landed)
                    sp.dma_start(ends[:, slot, :], edges[bass.ds(g, 1)].rearrange("a p e -> p (a e)")
                                 ).then_inc(ends_landed[slot], 16)
                split_groups(sp, body)

            @block.gpsimd
            def _(pool):
                landed_reg, past_reg = pool.alloc_register(f"{name}_pool_landed"), pool.alloc_register(f"{name}_pool_past")

                def body(g, slot, r):
                    landed = worked_out(pool, landed_reg, r * 16 + 16)
                    past = worked_out(pool, past_reg, g - (SLOTS - 2))
                    pool.wait_ge(ends_landed[0], 16)
                    pool.wait_ge(ends_landed[slot], landed)
                    if later(g, SLOTS):
                        pool.wait_ge(groups_past, past)
                    for t in range(T):
                        pool.indirect_dma_start(
                            out=rows[:, slot, t, :], out_offset=None, in_=table,
                            in_offset=bass.IndirectOffsetOnAxis(ap=ends[:, slot, t:t + 1], axis=0),
                        ).then_inc(rows_landed[slot], 16)
                split_groups(pool, body)

            @block.vector
            def _(dve):
                dve.memset(acc[:], 0.0)
                if degree_row is not None:
                    dve.memset(degree_row[:], 0.0)
                dve.memset(sums[:], 0.0)
                dve.memset(counts[:], 0.0)
                dve.tensor_copy(iota[:, 0:P], c.iota[:]).then_inc(cleared, 1)
                dve.wait_ge(cleared, 1)
                visits = dve.alloc_register(f"{name}_dve_visits")
                rels = dve.alloc_register(f"{name}_dve_rels")
                before = dve.alloc_register(f"{name}_dve_before")
                bounds = Bounds(dve, name + "_dve_bound", c)
                bounds.load(0, 0)
                dve.reg_mov(visits, 0)
                dve.reg_mov(rels, 0)
                dve.reg_mov(before, NB)

                def add_sums():
                    at = dve.snap(before, min_val=0, max_val=NB)
                    dve.wait_ge(sums_ready, visits)
                    dve.wait_ge(sums_added, visits)
                    if degree_row is not None:
                        dve.tensor_tensor(degree_row[:, at, :], degree_row[:, at, :], counts[0:1, 0:P], ALU.add)
                    dve.tensor_tensor(acc[:, at, :], acc[:, at, :], sums[:, 0:P], ALU.add
                                      ).then_inc(sums_added, 1)

                def body(g, slot, r):
                    first, past = bounds.of(slot)
                    dve.wait_ge(ends_landed[slot], r * 16 + 16)
                    dve.wait_ge(rel_ready, rels)
                    dve.tensor_scalar(rel[:], ends[:, slot, T:2 * T], c.base[:, bass.ds(g, 1)], None,
                                      ALU.subtract).then_inc(rel_ready, 1)
                    dve.reg_add(rels, rels, 1)
                    bounds.load_next(g, slot)
                    with dve.Fori(first, past) as blk:
                        add_sums()
                        dve.wait_ge(rel_ready, rels)
                        dve.tensor_tensor(hot[:], iota[:, None, 0:P].to_broadcast([P, T, P]),
                                          rel[:, :, None].to_broadcast([P, T, P]), ALU.is_equal
                                          ).then_inc(hot_ready, 1)
                        dve.reg_add(visits, visits, 1)
                        dve.reg_add(rels, rels, 1)
                        dve.reg_mov(before, blk)
                        dve.wait_ge(hot_ready, visits)
                        dve.tensor_scalar(rel[:], rel[:], float(-P), None, ALU.add).then_inc(rel_ready, 1)
                    dve.sem_inc(groups_past, 1)
                split_groups(dve, body)
                add_sums()

            @block.tensor
            def _(pe):
                visits = pe.alloc_register(f"{name}_pe_visits")
                bounds = Bounds(pe, name + "_pe_bound", c)
                bounds.load(0, 0)
                pe.reg_mov(visits, 1)

                def body(g, slot, r):
                    first, past = bounds.of(slot)
                    bounds.load_next(g, slot)
                    rows_due = pe.snap(r * (16 * T) + 16 * T)
                    with pe.Fori(first, past):
                        pe.wait_ge(rows_landed[slot], rows_due)
                        pe.wait_ge(hot_ready, visits)
                        for t in range(T):
                            mm = pe.matmul(sums[:, 0:P], rows[:, slot, t, :], hot[:, t, :],
                                           start=t == 0, stop=t == T - 1)
                            if degree_row is not None:
                                mm = pe.matmul(counts[0:1, 0:P], c.one_row[:], hot[:, t, :],
                                               start=t == 0, stop=t == T - 1)
                        mm.then_inc(sums_ready, 1)
                        pe.reg_add(visits, visits, 1)
                split_groups(pe, body)


def inward_degrees(nc, c, degree_row, degree_dram):
    ctx = ExitStack()
    with ctx:
        rows = ctx.enter_context(nc.sbuf_tensor("i_rows", [NB, P], F32))
        degree = ctx.enter_context(nc.sbuf_tensor("i_degree", [P, NB], F32))
        root = ctx.enter_context(nc.sbuf_tensor("i_root", [P, NB], F32))
        turned = ctx.enter_context(nc.psum_tensor("i_turned", [P, 512], F32))
        stored, landed, turned_ready, degree_ready, root_ready, din_ready = [
            ctx.enter_context(nc.semaphore("i_" + n))
            for n in ("stored", "landed", "turned_ready", "degree_ready", "root_ready", "din_ready")]

        with nc.Block() as block:
            @block.sync
            def _(sp):
                sp.dma_start(degree_dram.rearrange("(a b) p -> a (b p)", a=1),
                             degree_row[0:1, 0:NB, :].rearrange("a b p -> a (b p)")).then_inc(stored, 16)
                sp.wait_ge(stored, 16)
                sp.dma_start(rows[:], degree_dram).then_inc(landed, 16)

            @block.tensor
            def _(pe):
                pe.wait_ge(landed, 16)
                pe.transpose(turned[:, 0:NB], rows[:], c.ident[0:NB, 0:NB]).then_inc(turned_ready, 1)

            @block.scalar
            def _(act):
                act.wait_ge(degree_ready, 1)
                act.activation(root[:], degree[:], ACT.Sqrt).then_inc(root_ready, 1)

            @block.vector
            def _(dve):
                dve.wait_ge(turned_ready, 1)
                dve.tensor_scalar(degree[:], turned[:, 0:NB], 1.0, None, ALU.max).then_inc(degree_ready, 1)
                dve.wait_ge(root_ready, 1)
                dve.reciprocal(c.din[:], root[:]).then_inc(din_ready, 1)
                dve.wait_ge(din_ready, 1)
                dve.tensor_tensor(c.dinout[:], c.din[:], c.dout[:], ALU.mult)


def first_nodes(nc, c, acc, table):
    ctx = ExitStack()
    with ctx:
        agg = ctx.enter_context(nc.sbuf_tensor("n1_agg", [P, 2, QB, P], F32))
        bias = ctx.enter_context(nc.sbuf_tensor("n1_bias", [P, 2, QB, D], F32))
        out = ctx.enter_context(nc.sbuf_tensor("n1_out", [P, 2, QB, D], F32))
        prod = [ctx.enter_context(nc.psum_tensor(f"n1_prod{b}", [P, QB, D], F32)) for b in range(2)]
        agg_ready, prod_ready, bias_ready, made = [
            ctx.enter_context(nc.semaphore("n1_" + n)) for n in ("agg_ready", "prod_ready", "bias_ready", "made")]
        stored = [ctx.enter_context(nc.semaphore(f"n1_stored{i}")) for i in range(2)]

        with nc.Block() as block:
            @block.scalar
            def _(act):
                def body(i, b, blocks):
                    if later(i, 2):
                        act.wait_ge(prod_ready, i - 1)
                    act.activation(agg[:, b, 0:len(blocks)], acc[:, bass.ds(i * QB, len(blocks)), :],
                                   ACT.Copy).then_inc(agg_ready, 1)
                node_steps(act, body)

            @block.tensor
            def _(pe):
                def body(i, b, blocks):
                    pe.wait_ge(agg_ready, i + 1)
                    if later(i, 2):
                        pe.wait_ge(made, i - 1)
                    for j, n in enumerate(blocks):
                        mm = pe.matmul(prod[b][0:n, j, :], agg[:, b, j, 0:n], c.w1[:], start=True, stop=True)
                    mm.then_inc(prod_ready, 1)
                node_steps(pe, body)

            @block.vector
            def _(dve):
                def body(i, b, blocks):
                    if later(i, 2):
                        dve.wait_ge(stored[b], (i - b) * 8)
                        dve.wait_ge(made, i - 1)
                    for j, n in enumerate(blocks):
                        last = dve.tensor_scalar(bias[0:n, b, j], c.b1[0:n], c.dout[0:n, bass.ds(i * QB + j, 1)],
                                                 None, ALU.mult)
                    last.then_inc(bias_ready, 1)
                    dve.wait_ge(bias_ready, i + 1)
                    dve.wait_ge(prod_ready, i + 1)
                    for j, n in enumerate(blocks):
                        last = dve.scalar_tensor_tensor(out[0:n, b, j], prod[b][0:n, j, :],
                                                        c.dinout[0:n, bass.ds(i * QB + j, 1)], bias[0:n, b, j],
                                                        ALU.mult, ALU.add)
                    last.then_inc(made, 1)
                node_steps(dve, body)

            @block.sync
            def _(sp):
                def body(i, b, blocks):
                    sp.wait_ge(made, i + 1)
                    for p, s, rows in rows_of(table, i, blocks):
                        sp.dma_start(rows, out[p, b, s]).then_inc(stored[b], 16)
                node_steps(sp, body)
                for b in range(2):
                    sp.wait_ge(stored[b], 16 * stores_of(b))


def stores_of(b):
    steps = (NQ - b + 1) // 2
    return steps + (NB - NQ * QB if NQ % 2 == b else 0)


class Chain:

    def __init__(self, engine, sem, base):
        self.engine, self.sem, self.base, self.n = engine, sem, base, 0

    def link(self, ins, reg=None, met=None):
        self.n += 1
        ins.then_inc(self.sem, 1)
        value = self.base + self.n
        if met is not None:
            value = worked_out(self.engine, reg, value)
            self.engine.wait_ge(met, 1)
        self.engine.wait_ge(self.sem, value)


def layernorm(dve, chain, c, y, out, s, blocks, var_ready, root_ready, step):
    for j, n in enumerate(blocks):
        last = dve.bn_stats(s.stats[0:n, j, :], y[0:n, j])
    chain.link(last, s.reg, s.eps_ready)
    for j, n in enumerate(blocks):
        last = dve.bn_aggr(s.mean_var[0:n, j, :], s.stats[0:n, j, :])
    last.then_inc(var_ready, 1)
    dve.wait_ge(root_ready, step + 1)
    chain.link(dve.reciprocal(s.rstd[:, 0:len(blocks)], s.root[:, 0:len(blocks)]))
    for j, n in enumerate(blocks):
        last = dve.tensor_scalar(out[0:n, j], y[0:n, j], s.mean_var[0:n, j, 0:1], s.rstd[0:n, j:j + 1],
                                 ALU.subtract, ALU.mult)
    return last


class Norm:

    def __init__(self, nc, ctx, name):
        sb = lambda n, shape: ctx.enter_context(nc.sbuf_tensor(name + n, shape, F32))
        self.stats = sb("stats", [P, QB, 6])
        self.mean_var = sb("mean_var", [P, QB, 2])
        self.root = sb("root", [P, QB])
        self.rstd = sb("rstd", [P, QB])
        self.eps = sb("eps", [P, 1])
        self.reg = nc.vector.alloc_register(name + "chain_value")


def second_nodes(nc, c, x, acc, x1_dram, table, skip_dram):
    ctx = ExitStack()
    with ctx:
        def sb(n, shape):
            return ctx.enter_context(nc.sbuf_tensor("n2_" + n, shape, F32))

        def sem(n):
            return ctx.enter_context(nc.semaphore("n2_" + n))

        agg = sb("agg", [P, 2, QB, P])
        xin = sb("xin", [P, 2, QB, D])
        y = sb("y", [P, QB, D])
        x1 = sb("x1", [P, 2, QB, D])
        x1t = sb("x1t", [P, 2, QB, P])
        feat = sb("feat", [P, 2, QB, 2 * D])
        s = Norm(nc, ctx, "n2_")
        s.eps_ready = sem("eps_ready")
        prod = [ctx.enter_context(nc.psum_tensor(f"n2_prod{b}", [P, QB, D], F32)) for b in range(2)]
        turned = ctx.enter_context(nc.psum_tensor("n2_turned", [P, QB, P], F32))
        both = [ctx.enter_context(nc.psum_tensor(f"n2_both{h}", [P, 2, 2 * D], F32)) for h in range(2)]
        agg_ready, prod_ready, chain_sem, var_ready, root_ready, x1_ready, turned_ready, x1t_ready = [
            sem(n) for n in ("agg_ready", "prod_ready", "chain", "var_ready", "root_ready", "x1_ready",
                             "turned_ready", "x1t_ready")]
        both_ready, feat_ready, eps_ready, tail = sem("both_ready"), sem("feat_ready"), s.eps_ready, sem("tail")
        landed = [sem(f"landed{i}") for i in range(2)]
        stored = [sem(f"stored{i}") for i in range(2)]
        LINKS = 4

        with nc.Block() as block:
            @block.sync
            def _(sp):
                def body(i, b, blocks):
                    if later(i, 2):
                        sp.wait_ge(x1_ready, i - 1)
                    for p, sl, rows in rows_of(x, i, blocks):
                        sp.dma_start(xin[p, b, sl], rows).then_inc(tail if blocks[-1] < P else landed[b], 16)
                node_steps(sp, body)

            @block.gpsimd
            def _(pool):
                def body(i, b, blocks):
                    pool.wait_ge(eps_ready, 1)
                    pool.wait_ge(x1_ready, i + 1)
                    for p, sl, rows in rows_of(x1_dram, i, blocks):
                        pool.dma_start(rows, x1[p, b, sl]).then_inc(stored[b], 16)
                    pool.wait_ge(eps_ready, 1)
                    pool.wait_ge(feat_ready, i + 1)
                    for p, sl, rows in rows_of(table, i, blocks):
                        pool.dma_start(rows, feat[p, b, sl, 0:D]).then_inc(stored[b], 16)
                    for p, sl, rows in rows_of(skip_dram, i, blocks):
                        pool.dma_start(rows, feat[p, b, sl, D:2 * D]).then_inc(stored[b], 16)
                node_steps(pool, body)
                for b in range(2):
                    pool.wait_ge(stored[b], 48 * stores_of(b))

            @block.scalar
            def _(act):
                act.wait_ge(eps_ready, 1)

                def body(i, b, blocks):
                    k = len(blocks)
                    if later(i, 2):
                        act.wait_ge(prod_ready, i - 1)
                    act.activation(agg[:, b, 0:k], acc[:, bass.ds(i * QB, k), :], ACT.Copy).then_inc(agg_ready, 1)
                    act.wait_ge(var_ready, i + 1)
                    if later(i, 1):
                        act.wait_ge(x1_ready, i)
                    act.activation(s.root[:, 0:k], s.mean_var[:, 0:k, 1], ACT.Sqrt, bias=s.eps[:, 0:1]
                                   ).then_inc(root_ready, 1)
                    act.wait_ge(turned_ready, i + 1)
                    if later(i, 2):
                        act.wait_ge(both_ready, i - 1)
                    act.activation(x1t[:, b, 0:k], turned[:, 0:k], ACT.Copy).then_inc(x1t_ready, 1)
                node_steps(act, body)

            @block.tensor
            def _(pe):
                def body(i, b, blocks):
                    pe.wait_ge(agg_ready, i + 1)
                    for j, n in enumerate(blocks):
                        mm = pe.matmul(prod[b][0:n, j, :], agg[:, b, j, 0:n], c.w2[:], start=True, stop=True)
                    mm.then_inc(prod_ready, 1)
                    pe.wait_ge(x1_ready, i + 1)
                    if later(i, 1):
                        pe.wait_ge(x1t_ready, i)
                    for j, n in enumerate(blocks):
                        mm = pe.transpose(turned[:, j, 0:n], x1[0:n, b, j], c.ident[0:n, 0:n])
                    mm.then_inc(turned_ready, 1)
                    pe.wait_ge(x1t_ready, i + 1)
                    if later(i, 1):
                        pe.wait_ge(feat_ready, i)
                    for j, n in enumerate(blocks):
                        mm = pe.matmul(both[j // 2][0:n, j % 2, :], x1t[:, b, j, 0:n], c.w_node[:],
                                       start=True, stop=True)
                    mm.then_inc(both_ready, 1)
                node_steps(pe, body)

            @block.vector
            def _(dve):
                dve.memset(s.eps[:], EPS)
                dve.memset(s.mean_var[:], 0.0)
                dve.memset(turned[:], 0.0).then_inc(eps_ready, 1)
                dve.wait_ge(eps_ready, 1)

                def body(i, b, blocks):
                    chain = Chain(dve, chain_sem, i * LINKS)
                    if blocks[-1] < P:
                        dve.wait_ge(tail, 16 * len(blocks))
                    else:
                        dve.wait_ge(landed[b], (i - b) * 8 + 16)
                    dve.wait_ge(prod_ready, i + 1)
                    for j, n in enumerate(blocks):
                        last = dve.scalar_tensor_tensor(y[0:n, j], prod[b][0:n, j, :],
                                                        c.din[0:n, bass.ds(i * QB + j, 1)], c.b2[0:n],
                                                        ALU.mult, ALU.add)
                    chain.link(last)
                    for j, n in enumerate(blocks):
                        last = dve.tensor_tensor(y[0:n, j], y[0:n, j], xin[0:n, b, j], ALU.add)
                    chain.link(last)
                    if later(i, 2):
                        dve.wait_ge(stored[b], (i - b) * 24)
                    layernorm(dve, chain, c, y, x1[:, b], s, blocks, var_ready, root_ready, i
                              ).then_inc(x1_ready, 1)
                    dve.wait_ge(both_ready, i + 1)
                    for j, n in enumerate(blocks):
                        last = dve.tensor_scalar(feat[0:n, b, j], both[j // 2][0:n, j % 2, :],
                                                 c.node_vec[0:n, bass.ds(i * QB + j, 1)], None, ALU.mult)
                    last.then_inc(feat_ready, 1)
                    assert chain.n == LINKS
                node_steps(dve, body)


def product_edges(nc, c, table, edges, attr, scalars, acc_ad, acc_bc):
    ctx = ExitStack()
    with ctx:
        def sb(n, shape, dt=F32):
            return ctx.enter_context(nc.sbuf_tensor("t_" + n, shape, dt))

        def ps(n, shape=(P, 512)):
            return ctx.enter_context(nc.psum_tensor("t_" + n, list(shape), F32))

        def sem(n):
            return ctx.enter_context(nc.semaphore("t_" + n))

        ends = sb("ends", [P, SLOTS, 2 * T], I32)
        attrs = sb("attrs", [P, SLOTS, T, 4])
        scal = sb("scal", [P, SLOTS, T * ES])
        rows = sb("rows", [P, SLOTS, T, D])
        scal_t = sb("scal_t", [P, T // 2 * P])
        hidden = sb("hidden", [P, T // 2 * P])
        ad = sb("ad", [P, 2, T, 2 * MUL])
        cg = sb("cg", [P, T, MUL])
        ge = sb("ge", [P, T, 3, MUL])
        dot = sb("dot", [P, T, MUL])
        dot3 = sb("dot3", [P, T, MUL])
        msg_ad = sb("msg_ad", [P, 2, T, D])
        msg_bc = sb("msg_bc", [P, 2, T, D])
        rel = sb("rel", [P, T])
        hot = sb("hot", [P, T, P])
        iota = ps("iota")
        sums = ps("sums")
        turned = ps("turned")
        layer1 = ps("layer1")
        weight = [ps(f"weight{i}", (P, T, 4 * MUL)) for i in range(2)]
        ends_landed = [sem(f"ends_landed{i}") for i in range(SLOTS)]
        attrs_landed = [sem(f"attrs_landed{i}") for i in range(SLOTS)]
        scal_landed = [sem(f"scal_landed{i}") for i in range(SLOTS)]
        rows_landed = [sem(f"rows_landed{i}") for i in range(SLOTS)]
        groups_past, cleared, rel_ready, hot_ready, sums_ready, sums_added = [
            sem(n) for n in ("groups_past", "cleared", "rel_ready", "hot_ready", "sums_ready", "sums_added")]
        turned_ready, scal_t_ready, layer1_ready, hidden_ready, weight_ready, msg_ready, chain_sem = [
            sem(n) for n in ("turned_ready", "scal_t_ready", "layer1_ready", "hidden_ready", "weight_ready",
                             "msg_ready", "chain")]
        ad_ready = sem("ad_ready")

        with nc.Block() as block:
            @block.sync
            def _(sp):
                past_reg, landed_reg = sp.alloc_register("t_sp_past"), sp.alloc_register("t_sp_landed")

                def body(g, slot, r):
                    at = g * GE if not isinstance(g, int) else min(g * GE, E - GE)
                    if later(g, SLOTS):
                        past = worked_out(sp, past_reg, g - (SLOTS - 1))
                        landed = worked_out(sp, landed_reg, r * (16 * T))
                        sp.wait_ge(turned_ready, past)
                    sp.dma_start(scal[:, slot], scalars[bass.ds(at, GE), :].rearrange("(p t) e -> p (t e)", t=T)
                                 ).then_inc(scal_landed[slot], 16)
                    if later(g, SLOTS):
                        sp.wait_ge(groups_past, past)
                        sp.wait_ge(rows_landed[slot], landed)
                    sp.dma_start(ends[:, slot, :], edges[bass.ds(g, 1)].rearrange("a p e -> p (a e)")
                                 ).then_inc(ends_landed[slot], 16)
                    if later(g, SLOTS):
                        sp.wait_ge(msg_ready, past)
                    sp.dma_start(attrs[:, slot].rearrange("p t k -> p (t k)"),
                                 attr[bass.ds(at, GE), :].rearrange("(p t) e -> p (t e)", t=T)
                                 ).then_inc(attrs_landed[slot], 16)
                split_groups(sp, body)

            @block.gpsimd
            def _(pool):
                landed_reg, past_reg = pool.alloc_register("t_pool_landed"), pool.alloc_register("t_pool_past")

                def body(g, slot, r):
                    landed = worked_out(pool, landed_reg, r * 16 + 16)
                    past = worked_out(pool, past_reg, g - (SLOTS - 1))
                    pool.wait_ge(ends_landed[0], 16)
                    pool.wait_ge(ends_landed[slot], landed)
                    if later(g, SLOTS):
                        pool.wait_ge(msg_ready, past)
                    for t in range(T):
                        pool.indirect_dma_start(
                            out=rows[:, slot, t, :], out_offset=None, in_=table,
                            in_offset=bass.IndirectOffsetOnAxis(ap=ends[:, slot, t:t + 1], axis=0),
                        ).then_inc(rows_landed[slot], 16)
                split_groups(pool, body)

            @block.scalar
            def _(act):
                def turn(g):
                    act.wait_ge(turned_ready, g + 1)
                    if later(g, 1):
                        act.wait_ge(layer1_ready, g)
                    act.activation(scal_t[:], turned[:], ACT.Copy).then_inc(scal_t_ready, 1)

                def hide(g):
                    act.wait_ge(layer1_ready, g + 1)
                    if later(g, 1):
                        act.wait_ge(weight_ready, g)
                    act.activation(hidden[:], layer1[:], ACT.Silu, scale=0.125).then_inc(hidden_ready, 1)

                def scale_ad(g, slot, r):
                    act.wait_ge(attrs_landed[slot], r * 16 + 16)
                    if later(g, 2):
                        act.wait_ge(msg_ready, g - 1)
                    act.wait_ge(weight_ready, g + 1)
                    for t in range(T):
                        mul = act.activation(ad[:, slot % 2, t], weight[slot % 2][:, t, 0:2 * MUL], ACT.Copy,
                                             scale=attrs[:, slot, t, 0:1])
                    mul.then_inc(ad_ready, 1)

                turn(0)
                hide(0)
                turn(1)
                scale_ad(0, 0, 0)
                hide(1)

                def body(g, slot, r):
                    if not isinstance(g, int) or g + 2 < NG:
                        turn(g + 2)
                    if not isinstance(g, int) or g + 1 < NG:
                        scale_ad(g + 1, (slot + 1) % SLOTS, r + (slot + 1) // SLOTS)
                    if not isinstance(g, int) or g + 2 < NG:
                        hide(g + 2)
                split_groups(act, body)

            @block.tensor
            def _(pe):
                visits = pe.alloc_register("t_pe_visits")
                bounds = Bounds(pe, "t_pe_bound", c)
                bounds.load(0, 0)
                pe.reg_mov(visits, 1)

                def turn(g, slot, r):
                    pe.wait_ge(scal_landed[slot], r * 16 + 16)
                    if later(g, 1):
                        pe.wait_ge(scal_t_ready, g)
                    for j in range(T // 2):
                        mm = pe.transpose(turned[:, j * P:(j + 1) * P], scal[:, slot, j * P:(j + 1) * P],
                                          c.ident[:])
                    mm.then_inc(turned_ready, 1)

                def layer_1(g):
                    pe.wait_ge(scal_t_ready, g + 1)
                    if later(g, 1):
                        pe.wait_ge(hidden_ready, g)
                    pe.matmul(layer1[:], c.w_fc1[:], scal_t[:], start=True, stop=True).then_inc(layer1_ready, 1)

                def layer_2(g, b):
                    pe.wait_ge(hidden_ready, g + 1)
                    if later(g, 2):
                        pe.wait_ge(msg_ready, g - 1)
                    for j in range(T // 2):
                        mm = pe.matmul(weight[b][:, 2 * j:2 * j + 2, :], hidden[:, j * P:(j + 1) * P],
                                       c.w_fc2[:], start=True, stop=True)
                    mm.then_inc(weight_ready, 1)

                turn(0, 0, 0)
                layer_1(0)
                turn(1, 1, 0)
                layer_2(0, 0)
                layer_1(1)

                def body(g, slot, r):
                    first, past = bounds.of(slot)
                    if not isinstance(g, int) or g + 2 < NG:
                        turn(g + 2, (slot + 2) % SLOTS, r + (slot + 2) // SLOTS)
                    if not isinstance(g, int) or g + 1 < NG:
                        layer_2(g + 1, (slot + 1) % 2)
                    bounds.load_next(g, slot)
                    if not isinstance(g, int) or g + 2 < NG:
                        layer_1(g + 2)
                    msg_due = pe.snap(g + 1)
                    with pe.Fori(first, past):
                        pe.wait_ge(msg_ready, msg_due)
                        pe.wait_ge(hot_ready, visits)
                        for t in range(T):
                            pe.matmul(sums[:, 0:P], msg_ad[:, slot % 2, t, :], hot[:, t, :],
                                      start=t == 0, stop=t == T - 1)
                        for t in range(T):
                            mm = pe.matmul(sums[:, P:2 * P], msg_bc[:, slot % 2, t, :], hot[:, t, :],
                                           start=t == 0, stop=t == T - 1)
                        mm.then_inc(sums_ready, 1)
                        pe.reg_add(visits, visits, 1)
                split_groups(pe, body)

            @block.vector
            def _(dve):
                dve.memset(acc_ad[:], 0.0)
                dve.memset(acc_bc[:], 0.0)
                dve.memset(sums[:], 0.0)
                dve.tensor_copy(iota[:, 0:P], c.iota[:]).then_inc(cleared, 1)
                dve.wait_ge(cleared, 1)
                visits = dve.alloc_register("t_dve_visits")
                rels = dve.alloc_register("t_dve_rels")
                before = dve.alloc_register("t_dve_before")
                bounds = Bounds(dve, "t_dve_bound", c)
                bounds.load(0, 0)
                dve.reg_mov(visits, 0)
                dve.reg_mov(rels, 0)
                dve.reg_mov(before, NB)
                LINKS = 5

                def add_sums():
                    at = dve.snap(before, min_val=0, max_val=NB)
                    dve.wait_ge(sums_ready, visits)
                    dve.wait_ge(sums_added, visits)
                    dve.tensor_tensor(acc_ad[:, at, :], acc_ad[:, at, :], sums[:, 0:P], ALU.add)
                    dve.tensor_tensor(acc_bc[:, at, :], acc_bc[:, at, :], sums[:, P:2 * P], ALU.add
                                      ).then_inc(sums_added, 1)

                def messages(g, slot, r):
                    b = slot % 2
                    w = weight[b]
                    e0 = attrs[:, slot, :, 0:1]
                    e1 = attrs[:, slot, :, 1:4]
                    g0 = rows[:, slot, :, 0:MUL]
                    g1 = rows[:, slot, :, MUL:D].rearrange("p t (k u) -> p t k u", k=3)
                    base = g * LINKS
                    wide = [P, T, 3, MUL]
                    dve.wait_ge(attrs_landed[slot], r * 16 + 16)
                    dve.wait_ge(rows_landed[slot], r * (16 * T) + 16 * T)
                    if later(g, 1):
                        dve.wait_ge(msg_ready, g)
                    dve.tensor_tensor(ge[:], g1, e1[:, :, :, None].to_broadcast(wide), ALU.mult
                                      ).then_inc(chain_sem, 1)
                    dve.wait_ge(ad_ready, g + 1)
                    dve.tensor_tensor(cg[:], w[:, :, 2 * MUL:3 * MUL], g0, ALU.mult).then_inc(chain_sem, 1)
                    dve.tensor_tensor(msg_ad[:, b, :, MUL:D].rearrange("p t (k u) -> p t k u", k=3),
                                      ad[:, b, :, None, MUL:2 * MUL].to_broadcast(wide), g1, ALU.mult)
                    dve.tensor_tensor(msg_ad[:, b, :, 0:MUL], ad[:, b, :, 0:MUL], g0, ALU.mult
                                      ).then_inc(chain_sem, 1)
                    bounds.load_next(g, slot)
                    dve.wait_ge(chain_sem, base + 3)
                    dve.tensor_tensor(dot[:], ge[:, :, 0], ge[:, :, 1], ALU.add).then_inc(chain_sem, 1)
                    dve.tensor_tensor(msg_bc[:, b, :, MUL:D].rearrange("p t (k u) -> p t k u", k=3),
                                      cg[:, :, None, :].to_broadcast(wide),
                                      e1[:, :, :, None].to_broadcast(wide), ALU.mult)
                    dve.wait_ge(chain_sem, base + 4)
                    dve.tensor_tensor(dot3[:], dot[:], ge[:, :, 2], ALU.add).then_inc(chain_sem, 1)
                    dve.wait_ge(chain_sem, base + 5)
                    dve.tensor_tensor(msg_bc[:, b, :, 0:MUL], w[:, :, 3 * MUL:4 * MUL], dot3[:], ALU.mult
                                      ).then_inc(msg_ready, 1)

                def body(g, slot, r):
                    first, past = bounds.of(slot)
                    messages(g, slot, r)
                    dve.wait_ge(ends_landed[slot], r * 16 + 16)
                    dve.wait_ge(rel_ready, rels)
                    dve.tensor_scalar(rel[:], ends[:, slot, T:2 * T], c.base[:, bass.ds(g, 1)], None,
                                      ALU.subtract).then_inc(rel_ready, 1)
                    dve.reg_add(rels, rels, 1)
                    with dve.Fori(first, past) as blk:
                        add_sums()
                        dve.wait_ge(rel_ready, rels)
                        dve.tensor_tensor(hot[:], iota[:, None, 0:P].to_broadcast([P, T, P]),
                                          rel[:, :, None].to_broadcast([P, T, P]), ALU.is_equal
                                          ).then_inc(hot_ready, 1)
                        dve.reg_add(visits, visits, 1)
                        dve.reg_add(rels, rels, 1)
                        dve.reg_mov(before, blk)
                        dve.wait_ge(hot_ready, visits)
                        dve.tensor_scalar(rel[:], rel[:], float(-P), None, ALU.add).then_inc(rel_ready, 1)
                    dve.sem_inc(groups_past, 1)
                split_groups(dve, body)
                add_sums()


def last_nodes(nc, c, acc_ad, acc_bc, x1_dram, skip_dram, out_dram):
    ctx = ExitStack()
    with ctx:
        def sb(n, shape):
            return ctx.enter_context(nc.sbuf_tensor("n3_" + n, shape, F32))

        def sem(n):
            return ctx.enter_context(nc.semaphore("n3_" + n))

        agg = sb("agg", [P, 2, 2, QB, P])
        x1 = sb("x1", [P, 2, QB, D])
        skip = sb("skip", [P, 2, QB, D])
        y = sb("y", [P, QB, D])
        z = sb("z", [P, QB, D])
        out = sb("out", [P, 2, QB, D])
        ang = sb("ang", [P, QB])
        turns = sb("turns", [P, QB])
        whole = sb("whole", [P, QB])
        r1 = sb("r1", [P, QB])
        r2 = sb("r2", [P, QB])
        r3 = sb("r3", [P, QB])
        fold = sb("fold", [P, QB])
        args = sb("args", [P, 2, QB])
        trig = sb("trig", [P, 2, QB])
        sin_a = sb("sin_a", [P, QB])
        s = Norm(nc, ctx, "n3_")
        s.eps_ready = sem("eps_ready")
        conv = [ctx.enter_context(nc.psum_tensor(f"n3_conv{b}", [P, 2, 512], F32)) for b in range(2)]
        agg_ready, conv_ready, chain_sem, args_ready, trig_ready, var_ready, root_ready, out_ready, tail = [
            sem(n) for n in ("agg_ready", "conv_ready", "chain", "args_ready", "trig_ready", "var_ready",
                             "root_ready", "out_ready", "tail")]
        eps_ready = s.eps_ready
        landed = [sem(f"landed{i}") for i in range(2)]
        stored = [sem(f"stored{i}") for i in range(2)]
        W = D + 1
        LINKS = 14

        def conv_of(b, j):
            return conv[b][:, j // 2, (j % 2) * W:(j % 2) * W + W]

        with nc.Block() as block:
            @block.sync
            def _(sp):
                def body(i, b, blocks):
                    if later(i, 2):
                        sp.wait_ge(out_ready, i - 1)
                    for dst, src in ((x1, x1_dram), (skip, skip_dram)):
                        for p, sl, rows in rows_of(src, i, blocks):
                            sp.dma_start(dst[p, b, sl], rows).then_inc(tail if blocks[-1] < P else landed[b], 16)
                node_steps(sp, body)

            @block.gpsimd
            def _(pool):
                def body(i, b, blocks):
                    pool.wait_ge(eps_ready, 1)
                    pool.wait_ge(out_ready, i + 1)
                    for p, sl, rows in rows_of(out_dram, i, blocks):
                        pool.dma_start(rows, out[p, b, sl]).then_inc(stored[b], 16)
                node_steps(pool, body)
                for b in range(2):
                    pool.wait_ge(stored[b], 16 * stores_of(b))

            @block.scalar
            def _(act):
                act.wait_ge(eps_ready, 1)

                def body(i, b, blocks):
                    k = len(blocks)
                    if later(i, 2):
                        act.wait_ge(conv_ready, i - 1)
                    act.activation(agg[:, b, 0, 0:k], acc_ad[:, bass.ds(i * QB, k), :], ACT.Copy)
                    act.activation(agg[:, b, 1, 0:k], acc_bc[:, bass.ds(i * QB, k), :], ACT.Copy
                                   ).then_inc(agg_ready, 1)
                    act.wait_ge(args_ready, i + 1)
                    act.activation(trig[:], args[:], ACT.Sin).then_inc(trig_ready, 1)
                    act.wait_ge(var_ready, i + 1)
                    act.activation(s.root[:, 0:k], s.mean_var[:, 0:k, 1], ACT.Sqrt, bias=s.eps[:, 0:1]
                                   ).then_inc(root_ready, 1)
                node_steps(act, body)

            @block.tensor
            def _(pe):
                def body(i, b, blocks):
                    pe.wait_ge(agg_ready, i + 1)
                    if later(i, 2):
                        pe.wait_ge(out_ready, i - 1)
                    for j, n in enumerate(blocks):
                        pe.matmul(conv_of(b, j)[0:n], agg[:, b, 0, j, 0:n], c.w_ad[:], start=True, stop=False)
                        mm = pe.matmul(conv_of(b, j)[0:n], agg[:, b, 1, j, 0:n], c.w_bc[:], start=False, stop=True)
                    mm.then_inc(conv_ready, 1)
                node_steps(pe, body)

            @block.vector
            def _(dve):
                dve.memset(s.eps[:], EPS)
                dve.memset(s.mean_var[:], 0.0)
                dve.memset(ang[:], 0.0).then_inc(eps_ready, 1)
                dve.wait_ge(eps_ready, 1)

                def body(i, b, blocks):
                    chain = Chain(dve, chain_sem, i * LINKS)
                    if blocks[-1] < P:
                        dve.wait_ge(tail, 32 * len(blocks))
                    else:
                        dve.wait_ge(landed[b], (i - b) * 16 + 32)
                    dve.wait_ge(conv_ready, i + 1)
                    for j, n in enumerate(blocks):
                        last = dve.tensor_scalar(ang[0:n, j:j + 1], conv_of(b, j)[0:n, D:W],
                                                 c.node_vec[0:n, bass.ds(i * QB + j, 1)], None, ALU.mult)
                    chain.link(last)
                    chain.link(dve.tensor_scalar(turns[:], ang[:], 1.0 / (2 * PI), ROUND, ALU.mult, ALU.add))
                    chain.link(dve.tensor_scalar(whole[:], turns[:], -ROUND, None, ALU.add))
                    chain.link(dve.scalar_tensor_tensor(r1[:], whole[:], -TAU_A, ang[:], ALU.mult, ALU.add))
                    chain.link(dve.scalar_tensor_tensor(r2[:], whole[:], -TAU_B, r1[:], ALU.mult, ALU.add))
                    chain.link(dve.scalar_tensor_tensor(r3[:], whole[:], -TAU_C, r2[:], ALU.mult, ALU.add))
                    chain.link(dve.scalar_tensor_tensor(fold[:], r3[:], -1.0, r3[:], ALU.mult, ALU.max))
                    chain.link(dve.tensor_scalar(args[:, 1], fold[:], -1.0, PI / 2, ALU.mult, ALU.add))
                    dve.tensor_scalar(args[:, 0], r3[:], float(np.float32(3.1415925)), float(np.float32(-3.1415925)),
                                      ALU.min, ALU.max).then_inc(args_ready, 1)
                    dve.wait_ge(trig_ready, i + 1)
                    for j, n in enumerate(blocks):
                        dve.scalar_tensor_tensor(y[0:n, j], skip[0:n, b, j], trig[0:n, 1, j:j + 1], x1[0:n, b, j],
                                                 ALU.mult, ALU.add)
                        last = dve.tensor_scalar(sin_a[0:n, j:j + 1], trig[0:n, 0, j:j + 1],
                                                 c.node_vec[0:n, bass.ds(i * QB + j, 1)], None, ALU.mult)
                    chain.link(last)
                    for j, n in enumerate(blocks):
                        last = dve.scalar_tensor_tensor(z[0:n, j], conv_of(b, j)[0:n, 0:D], sin_a[0:n, j:j + 1],
                                                        y[0:n, j], ALU.mult, ALU.add)
                    chain.link(last)
                    if later(i, 2):
                        dve.wait_ge(stored[b], (i - b) * 8)
                    chain.link(layernorm(dve, chain, c, z, out[:, b], s, blocks, var_ready, root_ready, i))
                    dve.sem_inc(out_ready, 1)
                    chain.n += 1
                    dve.sem_inc(chain_sem, 1)
                    assert chain.n == LINKS, chain.n
                node_steps(dve, body)


def gnn_kernel(nc, x, edges, dst_groups, src, attr, scalars, node_vec, w, out):
    def dram(name, shape, dt=F32):
        return nc.dram_tensor(name, shape, dt, kind="Internal").ap()

    bounds_dram = dram("bounds_dram", [TC * P, 2], I32)
    base_dram = dram("base_dram", [TC * P])
    degree_dram = dram("degree_dram", [NB, P])
    table_0, table_1, table_2 = (dram(f"table_{i}", [N, D]) for i in range(3))
    x1_dram = dram("x1_dram", [N, D])
    skip_dram = dram("skip_dram", [N, D])

    class Kept:
        pass

    ctx = ExitStack()
    with ctx:
        def sb(name, shape, dt=F32):
            return ctx.enter_context(nc.sbuf_tensor(name, shape, dt))

        c = Kept()
        c.iota = sb("c_iota", [P, P])
        c.ident = sb("c_ident", [P, P])
        c.one_row = sb("c_one_row", [P, 1])
        c.w1, c.w2 = sb("c_w1", [D, D]), sb("c_w2", [D, D])
        c.b1, c.b2 = sb("c_b1", [P, D]), sb("c_b2", [P, D])
        c.w_node = sb("c_w_node", [D, 2 * D])
        c.w_ad, c.w_bc = sb("c_w_ad", [P, D + 1]), sb("c_w_bc", [P, D + 1])
        c.w_fc1 = sb("c_w_fc1", [2 * ES, 2 * ES])
        c.w_fc2 = sb("c_w_fc2", [2 * ES, 2 * P])
        c.bounds = sb("c_bounds", [1, TC * P * 2], I32)
        c.base = sb("c_base", [P, TC * P])
        c.node_vec = sb("c_node_vec", [P, NB])
        c.dout, c.din, c.dinout = sb("c_dout", [P, NB]), sb("c_din", [P, NB]), sb("c_dinout", [P, NB])

        constants(nc, c, w)
        bounds_table(nc, c, dst_groups, bounds_dram, base_dram)
        source_degrees(nc, c, src, node_vec)
        scaled_table(nc, c, x, table_0)
        with nc.sbuf_tensor("acc_0", [D, NB + 1, P], F32) as acc:
            with nc.sbuf_tensor("degree_row", [1, NB + 1, P], F32) as degree_row:
                convolve_edges(nc, c, "c1", table_0, edges, acc, degree_row)
                inward_degrees(nc, c, degree_row, degree_dram)
            first_nodes(nc, c, acc, table_1)
            convolve_edges(nc, c, "c2", table_1, edges, acc, None)
            second_nodes(nc, c, x, acc, x1_dram, table_2, skip_dram)
        with nc.sbuf_tensor("acc_ad", [D, NB + 1, P], F32) as acc_ad, \
                nc.sbuf_tensor("acc_bc", [D, NB + 1, P], F32) as acc_bc:
            product_edges(nc, c, table_2, edges, attr, scalars, acc_ad, acc_bc)
            last_nodes(nc, c, acc_ad, acc_bc, x1_dram, skip_dram, out)


WEIGHTS = ["L0_gnn_W1", "L0_gnn_b1", "L0_gnn_W2", "L0_gnn_b2", "L1_gnn_W_sc0", "L1_gnn_W_sc1", "L1_gnn_W_l1_0",
           "L1_gnn_W_l1_1", "L1_gnn_W_fc1", "L1_gnn_W_fc2", "L1_gnn_W_l2_A0", "L1_gnn_W_l2_B0", "L1_gnn_W_l2_C1",
           "L1_gnn_W_l2_D1", "L1_gnn_W_l3_A", "L1_gnn_W_l3_B"]


def kernel(**inputs):
    import concourse.bacc as bacc
    from concourse.bass_utils import run_bass_kernel_spmd

    src, dst = np.asarray(inputs["src"]), np.asarray(inputs["dst"])
    full = (NG - 1) * GE
    repeated = full - (E - GE)
    src_groups = np.concatenate([src[:full], src[E - GE:]]).reshape(NG, P, T)
    far = np.full(repeated, FAR, dst.dtype)
    dst_groups = np.concatenate([dst[:full], far, dst[full:]]).reshape(NG, GE)
    edges = np.concatenate([src_groups, dst_groups.reshape(NG, P, T)], axis=2)

    nc = bacc.Bacc("TRN2", target_bir_lowering=False, num_devices=1)
    arrays = {}

    def given(name, a):
        a = np.ascontiguousarray(a)
        arrays[f"in_{name}"] = a
        return nc.dram_tensor(f"in_{name}", a.shape, mybir.dt.from_np(a.dtype), kind="ExternalInput").ap()

    x = given("x", inputs["x"])
    edges_d = given("edges", edges)
    dst_d = given("dst_groups", dst_groups)
    src_d = given("src", src)
    attr = given("edge_attr_4", inputs["edge_attr_4"])
    scalars = given("edge_attr_64", inputs["edge_attr_64"])
    node_vec = given("node_vec1", inputs["node_vec1"])
    w = {name: given(name, inputs[name]) for name in WEIGHTS}
    out = nc.dram_tensor("out_0", [N, D], F32, kind="ExternalOutput").ap()
    gnn_kernel(nc, x, edges_d, dst_d, src_d, attr, scalars, node_vec, w, out)
    result = run_bass_kernel_spmd(nc, [arrays], core_ids=[0])
    return result.results[0]["out_0"]
```

```python
from contextlib import ExitStack

import numpy as np
import concourse.bass as bass
from concourse import mybir
from concourse.alu_op_type import AluOpType as ALU

ACT = mybir.ActivationFunctionType
AX = mybir.AxisListType
F32 = mybir.dt.float32
BF16 = mybir.dt.bfloat16
I32 = mybir.dt.int32

P = 128
N = 12500
E = 412500
D = 128
MUL = 32
ES = 64
NB = -(-N // P)
TAIL = N - (NB - 1) * P
T = 8
GE = P * T
NG = -(-E // GE)
SLOTS = 4
FAR = 1 << 14
HP = 125
HC = E // HP
HT = 22
NCH = HC // HT
TC = -(-NG // P)
QB = 4
NQ = (NB - 1) // QB
PEELED = 8
EPS = 1e-5
K_MSG = 1.679 / 8.0 / 4.0 / 8.0
K_DOT = K_MSG / 3.0 ** 0.5
K_F = 1.0 / 32.0 ** 0.5
PI = float(np.pi)
SINE_END = 3.1415925
ROUND = 1.5 * 2.0 ** 23
TAU_A = 6.28125
TAU_B = float(np.float32(np.floor((2 * np.pi - TAU_A) * 2.0 ** 21) / 2.0 ** 21))
TAU_C = float(np.float32(2 * np.pi - TAU_A - TAU_B))


def split_groups(engine, body):
    rounds = NG // SLOTS
    for g in range(SLOTS):
        body(g, g, 0)
    with engine.Fori(1, rounds) as r:
        for s in range(SLOTS):
            body(r * SLOTS + s, s, r)
    for g in range(rounds * SLOTS, NG):
        body(g, g % SLOTS, rounds)


def node_steps(engine, body):
    full = [P] * QB
    body(0, 0, full)
    body(1, 1, full)
    with engine.Fori(1, NQ // 2) as h:
        for j in range(2):
            body(h * 2 + j, j, full)
    body(NQ, NQ % 2, [P] * (NB - 1 - NQ * QB) + [TAIL])


def staged_steps(engine, stages):
    def round_of(i, parity):
        for k, stage in enumerate(stages):
            if stage is not None and (not isinstance(i, int) or 0 <= i - k <= NQ):
                last = isinstance(i, int) and i - k == NQ
                stage(i - k, (parity - k) % 2, [P] * (NB - 1 - NQ * QB) + [TAIL] if last else [P] * QB)

    for i in range(PEELED):
        round_of(i, i % 2)
    with engine.Fori(PEELED // 2, NQ // 2) as h:
        for j in range(2):
            round_of(h * 2 + j, j)
    for i in range(NQ, NQ + len(stages)):
        round_of(i, i % 2)


def rows_of(dram, step, blocks):
    if blocks[-1] == P:
        return [(slice(0, P), slice(0, len(blocks)),
                 dram[bass.ds(step * (QB * P), QB * P), :].rearrange("(s p) d -> p s d", p=P))]
    out = []
    for j, n in enumerate(blocks):
        r0 = (step * QB + j) * P
        out.append((slice(0, n), slice(j, j + 1), dram[r0:r0 + n, :].rearrange("(s p) d -> p s d", s=1)))
    return out


def later(g, n):
    return not isinstance(g, int) or g >= n


def worked_out(engine, reg, value):
    if isinstance(value, int):
        return value
    engine.reg_mov(reg, value)
    return reg


class Bounds:

    def __init__(self, engine, name, c):
        self.engine, self.c = engine, c
        self.pairs = [[engine.alloc_register(f"{name}_{p}{i}") for i in range(4)] for p in "ab"]

    def load(self, g, pair):
        self.engine.load(self.pairs[pair], self.c.bounds[0:1, bass.ds(g * 2, 4)])

    def load_next(self, g, slot):
        if slot % 2 == 1 and (not isinstance(g, int) or g + 1 < NG):
            self.load(g + 1, (slot // 2 + 1) % 2)

    def of(self, slot):
        pair = self.pairs[slot // 2]
        return pair[slot % 2 * 2], pair[slot % 2 * 2 + 1]


def constants(nc, c, w):
    ctx = ExitStack()
    with ctx:
        def sb(name, shape, dt=F32):
            return ctx.enter_context(nc.sbuf_tensor(name, shape, dt))

        def sem(name):
            return ctx.enter_context(nc.semaphore(name))

        iota_i = sb("iota_i", [P, P], I32)
        col_i = sb("col_i", [P, 1], I32)
        col = sb("col", [P, 1])
        vec_i = sb("vec_i", [P, 3, MUL], I32)
        vec_hit = sb("vec_hit", [P, 3, MUL])
        vec_mask = sb("vec_mask", [P, 3])
        quad_i = sb("quad_i", [P, 4], I32)
        quad_ge = sb("quad_ge", [P, 4])
        quad_mask = sb("quad_mask", [P, 4])
        w_f = sb("w_f", [P, MUL])
        w_sc = sb("w_sc", [P, MUL])
        w_ad = sb("w_ad", [P, MUL])
        w_bc = sb("w_bc", [P, MUL])
        l3 = sb("l3", [P, 2])
        loaded = sem("weights_loaded")
        iotas = sem("iotas_made")
        cleared = sem("weights_cleared")
        made = sem("masks_made")
        n_loads = [0]

        with nc.Block() as block:
            @block.gpsimd
            def _(pool):
                pool.iota(iota_i[:], [[1, P]], base=0, channel_multiplier=0).then_inc(iotas, 1)
                pool.iota(col_i[:], [[1, 1]], base=0, channel_multiplier=1).then_inc(iotas, 1)
                pool.iota(vec_i[:], [[1, 3], [3, MUL]], base=MUL, channel_multiplier=-1).then_inc(iotas, 1)
                pool.iota(quad_i[:], [[-MUL, 4]], base=0, channel_multiplier=1).then_inc(iotas, 1)

            @block.sync
            def _(sp):
                def load(dst, src):
                    n_loads[0] += 1
                    sp.dma_start(dst, src).then_inc(loaded, 16)

                load(c.w1[:], w["L0_gnn_W1"])
                load(c.w2[:], w["L0_gnn_W2"])
                load(c.b1[:], w["L0_gnn_b1"].partition_broadcast(P))
                load(c.b2[:], w["L0_gnn_b2"].partition_broadcast(P))
                load(w_f[0:MUL, :], w["L1_gnn_W_l1_0"])
                load(w_sc[0:MUL, :], w["L1_gnn_W_sc0"])
                for dst, name in ((w_f, "L1_gnn_W_l1_1"), (w_sc, "L1_gnn_W_sc1")):
                    src = w[name]
                    load(dst[MUL:P, :], bass.AP(tensor=src.tensor, offset=src.offset,
                                                ap=[[MUL, MUL], [0, 3], [1, MUL]]))
                load(w_ad[0:MUL, :], w["L1_gnn_W_l2_A0"])
                load(w_bc[0:MUL, :], w["L1_gnn_W_l2_B0"])
                for k in range(3):
                    rows = slice(MUL * (k + 1), MUL * (k + 2))
                    load(w_ad[rows, :], w["L1_gnn_W_l2_D1"])
                    load(w_bc[rows, :], w["L1_gnn_W_l2_C1"])
                sp.wait_ge(cleared, 1)
                load(l3[0:MUL, 0:1], w["L1_gnn_W_l3_A"])
                load(l3[0:MUL, 1:2], w["L1_gnn_W_l3_B"])
                for i in range(2):
                    half = slice(ES * i, ES * (i + 1))
                    load(c.w_fc1[half, half], w["L1_gnn_W_fc1"])
                    for to, at in enumerate((0, 2, 1, 3)):
                        load(c.w_fc2[half, P * i + MUL * to:P * i + MUL * (to + 1)],
                             w["L1_gnn_W_fc2"][:, MUL * at:MUL * (at + 1)])

            @block.vector
            def _(dve):
                dve.memset(l3[:], 0.0)
                dve.memset(c.w_fc1[:], 0.0)
                dve.memset(c.w_fc2[:], 0.0).then_inc(cleared, 1)
                dve.memset(c.one_row[:], 1.0)
                dve.wait_ge(iotas, 4)
                dve.tensor_copy(c.iota[:], iota_i[:]).then_inc(made, 1)
                dve.tensor_copy(col[:], col_i[:]).then_inc(made, 1)
                dve.tensor_scalar(vec_hit[:], vec_i[:], 0.0, None, ALU.is_equal).then_inc(made, 1)
                dve.tensor_scalar(quad_ge[:], quad_i[:], 0.0, None, ALU.is_ge).then_inc(made, 1)
                dve.wait_ge(made, 4)
                dve.tensor_scalar(c.ident[:], c.iota[:], col[:, 0:1], None, ALU.is_equal)
                dve.tensor_reduce(vec_mask[:], vec_hit[:], AX.X, ALU.add).then_inc(made, 1)
                dve.scalar_tensor_tensor(quad_mask[:], quad_i[:], float(MUL), quad_ge[:],
                                         ALU.is_lt, ALU.mult).then_inc(made, 1)
                dve.wait_ge(made, 6)
                dve.wait_ge(loaded, 16 * n_loads[0])
                dve.tensor_scalar(c.w_node[:, 0:MUL], w_f[:], quad_mask[:, 0:1], K_F, ALU.mult, ALU.mult)
                dve.tensor_scalar(c.w_node[:, D:D + MUL], w_sc[:], quad_mask[:, 0:1], K_F, ALU.mult, ALU.mult)
                for k in range(3):
                    at = MUL * (k + 1)
                    out = slice(MUL + k, D, 3)
                    dve.tensor_scalar(c.w_node[:, at:at + MUL], w_f[:], vec_mask[:, k:k + 1], K_F,
                                      ALU.mult, ALU.mult)
                    dve.tensor_scalar(c.w_node[:, D + MUL + k:2 * D:3], w_sc[:], vec_mask[:, k:k + 1], K_F,
                                      ALU.mult, ALU.mult)
                    dve.tensor_scalar(c.w_ad[:, out], w_ad[:], quad_mask[:, k + 1:k + 2], K_MSG,
                                      ALU.mult, ALU.mult)
                    dve.tensor_scalar(c.w_bc[:, out], w_bc[:], quad_mask[:, k + 1:k + 2], K_MSG,
                                      ALU.mult, ALU.mult)
                dve.tensor_scalar(c.w_ad[:, 0:MUL], w_ad[:], quad_mask[:, 0:1], K_MSG, ALU.mult, ALU.mult)
                dve.tensor_scalar(c.w_bc[:, 0:MUL], w_bc[:], quad_mask[:, 0:1], K_DOT, ALU.mult, ALU.mult)
                dve.tensor_scalar(c.w_ad[:, D:D + 1], l3[:, 0:1], 0.1 * K_MSG, None, ALU.mult)
                dve.tensor_scalar(c.w_bc[:, D:D + 1], l3[:, 1:2], 0.1 * K_DOT, None, ALU.mult)


def bounds_table(nc, c, dst_groups, bounds_dram, base_dram):
    ctx = ExitStack()
    with ctx:
        def sb(name, shape, dt=F32):
            return ctx.enter_context(nc.sbuf_tensor(name, shape, dt))

        def sem(name):
            return ctx.enter_context(nc.semaphore(name))

        dst = sb("bt_dst", [P, TC, GE], I32)
        least = sb("bt_least", [P, TC], I32)
        most = sb("bt_most", [P, TC], I32)
        most_in = sb("bt_most_in", [P, TC], I32)
        most_block = sb("bt_most_block", [P, TC], I32)
        bounds = sb("bt_bounds", [P, TC, 2], I32)
        base = sb("bt_base", [P, TC])
        landed = sem("bt_landed")
        step = sem("bt_step")
        stored = sem("bt_stored")
        done = sem("bt_back")
        counts = [min(P, NG - P * i) for i in range(TC)]

        with nc.Block() as block:
            @block.sync
            def _(sp):
                for i, n in enumerate(counts):
                    sp.dma_start(dst[0:n, i, :], dst_groups[P * i:P * i + n, :]).then_inc(landed, 16)
                sp.wait_ge(step, 7)
                with nc.allow_non_contiguous_dma(reason="a table of a few numbers per partition"):
                    sp.dma_start(bounds_dram.rearrange("(c p) e -> p c e", p=P), bounds[:]).then_inc(stored, 16)
                    sp.dma_start(base_dram.rearrange("(c p) -> p c", p=P), base[:]).then_inc(stored, 16)
                sp.wait_ge(stored, 32)
                sp.dma_start(c.bounds[:], bounds_dram.rearrange("(a g) e -> a (g e)", a=1)).then_inc(done, 16)
                sp.dma_start(c.base[:], base_dram.partition_broadcast(P)).then_inc(done, 16)
                sp.wait_ge(done, 32)

            @block.vector
            def _(dve):
                dve.memset(least[:], 0)
                dve.memset(most[:], 0).then_inc(step, 1)
                dve.wait_ge(step, 1)
                dve.wait_ge(landed, 16 * TC)
                for i, n in enumerate(counts):
                    dve.tensor_reduce(least[0:n, i:i + 1], dst[0:n, i, :], AX.X, ALU.min)
                    last = dve.tensor_reduce(most[0:n, i:i + 1], dst[0:n, i, :], AX.X, ALU.max)
                last.then_inc(step, 1)
                dve.wait_ge(step, 2)
                dve.tensor_scalar(most_in[:], most[:], float(NB * P - 1), None, ALU.min).then_inc(step, 1)
                dve.tensor_scalar(bounds[:, :, 0], least[:], 7, None, ALU.arith_shift_right).then_inc(step, 1)
                dve.wait_ge(step, 4)
                dve.tensor_scalar(most_block[:], most_in[:], 7, None, ALU.arith_shift_right).then_inc(step, 1)
                dve.wait_ge(step, 5)
                dve.tensor_scalar(bounds[:, :, 1], most_block[:], 1.0, None, ALU.add).then_inc(step, 1)
                dve.tensor_scalar(base[:], bounds[:, :, 0], float(P), None, ALU.mult).then_inc(step, 1)


def source_degrees(nc, c, src, node_vec):
    ctx = ExitStack()
    with ctx:
        def sb(name, shape, dt=F32):
            return ctx.enter_context(nc.sbuf_tensor(name, shape, dt))

        def sem(name):
            return ctx.enter_context(nc.semaphore(name))

        src_i = sb("h_src", [HP, HC], I32)
        part_i = sb("h_part", [HP, HC], I32)
        hi = sb("h_hi", [HP, HC], BF16)
        lo = sb("h_lo", [HP, HC], BF16)
        iota_t = sb("h_iota", [P, P, HT], BF16)
        one_hi = sb("h_one_hi", [HP, 2, NB, HT], BF16)
        one_lo = sb("h_one_lo", [HP, 2, P, HT], BF16)
        count_rows = sb("h_rows", [NB, P])
        vec_rows = sb("h_vec", [NB, P])
        degree = sb("h_degree", [P, NB])
        root = sb("h_root", [P, NB])
        counts = ctx.enter_context(nc.psum_tensor("h_counts", [NB, 512], F32))
        turned = ctx.enter_context(nc.psum_tensor("h_turned", [P, 512], F32))
        landed = sem("h_landed")
        split = sem("h_split")
        hot = sem("h_hot")
        hot_used = sem("h_hot_used")
        rows_ready = sem("h_rows_ready")
        turned_ready = sem("h_turned_ready")
        degree_ready = sem("h_degree_ready")
        root_ready = sem("h_root_ready")

        with nc.Block() as block:
            @block.sync
            def _(sp):
                sp.dma_start(src_i[:], src.rearrange("(p c) -> p c", p=HP)).then_inc(landed, 16)
                sp.wait_ge(split, 1)
                sp.dma_start(vec_rows[0:NB - 1, :],
                             node_vec[0:(NB - 1) * P, :].rearrange("(b p) e -> b (p e)", p=P)).then_inc(landed, 16)
                sp.dma_start(vec_rows[NB - 1:NB, 0:TAIL],
                             node_vec[(NB - 1) * P:N, :].rearrange("(b p) e -> b (p e)", b=1)).then_inc(landed, 16)

            @block.gpsimd
            def _(pool):
                pool.memset(vec_rows[96:NB, :], 0.0).then_inc(split, 1)

            @block.vector
            def _(dve):
                dve.tensor_copy(iota_t[:], c.iota[:, :, None].to_broadcast([P, P, HT]))
                dve.wait_ge(landed, 48)
                dve.tensor_scalar(part_i[:], src_i[:], 7, None, ALU.arith_shift_right).then_inc(split, 1)
                dve.wait_ge(split, 2)
                dve.tensor_copy(hi[:], part_i[:]).then_inc(split, 1)
                dve.wait_ge(split, 3)
                dve.tensor_scalar(part_i[:], src_i[:], P - 1, None, ALU.bitwise_and).then_inc(split, 1)
                dve.wait_ge(split, 4)
                dve.tensor_copy(lo[:], part_i[:]).then_inc(split, 1)
                dve.wait_ge(split, 5)

                def chunk(i, b):
                    dve.tensor_tensor(one_hi[:, b], hi[:, None, bass.ds(i * HT, HT)].to_broadcast([HP, NB, HT]),
                                      iota_t[0:HP, 0:NB, :], ALU.is_equal)
                    dve.tensor_tensor(one_lo[:, b], lo[:, None, bass.ds(i * HT, HT)].to_broadcast([HP, P, HT]),
                                      iota_t[0:HP, :, :], ALU.is_equal).then_inc(hot, 1)

                chunk(0, 0)
                chunk(1, 1)
                with dve.Fori(1, NCH // 2) as h:
                    for b in range(2):
                        dve.wait_ge(hot_used, h * 2 + (b - 1))
                        chunk(h * 2 + b, b)
                dve.wait_ge(hot_used, NCH)
                dve.tensor_copy(count_rows[:], counts[:, 0:P]).then_inc(rows_ready, 1)
                dve.wait_ge(turned_ready, 1)
                dve.tensor_scalar(degree[:], turned[:, 0:NB], 1.0, None, ALU.max).then_inc(degree_ready, 1)
                dve.tensor_copy(c.node_vec[:], turned[:, P:P + NB])
                dve.wait_ge(root_ready, 1)
                dve.reciprocal(c.dout[:], root[:])

            @block.scalar
            def _(act):
                act.wait_ge(degree_ready, 1)
                act.activation(root[:], degree[:], ACT.Sqrt).then_inc(root_ready, 1)

            @block.tensor
            def _(pe):
                def chunk(i, b, first, last):
                    pe.wait_ge(hot, i + 1)
                    for t in range(HT):
                        mm = pe.matmul(counts[:, 0:P], one_hi[:, b, :, t], one_lo[:, b, :, t],
                                       start=first and t == 0, stop=last and t == HT - 1)
                    mm.then_inc(hot_used, 1)

                chunk(0, 0, True, False)
                chunk(1, 1, False, False)
                with pe.Fori(1, NCH // 2 - 1) as h:
                    for b in range(2):
                        chunk(h * 2 + b, b, False, False)
                chunk(NCH - 2, 0, False, False)
                chunk(NCH - 1, 1, False, True)
                pe.wait_ge(rows_ready, 1)
                pe.wait_ge(landed, 48)
                pe.transpose(turned[:, 0:NB], count_rows[:], c.ident[0:NB, 0:NB])
                pe.transpose(turned[:, P:P + NB], vec_rows[:], c.ident[0:NB, 0:NB]).then_inc(turned_ready, 1)


def scaled_table(nc, c, x, table):
    ctx = ExitStack()
    with ctx:
        xin = ctx.enter_context(nc.sbuf_tensor("s_in", [P, 2, QB, D], F32))
        out = ctx.enter_context(nc.sbuf_tensor("s_out", [P, 2, QB, D], F32))
        landed = [ctx.enter_context(nc.semaphore(f"s_landed{i}")) for i in range(2)]
        stored = [ctx.enter_context(nc.semaphore(f"s_stored{i}")) for i in range(2)]
        tail = ctx.enter_context(nc.semaphore("s_tail"))
        scaled = ctx.enter_context(nc.semaphore("s_scaled"))

        with nc.Block() as block:
            @block.sync
            def _(sp):
                def body(i, b, blocks):
                    if later(i, 2):
                        sp.wait_ge(scaled, i - 1)
                    for p, s, rows in rows_of(x, i, blocks):
                        sp.dma_start(xin[p, b, s], rows).then_inc(tail if blocks[-1] < P else landed[b], 16)
                node_steps(sp, body)

            @block.vector
            def _(dve):
                def body(i, b, blocks):
                    if blocks[-1] < P:
                        dve.wait_ge(tail, 16 * len(blocks))
                    else:
                        dve.wait_ge(landed[b], (i - b) * 8 + 16)
                    if later(i, 2):
                        dve.wait_ge(stored[b], (i - b) * 8)
                    for j, n in enumerate(blocks):
                        mul = dve.tensor_scalar(out[0:n, b, j], xin[0:n, b, j],
                                                c.dout[0:n, bass.ds(i * QB + j, 1)], None, ALU.mult)
                    mul.then_inc(scaled, 1)
                node_steps(dve, body)

            @block.scalar
            def _(act):
                def body(i, b, blocks):
                    act.wait_ge(scaled, i + 1)
                    for p, s, rows in rows_of(table, i, blocks):
                        act.dma_start(rows, out[p, b, s]).then_inc(stored[b], 16)
                node_steps(act, body)
                for b in range(2):
                    steps = (NQ + 1 - b) // 2 + (NB - 1 - NQ * QB if NQ % 2 == b else 0) + (NQ % 2 == b)
                    act.wait_ge(stored[b], 16 * steps)


def convolve_edges(nc, c, name, table, edges, acc, degree_row):
    ctx = ExitStack()
    with ctx:
        def sb(n, shape, dt=F32):
            return ctx.enter_context(nc.sbuf_tensor(f"{name}_{n}", shape, dt))

        def ps(n):
            return ctx.enter_context(nc.psum_tensor(f"{name}_{n}", [P, 512], F32))

        def sem(n):
            return ctx.enter_context(nc.semaphore(f"{name}_{n}"))

        ends = sb("ends", [P, SLOTS, 2 * T], I32)
        rows = sb("rows", [P, SLOTS, T, D])
        rel = sb("rel", [P, T])
        hot = sb("hot", [P, T, P])
        iota = ps("iota")
        sums = ps("sums")
        counts = ps("counts")
        ends_landed = [sem(f"ends_landed{i}") for i in range(SLOTS)]
        rows_landed = [sem(f"rows_landed{i}") for i in range(SLOTS)]
        groups_past = sem("groups_past")
        cleared = sem("cleared")
        rel_ready = sem("rel_ready")
        hot_ready = sem("hot_ready")
        sums_ready = sem("sums_ready")
        sums_added = sem("sums_added")

        with nc.Block() as block:
            @block.sync
            def _(sp):
                past_reg, landed_reg = sp.alloc_register(f"{name}_sp_past"), sp.alloc_register(f"{name}_sp_landed")

                def body(g, slot, r):
                    if later(g, SLOTS):
                        past = worked_out(sp, past_reg, g - (SLOTS - 1))
                        landed = worked_out(sp, landed_reg, r * (16 * T))
                        sp.wait_ge(groups_past, past)
                        sp.wait_ge(rows_landed[slot], landed)
                    sp.dma_start(ends[:, slot, :], edges[bass.ds(g, 1)].rearrange("a p e -> p (a e)")
                                 ).then_inc(ends_landed[slot], 16)
                split_groups(sp, body)

            @block.gpsimd
            def _(pool):
                landed_reg, past_reg = pool.alloc_register(f"{name}_pool_landed"), pool.alloc_register(f"{name}_pool_past")

                def body(g, slot, r):
                    landed = worked_out(pool, landed_reg, r * 16 + 16)
                    past = worked_out(pool, past_reg, g - (SLOTS - 2))
                    pool.wait_ge(ends_landed[0], 16)
                    pool.wait_ge(ends_landed[slot], landed)
                    if later(g, SLOTS):
                        pool.wait_ge(groups_past, past)
                    for t in range(T):
                        pool.indirect_dma_start(
                            out=rows[:, slot, t, :], out_offset=None, in_=table,
                            in_offset=bass.IndirectOffsetOnAxis(ap=ends[:, slot, t:t + 1], axis=0),
                        ).then_inc(rows_landed[slot], 16)
                split_groups(pool, body)

            @block.vector
            def _(dve):
                dve.memset(acc[:], 0.0)
                if degree_row is not None:
                    dve.memset(degree_row[:], 0.0)
                dve.memset(sums[:], 0.0)
                dve.memset(counts[:], 0.0)
                dve.tensor_copy(iota[:, 0:P], c.iota[:]).then_inc(cleared, 1)
                dve.wait_ge(cleared, 1)
                visits = dve.alloc_register(f"{name}_dve_visits")
                rels = dve.alloc_register(f"{name}_dve_rels")
                before = dve.alloc_register(f"{name}_dve_before")
                bounds = Bounds(dve, name + "_dve_bound", c)
                bounds.load(0, 0)
                dve.reg_mov(visits, 0)
                dve.reg_mov(rels, 0)
                dve.reg_mov(before, NB)

                def add_sums():
                    at = dve.snap(before, min_val=0, max_val=NB)
                    dve.wait_ge(sums_ready, visits)
                    dve.wait_ge(sums_added, visits)
                    if degree_row is not None:
                        dve.tensor_tensor(degree_row[:, at, :], degree_row[:, at, :], counts[0:1, 0:P], ALU.add)
                    dve.tensor_tensor(acc[:, at, :], acc[:, at, :], sums[:, 0:P], ALU.add
                                      ).then_inc(sums_added, 1)

                def body(g, slot, r):
                    first, past = bounds.of(slot)
                    dve.wait_ge(ends_landed[slot], r * 16 + 16)
                    dve.wait_ge(rel_ready, rels)
                    dve.tensor_scalar(rel[:], ends[:, slot, T:2 * T], c.base[:, bass.ds(g, 1)], None,
                                      ALU.subtract).then_inc(rel_ready, 1)
                    dve.reg_add(rels, rels, 1)
                    bounds.load_next(g, slot)
                    with dve.Fori(first, past) as blk:
                        add_sums()
                        dve.wait_ge(rel_ready, rels)
                        dve.tensor_tensor(hot[:], iota[:, None, 0:P].to_broadcast([P, T, P]),
                                          rel[:, :, None].to_broadcast([P, T, P]), ALU.is_equal
                                          ).then_inc(hot_ready, 1)
                        dve.reg_add(visits, visits, 1)
                        dve.reg_add(rels, rels, 1)
                        dve.reg_mov(before, blk)
                        dve.wait_ge(hot_ready, visits)
                        dve.tensor_scalar(rel[:], rel[:], float(-P), None, ALU.add).then_inc(rel_ready, 1)
                    dve.sem_inc(groups_past, 1)
                split_groups(dve, body)
                add_sums()

            @block.tensor
            def _(pe):
                visits = pe.alloc_register(f"{name}_pe_visits")
                bounds = Bounds(pe, name + "_pe_bound", c)
                bounds.load(0, 0)
                pe.reg_mov(visits, 1)

                def body(g, slot, r):
                    first, past = bounds.of(slot)
                    bounds.load_next(g, slot)
                    rows_due = pe.snap(r * (16 * T) + 16 * T)
                    with pe.Fori(first, past):
                        pe.wait_ge(rows_landed[slot], rows_due)
                        pe.wait_ge(hot_ready, visits)
                        for t in range(T):
                            mm = pe.matmul(sums[:, 0:P], rows[:, slot, t, :], hot[:, t, :],
                                           start=t == 0, stop=t == T - 1)
                            if degree_row is not None:
                                mm = pe.matmul(counts[0:1, 0:P], c.one_row[:], hot[:, t, :],
                                               start=t == 0, stop=t == T - 1)
                        mm.then_inc(sums_ready, 1)
                        pe.reg_add(visits, visits, 1)
                split_groups(pe, body)


def inward_degrees(nc, c, degree_row, degree_dram):
    ctx = ExitStack()
    with ctx:
        rows = ctx.enter_context(nc.sbuf_tensor("i_rows", [NB, P], F32))
        degree = ctx.enter_context(nc.sbuf_tensor("i_degree", [P, NB], F32))
        root = ctx.enter_context(nc.sbuf_tensor("i_root", [P, NB], F32))
        turned = ctx.enter_context(nc.psum_tensor("i_turned", [P, 512], F32))
        stored, landed, turned_ready, degree_ready, root_ready, din_ready = [
            ctx.enter_context(nc.semaphore("i_" + n))
            for n in ("stored", "landed", "turned_ready", "degree_ready", "root_ready", "din_ready")]

        with nc.Block() as block:
            @block.sync
            def _(sp):
                sp.dma_start(degree_dram.rearrange("(a b) p -> a (b p)", a=1),
                             degree_row[0:1, 0:NB, :].rearrange("a b p -> a (b p)")).then_inc(stored, 16)
                sp.wait_ge(stored, 16)
                sp.dma_start(rows[:], degree_dram).then_inc(landed, 16)

            @block.tensor
            def _(pe):
                pe.wait_ge(landed, 16)
                pe.transpose(turned[:, 0:NB], rows[:], c.ident[0:NB, 0:NB]).then_inc(turned_ready, 1)

            @block.scalar
            def _(act):
                act.wait_ge(degree_ready, 1)
                act.activation(root[:], degree[:], ACT.Sqrt).then_inc(root_ready, 1)

            @block.vector
            def _(dve):
                dve.wait_ge(turned_ready, 1)
                dve.tensor_scalar(degree[:], turned[:, 0:NB], 1.0, None, ALU.max).then_inc(degree_ready, 1)
                dve.wait_ge(root_ready, 1)
                dve.reciprocal(c.din[:], root[:]).then_inc(din_ready, 1)
                dve.wait_ge(din_ready, 1)
                dve.tensor_tensor(c.dinout[:], c.din[:], c.dout[:], ALU.mult)


def first_nodes(nc, c, acc, table):
    ctx = ExitStack()
    with ctx:
        agg = ctx.enter_context(nc.sbuf_tensor("n1_agg", [P, 2, QB, P], F32))
        bias = ctx.enter_context(nc.sbuf_tensor("n1_bias", [P, 2, QB, D], F32))
        out = ctx.enter_context(nc.sbuf_tensor("n1_out", [P, 2, QB, D], F32))
        prod = [ctx.enter_context(nc.psum_tensor(f"n1_prod{b}", [P, QB, D], F32)) for b in range(2)]
        agg_ready, prod_ready, bias_ready, made = [
            ctx.enter_context(nc.semaphore("n1_" + n)) for n in ("agg_ready", "prod_ready", "bias_ready", "made")]
        stored = [ctx.enter_context(nc.semaphore(f"n1_stored{i}")) for i in range(2)]

        with nc.Block() as block:
            @block.scalar
            def _(act):
                def body(i, b, blocks):
                    if later(i, 2):
                        act.wait_ge(prod_ready, i - 1)
                    act.activation(agg[:, b, 0:len(blocks)], acc[:, bass.ds(i * QB, len(blocks)), :],
                                   ACT.Copy).then_inc(agg_ready, 1)
                node_steps(act, body)

            @block.tensor
            def _(pe):
                def body(i, b, blocks):
                    pe.wait_ge(agg_ready, i + 1)
                    if later(i, 2):
                        pe.wait_ge(made, i - 1)
                    for j, n in enumerate(blocks):
                        mm = pe.matmul(prod[b][0:n, j, :], agg[:, b, j, 0:n], c.w1[:], start=True, stop=True)
                    mm.then_inc(prod_ready, 1)
                node_steps(pe, body)

            @block.vector
            def _(dve):
                def body(i, b, blocks):
                    if later(i, 2):
                        dve.wait_ge(stored[b], (i - b) * 8)
                        dve.wait_ge(made, i - 1)
                    for j, n in enumerate(blocks):
                        last = dve.tensor_scalar(bias[0:n, b, j], c.b1[0:n], c.dout[0:n, bass.ds(i * QB + j, 1)],
                                                 None, ALU.mult)
                    last.then_inc(bias_ready, 1)
                    dve.wait_ge(bias_ready, i + 1)
                    dve.wait_ge(prod_ready, i + 1)
                    for j, n in enumerate(blocks):
                        last = dve.scalar_tensor_tensor(out[0:n, b, j], prod[b][0:n, j, :],
                                                        c.dinout[0:n, bass.ds(i * QB + j, 1)], bias[0:n, b, j],
                                                        ALU.mult, ALU.add)
                    last.then_inc(made, 1)
                node_steps(dve, body)

            @block.sync
            def _(sp):
                def body(i, b, blocks):
                    sp.wait_ge(made, i + 1)
                    for p, s, rows in rows_of(table, i, blocks):
                        sp.dma_start(rows, out[p, b, s]).then_inc(stored[b], 16)
                node_steps(sp, body)
                for b in range(2):
                    sp.wait_ge(stored[b], 16 * stores_of(b))


def stores_of(b):
    steps = (NQ - b + 1) // 2
    return steps + (NB - NQ * QB if NQ % 2 == b else 0)


class Norm:

    def __init__(self, nc, ctx, name):
        sb = lambda n, shape: ctx.enter_context(nc.sbuf_tensor(name + n, shape, F32))
        self.stats = sb("stats", [P, QB, 6])
        self.mean_var = sb("mean_var", [P, 2, QB, 2])
        self.root = sb("root", [P, 2, QB])
        self.rstd = sb("rstd", [P, 2, QB])
        self.eps = sb("eps", [P, 1])
        self.reg = nc.vector.alloc_register(name + "stats_due")

    def semaphores(self, sem):
        self.set_up, self.stats_ready, self.var_ready, self.root_ready, self.rstd_ready = [
            sem(n) for n in ("norm_set_up", "stats_ready", "var_ready", "root_ready", "rstd_ready")]

    def clear(self, dve):
        dve.memset(self.eps[:], EPS)
        dve.memset(self.mean_var[:], 0.0).then_inc(self.set_up, 1)
        dve.wait_ge(self.set_up, 1)

    def statistics(self, dve, y, i, b, blocks):
        for j, n in enumerate(blocks):
            last = dve.bn_stats(self.stats[0:n, j, :], y[0:n, j])
        last.then_inc(self.stats_ready, 1)
        due = worked_out(dve, self.reg, i + 1)
        dve.wait_ge(self.set_up, 1)
        dve.wait_ge(self.stats_ready, due)
        for j, n in enumerate(blocks):
            last = dve.bn_aggr(self.mean_var[0:n, b, j, :], self.stats[0:n, j, :])
        last.then_inc(self.var_ready, 1)

    def take_root(self, act, i, b, blocks):
        act.wait_ge(self.var_ready, i + 1)
        if later(i, 2):
            act.wait_ge(self.rstd_ready, i - 1)
        act.activation(self.root[:, b, 0:len(blocks)], self.mean_var[:, b, 0:len(blocks), 1], ACT.Sqrt,
                       bias=self.eps[:, 0:1]).then_inc(self.root_ready, 1)

    def invert_root(self, dve, i, b, blocks):
        dve.wait_ge(self.root_ready, i + 1)
        dve.reciprocal(self.rstd[:, b, 0:len(blocks)], self.root[:, b, 0:len(blocks)]).then_inc(self.rstd_ready, 1)

    def apply(self, dve, y, out, i, b, blocks):
        dve.wait_ge(self.rstd_ready, i + 1)
        for j, n in enumerate(blocks):
            last = dve.tensor_scalar(out[0:n, j], y[0:n, j], self.mean_var[0:n, b, j, 0:1], self.rstd[0:n, b, j:j + 1],
                                     ALU.subtract, ALU.mult)
        return last


def second_nodes(nc, c, x, acc, x1_dram, table, skip_dram):
    ctx = ExitStack()
    with ctx:
        def sb(n, shape):
            return ctx.enter_context(nc.sbuf_tensor("n2_" + n, shape, F32))

        def sem(n):
            return ctx.enter_context(nc.semaphore("n2_" + n))

        agg = sb("agg", [P, 2, QB, P])
        xin = sb("xin", [P, 2, QB, D])
        h = sb("h", [P, QB, D])
        y = sb("y", [P, 2, QB, D])
        x1 = sb("x1", [P, 2, QB, D])
        x1t = sb("x1t", [P, 2, QB, P])
        feat = sb("feat", [P, 2, QB, 2 * D])
        s = Norm(nc, ctx, "n2_")
        prod = [ctx.enter_context(nc.psum_tensor(f"n2_prod{b}", [P, QB, D], F32)) for b in range(2)]
        turned = ctx.enter_context(nc.psum_tensor("n2_turned", [P, QB, P], F32))
        both = [ctx.enter_context(nc.psum_tensor(f"n2_both{b}", [P, QB, 2 * D], F32)) for b in range(2)]
        agg_ready, prod_ready, chain_sem, y_ready, x1_ready, turned_ready, x1t_ready, both_ready, feat_ready, tail = [
            sem(n) for n in ("agg_ready", "prod_ready", "chain", "y_ready", "x1_ready", "turned_ready",
                             "x1t_ready", "both_ready", "feat_ready", "tail")]
        s.semaphores(sem)
        landed = [sem(f"landed{i}") for i in range(2)]
        x1_stored = [sem(f"x1_stored{i}") for i in range(2)]
        feat_stored = [sem(f"feat_stored{i}") for i in range(2)]

        with nc.Block() as block:
            @block.sync
            def _(sp):
                def load(i, b, blocks):
                    if later(i, 2):
                        sp.wait_ge(y_ready, i - 1)
                    for p, sl, rows in rows_of(x, i, blocks):
                        sp.dma_start(xin[p, b, sl], rows).then_inc(tail if blocks[-1] < P else landed[b], 16)

                def store_x1(i, b, blocks):
                    sp.wait_ge(x1_ready, i + 1)
                    for p, sl, rows in rows_of(x1_dram, i, blocks):
                        sp.dma_start(rows, x1[p, b, sl]).then_inc(x1_stored[b], 16)

                def store_features(i, b, blocks):
                    sp.wait_ge(feat_ready, i + 1)
                    for dram, cols in ((table, slice(0, D)), (skip_dram, slice(D, 2 * D))):
                        for p, sl, rows in rows_of(dram, i, blocks):
                            sp.dma_start(rows, feat[p, b, sl, cols]).then_inc(feat_stored[b], 16)

                staged_steps(sp, [load, None, store_x1, None, None, store_features])
                for b in range(2):
                    sp.wait_ge(x1_stored[b], 16 * stores_of(b))
                    sp.wait_ge(feat_stored[b], 32 * stores_of(b))

            @block.scalar
            def _(act):
                act.wait_ge(s.set_up, 1)

                def stage_sums(i, b, blocks):
                    if later(i, 2):
                        act.wait_ge(prod_ready, i - 1)
                    act.activation(agg[:, b, 0:len(blocks)], acc[:, bass.ds(i * QB, len(blocks)), :], ACT.Copy
                                   ).then_inc(agg_ready, 1)

                def turn(i, b, blocks):
                    act.wait_ge(turned_ready, i + 1)
                    if later(i, 2):
                        act.wait_ge(both_ready, i - 1)
                    act.activation(x1t[:, b, 0:len(blocks)], turned[:, 0:len(blocks)], ACT.Copy
                                   ).then_inc(x1t_ready, 1)

                def scale_features(i, b, blocks):
                    act.wait_ge(both_ready, i + 1)
                    if later(i, 2):
                        act.wait_ge(feat_stored[b], (i - b) * 16)
                    for j, n in enumerate(blocks):
                        last = act.activation(feat[0:n, b, j], both[b][0:n, j, :], ACT.Copy,
                                              scale=c.node_vec[0:n, bass.ds(i * QB + j, 1)])
                    last.then_inc(feat_ready, 1)

                staged_steps(act, [stage_sums, lambda i, b, blocks: s.take_root(act, i, b, blocks), turn, None,
                                   scale_features])

            @block.tensor
            def _(pe):
                def convolve(i, b, blocks):
                    pe.wait_ge(agg_ready, i + 1)
                    if later(i, 2):
                        pe.wait_ge(y_ready, i - 1)
                    for j, n in enumerate(blocks):
                        mm = pe.matmul(prod[b][0:n, j, :], agg[:, b, j, 0:n], c.w2[:], start=True, stop=True)
                    mm.then_inc(prod_ready, 1)

                def turn(i, b, blocks):
                    pe.wait_ge(x1_ready, i + 1)
                    if later(i, 1):
                        pe.wait_ge(x1t_ready, i)
                    for j, n in enumerate(blocks):
                        mm = pe.transpose(turned[:, j, 0:n], x1[0:n, b, j], c.ident[0:n, 0:n])
                    mm.then_inc(turned_ready, 1)

                def features(i, b, blocks):
                    pe.wait_ge(x1t_ready, i + 1)
                    if later(i, 2):
                        pe.wait_ge(feat_ready, i - 1)
                    for j, n in enumerate(blocks):
                        mm = pe.matmul(both[b][0:n, j, :], x1t[:, b, j, 0:n], c.w_node[:], start=True, stop=True)
                    mm.then_inc(both_ready, 1)

                pe.wait_ge(s.set_up, 1)
                staged_steps(pe, [convolve, None, turn, features])

            @block.vector
            def _(dve):
                dve.memset(turned[:], 0.0)
                s.clear(dve)

                def residual(i, b, blocks):
                    if blocks[-1] < P:
                        dve.wait_ge(tail, 16 * len(blocks))
                    else:
                        dve.wait_ge(landed[b], (i - b) * 8 + 16)
                    dve.wait_ge(prod_ready, i + 1)
                    if later(i, 1):
                        dve.wait_ge(y_ready, i)
                    for j, n in enumerate(blocks):
                        last = dve.scalar_tensor_tensor(h[0:n, j], prod[b][0:n, j, :],
                                                        c.din[0:n, bass.ds(i * QB + j, 1)], c.b2[0:n],
                                                        ALU.mult, ALU.add)
                    last.then_inc(chain_sem, 1)
                    dve.wait_ge(chain_sem, i + 1)
                    if later(i, 2):
                        dve.wait_ge(x1_ready, i - 1)
                    for j, n in enumerate(blocks):
                        last = dve.tensor_tensor(y[0:n, b, j], h[0:n, j], xin[0:n, b, j], ALU.add)
                    last.then_inc(y_ready, 1)
                    dve.wait_ge(s.set_up, 1)
                    dve.wait_ge(y_ready, i + 1)
                    s.statistics(dve, y[:, b], i, b, blocks)

                def normalise(i, b, blocks):
                    s.invert_root(dve, i, b, blocks)
                    if later(i, 2):
                        dve.wait_ge(turned_ready, i - 1)
                        dve.wait_ge(x1_stored[b], (i - b) * 8)
                    s.apply(dve, y[:, b], x1[:, b], i, b, blocks).then_inc(x1_ready, 1)

                staged_steps(dve, [residual, normalise])


def product_edges(nc, c, table, edges, attr, scalars, acc_ad, acc_bc):
    ctx = ExitStack()
    with ctx:
        def sb(n, shape, dt=F32):
            return ctx.enter_context(nc.sbuf_tensor("t_" + n, shape, dt))

        def ps(n, shape=(P, 512)):
            return ctx.enter_context(nc.psum_tensor("t_" + n, list(shape), F32))

        def sem(n):
            return ctx.enter_context(nc.semaphore("t_" + n))

        ends = sb("ends", [P, SLOTS, 2 * T], I32)
        attrs = sb("attrs", [P, SLOTS, T, 4])
        scal = sb("scal", [P, SLOTS, T * ES])
        rows = sb("rows", [P, SLOTS, T, D])
        scal_t = sb("scal_t", [P, T // 2 * P])
        hidden = sb("hidden", [P, T // 2 * P])
        ad = sb("ad", [P, 2, T, 2 * MUL])
        cg = sb("cg", [P, T, MUL])
        ge = sb("ge", [P, T, 3, MUL])
        dot = sb("dot", [P, T, MUL])
        dot3 = sb("dot3", [P, T, MUL])
        msg_ad = sb("msg_ad", [P, 2, T, D])
        msg_bc = sb("msg_bc", [P, 2, T, D])
        rel = sb("rel", [P, T])
        hot = sb("hot", [P, T, P])
        iota = ps("iota")
        sums = ps("sums")
        turned = ps("turned")
        layer1 = ps("layer1")
        weight = [ps(f"weight{i}", (P, T, 4 * MUL)) for i in range(2)]
        ends_landed = [sem(f"ends_landed{i}") for i in range(SLOTS)]
        attrs_landed = [sem(f"attrs_landed{i}") for i in range(SLOTS)]
        scal_landed = [sem(f"scal_landed{i}") for i in range(SLOTS)]
        rows_landed = [sem(f"rows_landed{i}") for i in range(SLOTS)]
        groups_past, cleared, rel_ready, hot_ready, sums_ready, sums_added = [
            sem(n) for n in ("groups_past", "cleared", "rel_ready", "hot_ready", "sums_ready", "sums_added")]
        turned_ready, scal_t_ready, layer1_ready, hidden_ready, weight_ready, msg_ready, chain_sem = [
            sem(n) for n in ("turned_ready", "scal_t_ready", "layer1_ready", "hidden_ready", "weight_ready",
                             "msg_ready", "chain")]
        ad_ready = sem("ad_ready")

        with nc.Block() as block:
            @block.sync
            def _(sp):
                past_reg, landed_reg = sp.alloc_register("t_sp_past"), sp.alloc_register("t_sp_landed")

                def body(g, slot, r):
                    at = g * GE if not isinstance(g, int) else min(g * GE, E - GE)
                    if later(g, SLOTS):
                        past = worked_out(sp, past_reg, g - (SLOTS - 1))
                        landed = worked_out(sp, landed_reg, r * (16 * T))
                        sp.wait_ge(turned_ready, past)
                    sp.dma_start(scal[:, slot], scalars[bass.ds(at, GE), :].rearrange("(p t) e -> p (t e)", t=T)
                                 ).then_inc(scal_landed[slot], 16)
                    if later(g, SLOTS):
                        sp.wait_ge(groups_past, past)
                        sp.wait_ge(rows_landed[slot], landed)
                    sp.dma_start(ends[:, slot, :], edges[bass.ds(g, 1)].rearrange("a p e -> p (a e)")
                                 ).then_inc(ends_landed[slot], 16)
                    if later(g, SLOTS):
                        sp.wait_ge(msg_ready, past)
                    sp.dma_start(attrs[:, slot].rearrange("p t k -> p (t k)"),
                                 attr[bass.ds(at, GE), :].rearrange("(p t) e -> p (t e)", t=T)
                                 ).then_inc(attrs_landed[slot], 16)
                split_groups(sp, body)

            @block.gpsimd
            def _(pool):
                landed_reg, past_reg = pool.alloc_register("t_pool_landed"), pool.alloc_register("t_pool_past")

                def body(g, slot, r):
                    landed = worked_out(pool, landed_reg, r * 16 + 16)
                    past = worked_out(pool, past_reg, g - (SLOTS - 1))
                    pool.wait_ge(ends_landed[0], 16)
                    pool.wait_ge(ends_landed[slot], landed)
                    if later(g, SLOTS):
                        pool.wait_ge(msg_ready, past)
                    for t in range(T):
                        pool.indirect_dma_start(
                            out=rows[:, slot, t, :], out_offset=None, in_=table,
                            in_offset=bass.IndirectOffsetOnAxis(ap=ends[:, slot, t:t + 1], axis=0),
                        ).then_inc(rows_landed[slot], 16)
                split_groups(pool, body)

            @block.scalar
            def _(act):
                def turn(g):
                    act.wait_ge(turned_ready, g + 1)
                    if later(g, 1):
                        act.wait_ge(layer1_ready, g)
                    act.activation(scal_t[:], turned[:], ACT.Copy).then_inc(scal_t_ready, 1)

                def hide(g):
                    act.wait_ge(layer1_ready, g + 1)
                    if later(g, 1):
                        act.wait_ge(weight_ready, g)
                    act.activation(hidden[:], layer1[:], ACT.Silu, scale=0.125).then_inc(hidden_ready, 1)

                def scale_ad(g, slot, r):
                    act.wait_ge(attrs_landed[slot], r * 16 + 16)
                    if later(g, 2):
                        act.wait_ge(msg_ready, g - 1)
                    act.wait_ge(weight_ready, g + 1)
                    for t in range(T):
                        mul = act.activation(ad[:, slot % 2, t], weight[slot % 2][:, t, 0:2 * MUL], ACT.Copy,
                                             scale=attrs[:, slot, t, 0:1])
                    mul.then_inc(ad_ready, 1)

                turn(0)
                hide(0)
                turn(1)
                scale_ad(0, 0, 0)
                hide(1)

                def body(g, slot, r):
                    if not isinstance(g, int) or g + 2 < NG:
                        turn(g + 2)
                    if not isinstance(g, int) or g + 1 < NG:
                        scale_ad(g + 1, (slot + 1) % SLOTS, r + (slot + 1) // SLOTS)
                    if not isinstance(g, int) or g + 2 < NG:
                        hide(g + 2)
                split_groups(act, body)

            @block.tensor
            def _(pe):
                visits = pe.alloc_register("t_pe_visits")
                bounds = Bounds(pe, "t_pe_bound", c)
                bounds.load(0, 0)
                pe.reg_mov(visits, 1)

                def turn(g, slot, r):
                    pe.wait_ge(scal_landed[slot], r * 16 + 16)
                    if later(g, 1):
                        pe.wait_ge(scal_t_ready, g)
                    for j in range(T // 2):
                        mm = pe.transpose(turned[:, j * P:(j + 1) * P], scal[:, slot, j * P:(j + 1) * P],
                                          c.ident[:])
                    mm.then_inc(turned_ready, 1)

                def layer_1(g):
                    pe.wait_ge(scal_t_ready, g + 1)
                    if later(g, 1):
                        pe.wait_ge(hidden_ready, g)
                    pe.matmul(layer1[:], c.w_fc1[:], scal_t[:], start=True, stop=True).then_inc(layer1_ready, 1)

                def layer_2(g, b):
                    pe.wait_ge(hidden_ready, g + 1)
                    if later(g, 2):
                        pe.wait_ge(msg_ready, g - 1)
                    for j in range(T // 2):
                        mm = pe.matmul(weight[b][:, 2 * j:2 * j + 2, :], hidden[:, j * P:(j + 1) * P],
                                       c.w_fc2[:], start=True, stop=True)
                    mm.then_inc(weight_ready, 1)

                turn(0, 0, 0)
                layer_1(0)
                turn(1, 1, 0)
                layer_2(0, 0)
                layer_1(1)

                def body(g, slot, r):
                    first, past = bounds.of(slot)
                    if not isinstance(g, int) or g + 2 < NG:
                        turn(g + 2, (slot + 2) % SLOTS, r + (slot + 2) // SLOTS)
                    if not isinstance(g, int) or g + 1 < NG:
                        layer_2(g + 1, (slot + 1) % 2)
                    bounds.load_next(g, slot)
                    if not isinstance(g, int) or g + 2 < NG:
                        layer_1(g + 2)
                    msg_due = pe.snap(g + 1)
                    with pe.Fori(first, past):
                        pe.wait_ge(msg_ready, msg_due)
                        pe.wait_ge(hot_ready, visits)
                        for t in range(T):
                            pe.matmul(sums[:, 0:P], msg_ad[:, slot % 2, t, :], hot[:, t, :],
                                      start=t == 0, stop=t == T - 1)
                        for t in range(T):
                            mm = pe.matmul(sums[:, P:2 * P], msg_bc[:, slot % 2, t, :], hot[:, t, :],
                                           start=t == 0, stop=t == T - 1)
                        mm.then_inc(sums_ready, 1)
                        pe.reg_add(visits, visits, 1)
                split_groups(pe, body)

            @block.vector
            def _(dve):
                dve.memset(acc_ad[:], 0.0)
                dve.memset(acc_bc[:], 0.0)
                dve.memset(sums[:], 0.0)
                dve.tensor_copy(iota[:, 0:P], c.iota[:]).then_inc(cleared, 1)
                dve.wait_ge(cleared, 1)
                visits = dve.alloc_register("t_dve_visits")
                rels = dve.alloc_register("t_dve_rels")
                before = dve.alloc_register("t_dve_before")
                bounds = Bounds(dve, "t_dve_bound", c)
                bounds.load(0, 0)
                dve.reg_mov(visits, 0)
                dve.reg_mov(rels, 0)
                dve.reg_mov(before, NB)
                LINKS = 5

                def add_sums():
                    at = dve.snap(before, min_val=0, max_val=NB)
                    dve.wait_ge(sums_ready, visits)
                    dve.wait_ge(sums_added, visits)
                    dve.tensor_tensor(acc_ad[:, at, :], acc_ad[:, at, :], sums[:, 0:P], ALU.add)
                    dve.tensor_tensor(acc_bc[:, at, :], acc_bc[:, at, :], sums[:, P:2 * P], ALU.add
                                      ).then_inc(sums_added, 1)

                def messages(g, slot, r):
                    b = slot % 2
                    w = weight[b]
                    e0 = attrs[:, slot, :, 0:1]
                    e1 = attrs[:, slot, :, 1:4]
                    g0 = rows[:, slot, :, 0:MUL]
                    g1 = rows[:, slot, :, MUL:D].rearrange("p t (k u) -> p t k u", k=3)
                    base = g * LINKS
                    wide = [P, T, 3, MUL]
                    dve.wait_ge(attrs_landed[slot], r * 16 + 16)
                    dve.wait_ge(rows_landed[slot], r * (16 * T) + 16 * T)
                    if later(g, 1):
                        dve.wait_ge(msg_ready, g)
                    dve.tensor_tensor(ge[:], g1, e1[:, :, :, None].to_broadcast(wide), ALU.mult
                                      ).then_inc(chain_sem, 1)
                    dve.wait_ge(ad_ready, g + 1)
                    dve.tensor_tensor(cg[:], w[:, :, 2 * MUL:3 * MUL], g0, ALU.mult).then_inc(chain_sem, 1)
                    dve.tensor_tensor(msg_ad[:, b, :, MUL:D].rearrange("p t (k u) -> p t k u", k=3),
                                      ad[:, b, :, None, MUL:2 * MUL].to_broadcast(wide), g1, ALU.mult)
                    dve.tensor_tensor(msg_ad[:, b, :, 0:MUL], ad[:, b, :, 0:MUL], g0, ALU.mult
                                      ).then_inc(chain_sem, 1)
                    bounds.load_next(g, slot)
                    dve.wait_ge(chain_sem, base + 3)
                    dve.tensor_tensor(dot[:], ge[:, :, 0], ge[:, :, 1], ALU.add).then_inc(chain_sem, 1)
                    dve.tensor_tensor(msg_bc[:, b, :, MUL:D].rearrange("p t (k u) -> p t k u", k=3),
                                      cg[:, :, None, :].to_broadcast(wide),
                                      e1[:, :, :, None].to_broadcast(wide), ALU.mult)
                    dve.wait_ge(chain_sem, base + 4)
                    dve.tensor_tensor(dot3[:], dot[:], ge[:, :, 2], ALU.add).then_inc(chain_sem, 1)
                    dve.wait_ge(chain_sem, base + 5)
                    dve.tensor_tensor(msg_bc[:, b, :, 0:MUL], w[:, :, 3 * MUL:4 * MUL], dot3[:], ALU.mult
                                      ).then_inc(msg_ready, 1)

                def body(g, slot, r):
                    first, past = bounds.of(slot)
                    messages(g, slot, r)
                    dve.wait_ge(ends_landed[slot], r * 16 + 16)
                    dve.wait_ge(rel_ready, rels)
                    dve.tensor_scalar(rel[:], ends[:, slot, T:2 * T], c.base[:, bass.ds(g, 1)], None,
                                      ALU.subtract).then_inc(rel_ready, 1)
                    dve.reg_add(rels, rels, 1)
                    with dve.Fori(first, past) as blk:
                        add_sums()
                        dve.wait_ge(rel_ready, rels)
                        dve.tensor_tensor(hot[:], iota[:, None, 0:P].to_broadcast([P, T, P]),
                                          rel[:, :, None].to_broadcast([P, T, P]), ALU.is_equal
                                          ).then_inc(hot_ready, 1)
                        dve.reg_add(visits, visits, 1)
                        dve.reg_add(rels, rels, 1)
                        dve.reg_mov(before, blk)
                        dve.wait_ge(hot_ready, visits)
                        dve.tensor_scalar(rel[:], rel[:], float(-P), None, ALU.add).then_inc(rel_ready, 1)
                    dve.sem_inc(groups_past, 1)
                split_groups(dve, body)
                add_sums()


def last_nodes(nc, c, acc_ad, acc_bc, x1_dram, skip_dram, out_dram):
    ctx = ExitStack()
    with ctx:
        def sb(n, shape):
            return ctx.enter_context(nc.sbuf_tensor("n3_" + n, shape, F32))

        def sem(n):
            return ctx.enter_context(nc.semaphore("n3_" + n))

        W = D + 1
        agg = sb("agg", [P, 2, 2, QB, P])
        x1 = sb("x1", [P, 2, QB, D])
        skip = sb("skip", [P, 2, QB, D])
        mix = sb("mix", [P, QB, D])
        y = sb("y", [P, 2, QB, D])
        out = sb("out", [P, 2, QB, D])
        raw, angle, turns, whole, r1, r2, r3, fold, cos_arg, sin_arg, cos, sin, sin_vec = [
            sb(n, [P, NB]) for n in ("raw", "angle", "turns", "whole", "r1", "r2", "r3", "fold", "cos_arg",
                                     "sin_arg", "cos", "sin", "sin_vec")]
        s = Norm(nc, ctx, "n3_")
        conv = [ctx.enter_context(nc.psum_tensor(f"n3_conv{b}", [P, 2, 512], F32)) for b in range(2)]
        agg_ready, conv_ready, conv_kept, angles, trig_ready, mix_ready, y_ready, out_ready, tail = [
            sem(n) for n in ("agg_ready", "conv_ready", "conv_kept", "angles", "trig_ready", "mix_ready",
                             "y_ready", "out_ready", "tail")]
        s.semaphores(sem)
        landed = [sem(f"landed{i}") for i in range(2)]
        stored = [sem(f"stored{i}") for i in range(2)]

        with nc.Block() as block:
            @block.sync
            def _(sp):
                def load(i, b, blocks):
                    if later(i, 2):
                        sp.wait_ge(y_ready, i - 1)
                    for dst, src in ((x1, x1_dram), (skip, skip_dram)):
                        for p, sl, rows in rows_of(src, i, blocks):
                            sp.dma_start(dst[p, b, sl], rows).then_inc(tail if blocks[-1] < P else landed[b], 16)

                def store(i, b, blocks):
                    sp.wait_ge(out_ready, i + 1)
                    for p, sl, rows in rows_of(out_dram, i, blocks):
                        sp.dma_start(rows, out[p, b, sl]).then_inc(stored[b], 16)

                staged_steps(sp, [load, None, store])
                for b in range(2):
                    sp.wait_ge(stored[b], 16 * stores_of(b))

            @block.scalar
            def _(act):
                def stage_sums(i, b, blocks):
                    k = len(blocks)
                    if later(i, 2):
                        act.wait_ge(conv_ready, i - 1)
                    act.activation(agg[:, b, 0, 0:k], acc_ad[:, bass.ds(i * QB, k), :], ACT.Copy)
                    act.activation(agg[:, b, 1, 0:k], acc_bc[:, bass.ds(i * QB, k), :], ACT.Copy
                                   ).then_inc(agg_ready, 1)

                node_steps(act, stage_sums)
                act.wait_ge(angles, 9)
                act.activation(cos[:], cos_arg[:], ACT.Sin).then_inc(trig_ready, 1)
                act.activation(sin[:], sin_arg[:], ACT.Sin).then_inc(trig_ready, 1)
                act.wait_ge(s.set_up, 1)
                staged_steps(act, [None, lambda i, b, blocks: s.take_root(act, i, b, blocks)])

            @block.tensor
            def _(pe):
                def body(i, b, blocks):
                    pe.wait_ge(agg_ready, i + 1)
                    if later(i, 2):
                        pe.wait_ge(conv_kept, i - 1)
                    for j, n in enumerate(blocks):
                        to = conv[b][0:n, j // 2, (j % 2) * W:(j % 2 + 1) * W]
                        pe.matmul(to, agg[:, b, 0, j, 0:n], c.w_ad[:], start=True, stop=False)
                        mm = pe.matmul(to, agg[:, b, 1, j, 0:n], c.w_bc[:], start=False, stop=True)
                    mm.then_inc(conv_ready, 1)
                node_steps(pe, body)

            @block.vector
            def _(dve):
                dve.memset(raw[:], 0.0)
                s.clear(dve)

                def keep(i, b, blocks):
                    dve.wait_ge(conv_ready, i + 1)
                    pairs = [(j, 2, P) for j in range(0, QB, 2)] if blocks[-1] == P else [
                        (j, 1, n) for j, n in enumerate(blocks)]
                    for j, k, n in pairs:
                        both = conv[b][0:n, j // 2, (j % 2) * W:(j % 2 + k) * W].rearrange("p (k w) -> p k w", k=k)
                        dve.tensor_copy(acc_ad[0:n, bass.ds(i * QB + j, k), :], both[:, :, 0:D])
                        last = dve.tensor_copy(raw[0:n, bass.ds(i * QB + j, k)], both[:, :, D])
                    last.then_inc(conv_kept, 1)
                node_steps(dve, keep)
                dve.wait_ge(conv_kept, NQ + 1)

                def link(n, ins):
                    ins.then_inc(angles, 1)
                    dve.wait_ge(angles, n)

                link(1, dve.tensor_tensor(angle[:], raw[:], c.node_vec[:], ALU.mult))
                link(2, dve.tensor_scalar(turns[:], angle[:], 1.0 / (2 * PI), ROUND, ALU.mult, ALU.add))
                link(3, dve.tensor_scalar(whole[:], turns[:], -ROUND, None, ALU.add))
                link(4, dve.scalar_tensor_tensor(r1[:], whole[:], -TAU_A, angle[:], ALU.mult, ALU.add))
                link(5, dve.scalar_tensor_tensor(r2[:], whole[:], -TAU_B, r1[:], ALU.mult, ALU.add))
                link(6, dve.scalar_tensor_tensor(r3[:], whole[:], -TAU_C, r2[:], ALU.mult, ALU.add))
                link(7, dve.scalar_tensor_tensor(fold[:], r3[:], -1.0, r3[:], ALU.mult, ALU.max))
                link(8, dve.tensor_scalar(cos_arg[:], fold[:], -1.0, PI / 2, ALU.mult, ALU.add))
                link(9, dve.tensor_scalar(sin_arg[:], r3[:], SINE_END, -SINE_END, ALU.min, ALU.max))
                dve.wait_ge(trig_ready, 2)
                link(10, dve.tensor_tensor(sin_vec[:], sin[:], c.node_vec[:], ALU.mult))

                def residual(i, b, blocks):
                    if blocks[-1] < P:
                        dve.wait_ge(tail, 32 * len(blocks))
                    else:
                        dve.wait_ge(landed[b], (i - b) * 16 + 32)
                    if later(i, 1):
                        dve.wait_ge(y_ready, i)
                    for j, n in enumerate(blocks):
                        last = dve.scalar_tensor_tensor(mix[0:n, j], skip[0:n, b, j],
                                                        cos[0:n, bass.ds(i * QB + j, 1)], x1[0:n, b, j],
                                                        ALU.mult, ALU.add)
                    last.then_inc(mix_ready, 1)
                    dve.wait_ge(mix_ready, i + 1)
                    if later(i, 2):
                        dve.wait_ge(out_ready, i - 1)
                    for j, n in enumerate(blocks):
                        at = bass.ds(i * QB + j, 1)
                        last = dve.scalar_tensor_tensor(y[0:n, b, j], acc_ad[0:n, at, :].rearrange("p a d -> p (a d)"),
                                                        sin_vec[0:n, at], mix[0:n, j], ALU.mult, ALU.add)
                    last.then_inc(y_ready, 1)
                    dve.wait_ge(s.set_up, 1)
                    dve.wait_ge(y_ready, i + 1)
                    s.statistics(dve, y[:, b], i, b, blocks)

                def normalise(i, b, blocks):
                    s.invert_root(dve, i, b, blocks)
                    if later(i, 2):
                        dve.wait_ge(stored[b], (i - b) * 8)
                    s.apply(dve, y[:, b], out[:, b], i, b, blocks).then_inc(out_ready, 1)

                staged_steps(dve, [residual, normalise])


def gnn_kernel(nc, x, edges, dst_groups, src, attr, scalars, node_vec, w, out):
    def dram(name, shape, dt=F32):
        return nc.dram_tensor(name, shape, dt, kind="Internal").ap()

    bounds_dram = dram("bounds_dram", [TC * P, 2], I32)
    base_dram = dram("base_dram", [TC * P])
    degree_dram = dram("degree_dram", [NB, P])
    table_0, table_1, table_2 = (dram(f"table_{i}", [N, D]) for i in range(3))
    x1_dram = dram("x1_dram", [N, D])
    skip_dram = dram("skip_dram", [N, D])

    class Kept:
        pass

    ctx = ExitStack()
    with ctx:
        def sb(name, shape, dt=F32):
            return ctx.enter_context(nc.sbuf_tensor(name, shape, dt))

        c = Kept()
        c.iota = sb("c_iota", [P, P])
        c.ident = sb("c_ident", [P, P])
        c.one_row = sb("c_one_row", [P, 1])
        c.w1, c.w2 = sb("c_w1", [D, D]), sb("c_w2", [D, D])
        c.b1, c.b2 = sb("c_b1", [P, D]), sb("c_b2", [P, D])
        c.w_node = sb("c_w_node", [D, 2 * D])
        c.w_ad, c.w_bc = sb("c_w_ad", [P, D + 1]), sb("c_w_bc", [P, D + 1])
        c.w_fc1 = sb("c_w_fc1", [2 * ES, 2 * ES])
        c.w_fc2 = sb("c_w_fc2", [2 * ES, 2 * P])
        c.bounds = sb("c_bounds", [1, TC * P * 2], I32)
        c.base = sb("c_base", [P, TC * P])
        c.node_vec = sb("c_node_vec", [P, NB])
        c.dout, c.din, c.dinout = sb("c_dout", [P, NB]), sb("c_din", [P, NB]), sb("c_dinout", [P, NB])

        constants(nc, c, w)
        bounds_table(nc, c, dst_groups, bounds_dram, base_dram)
        source_degrees(nc, c, src, node_vec)
        scaled_table(nc, c, x, table_0)
        with nc.sbuf_tensor("acc_0", [D, NB + 1, P], F32) as acc:
            with nc.sbuf_tensor("degree_row", [1, NB + 1, P], F32) as degree_row:
                convolve_edges(nc, c, "c1", table_0, edges, acc, degree_row)
                inward_degrees(nc, c, degree_row, degree_dram)
            first_nodes(nc, c, acc, table_1)
            convolve_edges(nc, c, "c2", table_1, edges, acc, None)
            second_nodes(nc, c, x, acc, x1_dram, table_2, skip_dram)
        with nc.sbuf_tensor("acc_ad", [D, NB + 1, P], F32) as acc_ad, \
                nc.sbuf_tensor("acc_bc", [D, NB + 1, P], F32) as acc_bc:
            product_edges(nc, c, table_2, edges, attr, scalars, acc_ad, acc_bc)
            last_nodes(nc, c, acc_ad, acc_bc, x1_dram, skip_dram, out)


WEIGHTS = ["L0_gnn_W1", "L0_gnn_b1", "L0_gnn_W2", "L0_gnn_b2", "L1_gnn_W_sc0", "L1_gnn_W_sc1", "L1_gnn_W_l1_0",
           "L1_gnn_W_l1_1", "L1_gnn_W_fc1", "L1_gnn_W_fc2", "L1_gnn_W_l2_A0", "L1_gnn_W_l2_B0", "L1_gnn_W_l2_C1",
           "L1_gnn_W_l2_D1", "L1_gnn_W_l3_A", "L1_gnn_W_l3_B"]


def kernel(**inputs):
    import concourse.bacc as bacc
    from concourse.bass_utils import run_bass_kernel_spmd

    src, dst = np.asarray(inputs["src"]), np.asarray(inputs["dst"])
    full = (NG - 1) * GE
    repeated = full - (E - GE)
    src_groups = np.concatenate([src[:full], src[E - GE:]]).reshape(NG, P, T)
    far = np.full(repeated, FAR, dst.dtype)
    dst_groups = np.concatenate([dst[:full], far, dst[full:]]).reshape(NG, GE)
    edges = np.concatenate([src_groups, dst_groups.reshape(NG, P, T)], axis=2)

    nc = bacc.Bacc("TRN2", target_bir_lowering=False, num_devices=1)
    arrays = {}

    def given(name, a):
        a = np.ascontiguousarray(a)
        arrays[f"in_{name}"] = a
        return nc.dram_tensor(f"in_{name}", a.shape, mybir.dt.from_np(a.dtype), kind="ExternalInput").ap()

    x = given("x", inputs["x"])
    edges_d = given("edges", edges)
    dst_d = given("dst_groups", dst_groups)
    src_d = given("src", src)
    attr = given("edge_attr_4", inputs["edge_attr_4"])
    scalars = given("edge_attr_64", inputs["edge_attr_64"])
    node_vec = given("node_vec1", inputs["node_vec1"])
    w = {name: given(name, inputs[name]) for name in WEIGHTS}
    out = nc.dram_tensor("out_0", [N, D], F32, kind="ExternalOutput").ap()
    gnn_kernel(nc, x, edges_d, dst_d, src_d, attr, scalars, node_vec, w, out)
    result = run_bass_kernel_spmd(nc, [arrays], core_ids=[0])
    return result.results[0]["out_0"]
```

```python
from contextlib import ExitStack

import numpy as np
import concourse.bass as bass
from concourse import mybir
from concourse.alu_op_type import AluOpType as ALU

ACT = mybir.ActivationFunctionType
AX = mybir.AxisListType
F32 = mybir.dt.float32
BF16 = mybir.dt.bfloat16
I32 = mybir.dt.int32

P = 128
N = 12500
E = 412500
D = 128
MUL = 32
ES = 64
NB = -(-N // P)
TAIL = N - (NB - 1) * P
T = 8
GE = P * T
NG = -(-E // GE)
SLOTS = 8
FAR = 1 << 14
HP = 125
HC = E // HP
HT = 22
NCH = HC // HT
BY_DVE = 4
HR = NCH // (BY_DVE + 1)
assert HR * (BY_DVE + 1) == NCH and HR % 2 == 0 and BY_DVE % 2 == 0
TC = -(-NG // P)
QB = 4
NQ = (NB - 1) // QB
PEELED = 8
AHEAD = 4
assert PEELED % AHEAD == 0 and NQ % AHEAD == 0
EPS = 1e-5
K_MSG = 1.679 / 8.0 / 4.0 / 8.0
K_DOT = K_MSG / 3.0 ** 0.5
K_F = 1.0 / 32.0 ** 0.5
PI = float(np.pi)
SINE_END = 3.1415925
ROUND = 1.5 * 2.0 ** 23
TAU_A = 6.28125
TAU_B = float(np.float32(np.floor((2 * np.pi - TAU_A) * 2.0 ** 21) / 2.0 ** 21))
TAU_C = float(np.float32(2 * np.pi - TAU_A - TAU_B))


def split_groups(engine, body):
    rounds = NG // SLOTS
    for g in range(SLOTS):
        body(g, g, 0)
    with engine.Fori(1, rounds) as r:
        for s in range(SLOTS):
            body(r * SLOTS + s, s, r)
    for g in range(rounds * SLOTS, NG):
        body(g, g % SLOTS, rounds)


def node_steps(engine, body):
    full = [P] * QB
    body(0, 0, full)
    body(1, 1, full)
    with engine.Fori(1, NQ // 2) as h:
        for j in range(2):
            body(h * 2 + j, j, full)
    body(NQ, NQ % 2, [P] * (NB - 1 - NQ * QB) + [TAIL])


def staged_steps(engine, stages, slots=2):
    def round_of(i, slot):
        for k, stage in enumerate(stages):
            if stage is not None and (not isinstance(i, int) or 0 <= i - k <= NQ):
                last = isinstance(i, int) and i - k == NQ
                stage(i - k, (slot - k) % slots, [P] * (NB - 1 - NQ * QB) + [TAIL] if last else [P] * QB)

    for i in range(PEELED):
        round_of(i, i % slots)
    with engine.Fori(PEELED // slots, NQ // slots) as h:
        for j in range(slots):
            round_of(h * slots + j, j)
    for i in range(NQ, NQ + len(stages)):
        round_of(i, i % slots)


def rows_of(dram, step, blocks):
    if blocks[-1] == P:
        return [(slice(0, P), slice(0, len(blocks)),
                 dram[bass.ds(step * (QB * P), QB * P), :].rearrange("(s p) d -> p s d", p=P))]
    out = []
    for j, n in enumerate(blocks):
        r0 = (step * QB + j) * P
        out.append((slice(0, n), slice(j, j + 1), dram[r0:r0 + n, :].rearrange("(s p) d -> p s d", s=1)))
    return out


def later(g, n):
    return not isinstance(g, int) or g >= n


def worked_out(engine, reg, value):
    if isinstance(value, int):
        return value
    engine.reg_mov(reg, value)
    return reg


class Bounds:

    def __init__(self, engine, name, c):
        self.engine, self.c = engine, c
        self.pairs = [[engine.alloc_register(f"{name}_{p}{i}") for i in range(4)] for p in "ab"]

    def load(self, g, pair):
        self.engine.load(self.pairs[pair], self.c.bounds[0:1, bass.ds(g * 2, 4)])

    def load_next(self, g, slot):
        if slot % 2 == 1 and (not isinstance(g, int) or g + 1 < NG):
            self.load(g + 1, (slot // 2 + 1) % 2)

    def of(self, slot):
        pair = self.pairs[slot // 2 % 2]
        return pair[slot % 2 * 2], pair[slot % 2 * 2 + 1]


class Constants:

    def __init__(self, nc, ctx, c, w):
        self.c, self.w, self.n_loads = c, w, 0

        def sb(name, shape, dt=F32):
            return ctx.enter_context(nc.sbuf_tensor(name, shape, dt))

        def sem(name):
            return ctx.enter_context(nc.semaphore(name))

        self.iota_i = sb("iota_i", [P, P], I32)
        self.col_i = sb("col_i", [P, 1], I32)
        self.col = sb("col", [P, 1])
        self.vec_i = sb("vec_i", [P, 3, MUL], I32)
        self.vec_hit = sb("vec_hit", [P, 3, MUL])
        self.vec_mask = sb("vec_mask", [P, 3])
        self.quad_i = sb("quad_i", [P, 4], I32)
        self.quad_ge = sb("quad_ge", [P, 4])
        self.quad_mask = sb("quad_mask", [P, 4])
        self.w_f = sb("w_f", [P, MUL])
        self.w_sc = sb("w_sc", [P, MUL])
        self.w_ad = sb("w_ad", [P, MUL])
        self.w_bc = sb("w_bc", [P, MUL])
        self.l3 = sb("l3", [P, 2])
        self.loaded = sem("weights_loaded")
        self.iotas = sem("iotas_made")
        self.cleared = sem("weights_cleared")
        self.made = sem("masks_made")

    def make_iotas(self, pool):
        pool.iota(self.iota_i[:], [[1, P]], base=0, channel_multiplier=0).then_inc(self.iotas, 1)
        pool.iota(self.col_i[:], [[1, 1]], base=0, channel_multiplier=1).then_inc(self.iotas, 1)
        pool.iota(self.vec_i[:], [[1, 3], [3, MUL]], base=MUL, channel_multiplier=-1).then_inc(self.iotas, 1)
        pool.iota(self.quad_i[:], [[-MUL, 4]], base=0, channel_multiplier=1).then_inc(self.iotas, 1)

    def load(self, sp):
        c, w = self.c, self.w

        def load(dst, src):
            self.n_loads += 1
            sp.dma_start(dst, src).then_inc(self.loaded, 16)

        load(c.w1[:], w["L0_gnn_W1"])
        load(c.w2[:], w["L0_gnn_W2"])
        load(c.b1[:], w["L0_gnn_b1"].partition_broadcast(P))
        load(c.b2[:], w["L0_gnn_b2"].partition_broadcast(P))
        load(self.w_f[0:MUL, :], w["L1_gnn_W_l1_0"])
        load(self.w_sc[0:MUL, :], w["L1_gnn_W_sc0"])
        for dst, name in ((self.w_f, "L1_gnn_W_l1_1"), (self.w_sc, "L1_gnn_W_sc1")):
            src = w[name]
            load(dst[MUL:P, :], bass.AP(tensor=src.tensor, offset=src.offset,
                                        ap=[[MUL, MUL], [0, 3], [1, MUL]]))
        load(self.w_ad[0:MUL, :], w["L1_gnn_W_l2_A0"])
        load(self.w_bc[0:MUL, :], w["L1_gnn_W_l2_B0"])
        for k in range(3):
            rows = slice(MUL * (k + 1), MUL * (k + 2))
            load(self.w_ad[rows, :], w["L1_gnn_W_l2_D1"])
            load(self.w_bc[rows, :], w["L1_gnn_W_l2_C1"])
        sp.wait_ge(self.cleared, 1)
        load(self.l3[0:MUL, 0:1], w["L1_gnn_W_l3_A"])
        load(self.l3[0:MUL, 1:2], w["L1_gnn_W_l3_B"])
        for i in range(2):
            half = slice(ES * i, ES * (i + 1))
            load(c.w_fc1[half, half], w["L1_gnn_W_fc1"])
            for to, at in enumerate((0, 2, 1, 3)):
                load(c.w_fc2[half, P * i + MUL * to:P * i + MUL * (to + 1)],
                     w["L1_gnn_W_fc2"][:, MUL * at:MUL * (at + 1)])

    def make_masks(self, dve):
        c = self.c
        dve.memset(self.l3[:], 0.0)
        dve.memset(c.w_fc1[:], 0.0)
        dve.memset(c.w_fc2[:], 0.0).then_inc(self.cleared, 1)
        dve.memset(c.one_row[:], 1.0)
        dve.wait_ge(self.iotas, 4)
        dve.tensor_copy(c.iota[:], self.iota_i[:]).then_inc(self.made, 1)
        dve.tensor_copy(self.col[:], self.col_i[:]).then_inc(self.made, 1)
        dve.tensor_scalar(self.vec_hit[:], self.vec_i[:], 0.0, None, ALU.is_equal).then_inc(self.made, 1)
        dve.tensor_scalar(self.quad_ge[:], self.quad_i[:], 0.0, None, ALU.is_ge).then_inc(self.made, 1)
        dve.wait_ge(self.made, 4)
        dve.tensor_scalar(c.ident[:], c.iota[:], self.col[:, 0:1], None, ALU.is_equal)
        dve.tensor_reduce(self.vec_mask[:], self.vec_hit[:], AX.X, ALU.add).then_inc(self.made, 1)
        dve.scalar_tensor_tensor(self.quad_mask[:], self.quad_i[:], float(MUL), self.quad_ge[:],
                                 ALU.is_lt, ALU.mult).then_inc(self.made, 1)

    def scale_weights(self, dve):
        c = self.c
        dve.wait_ge(self.made, 6)
        dve.wait_ge(self.loaded, 16 * self.n_loads)
        dve.tensor_scalar(c.w_node[:, 0:MUL], self.w_f[:], self.quad_mask[:, 0:1], K_F, ALU.mult, ALU.mult)
        dve.tensor_scalar(c.w_node[:, D:D + MUL], self.w_sc[:], self.quad_mask[:, 0:1], K_F, ALU.mult, ALU.mult)
        for k in range(3):
            at = MUL * (k + 1)
            out = slice(MUL + k, D, 3)
            dve.tensor_scalar(c.w_node[:, at:at + MUL], self.w_f[:], self.vec_mask[:, k:k + 1], K_F,
                              ALU.mult, ALU.mult)
            dve.tensor_scalar(c.w_node[:, D + MUL + k:2 * D:3], self.w_sc[:], self.vec_mask[:, k:k + 1], K_F,
                              ALU.mult, ALU.mult)
            dve.tensor_scalar(c.w_ad[:, out], self.w_ad[:], self.quad_mask[:, k + 1:k + 2], K_MSG,
                              ALU.mult, ALU.mult)
            dve.tensor_scalar(c.w_bc[:, out], self.w_bc[:], self.quad_mask[:, k + 1:k + 2], K_MSG,
                              ALU.mult, ALU.mult)
        dve.tensor_scalar(c.w_ad[:, 0:MUL], self.w_ad[:], self.quad_mask[:, 0:1], K_MSG, ALU.mult, ALU.mult)
        dve.tensor_scalar(c.w_bc[:, 0:MUL], self.w_bc[:], self.quad_mask[:, 0:1], K_DOT, ALU.mult, ALU.mult)
        dve.tensor_scalar(c.w_ad[:, D:D + 1], self.l3[:, 0:1], 0.1 * K_MSG, None, ALU.mult)
        dve.tensor_scalar(c.w_bc[:, D:D + 1], self.l3[:, 1:2], 0.1 * K_DOT, None, ALU.mult)


class BoundsTable:

    def __init__(self, nc, ctx, c, dst_groups, bounds_dram, base_dram):
        self.nc = nc
        self.c, self.dst_groups, self.bounds_dram, self.base_dram = c, dst_groups, bounds_dram, base_dram

        def sb(name, shape, dt=F32):
            return ctx.enter_context(nc.sbuf_tensor(name, shape, dt))

        def sem(name):
            return ctx.enter_context(nc.semaphore(name))

        self.dst = sb("bt_dst", [P, TC, GE], I32)
        self.least = sb("bt_least", [P, TC], I32)
        self.most = sb("bt_most", [P, TC], I32)
        self.most_in = sb("bt_most_in", [P, TC], I32)
        self.most_block = sb("bt_most_block", [P, TC], I32)
        self.bounds = sb("bt_bounds", [P, TC, 2], I32)
        self.base = sb("bt_base", [P, TC])
        self.landed = sem("bt_landed")
        self.step = sem("bt_step")
        self.moved = sem("bt_moved")
        self.counts = [min(P, NG - P * i) for i in range(TC)]

    def load(self, sp):
        for i, n in enumerate(self.counts):
            sp.dma_start(self.dst[0:n, i, :], self.dst_groups[P * i:P * i + n, :]).then_inc(self.landed, 16)

    def store(self, sp):
        c = self.c
        sp.wait_ge(self.step, 7)
        with self.nc.allow_non_contiguous_dma(reason="a table of a few numbers per partition"):
            sp.dma_start(self.bounds_dram.rearrange("(c p) e -> p c e", p=P), self.bounds[:]).then_inc(self.moved, 16)
            sp.dma_start(self.base_dram.rearrange("(c p) -> p c", p=P), self.base[:]).then_inc(self.moved, 16)
        sp.wait_ge(self.moved, 32)
        sp.dma_start(c.bounds[:], self.bounds_dram.rearrange("(a g) e -> a (g e)", a=1)).then_inc(self.moved, 16)
        sp.dma_start(c.base[:], self.base_dram.partition_broadcast(P)).then_inc(self.moved, 16)
        sp.wait_ge(self.moved, 64)

    def work_out(self, dve):
        dve.memset(self.least[:], 0)
        dve.memset(self.most[:], 0).then_inc(self.step, 1)
        dve.wait_ge(self.step, 1)
        dve.wait_ge(self.landed, 16 * TC)
        for i, n in enumerate(self.counts):
            dve.tensor_reduce(self.least[0:n, i:i + 1], self.dst[0:n, i, :], AX.X, ALU.min)
            last = dve.tensor_reduce(self.most[0:n, i:i + 1], self.dst[0:n, i, :], AX.X, ALU.max)
        last.then_inc(self.step, 1)
        dve.wait_ge(self.step, 2)
        dve.tensor_scalar(self.most_in[:], self.most[:], float(NB * P - 1), None, ALU.min).then_inc(self.step, 1)
        dve.tensor_scalar(self.bounds[:, :, 0], self.least[:], 7, None, ALU.arith_shift_right).then_inc(self.step, 1)
        dve.wait_ge(self.step, 4)
        dve.tensor_scalar(self.most_block[:], self.most_in[:], 7, None, ALU.arith_shift_right).then_inc(self.step, 1)
        dve.wait_ge(self.step, 5)
        dve.tensor_scalar(self.bounds[:, :, 1], self.most_block[:], 1.0, None, ALU.add).then_inc(self.step, 1)
        dve.tensor_scalar(self.base[:], self.bounds[:, :, 0], float(P), None, ALU.mult).then_inc(self.step, 1)


def first_table(nc, c, w, x, src, dst_groups, node_vec, table, bounds_dram, base_dram):
    ctx = ExitStack()
    with ctx:
        consts = Constants(nc, ctx, c, w)
        bounds = BoundsTable(nc, ctx, c, dst_groups, bounds_dram, base_dram)

        def sb(name, shape, dt=F32):
            return ctx.enter_context(nc.sbuf_tensor(name, shape, dt))

        def sem(name):
            return ctx.enter_context(nc.semaphore(name))

        xk = sb("h_x", [P, NB, D])
        src_i = sb("h_src", [HP, HC], I32)
        part_i = sb("h_part", [HP, HC], I32)
        hi = sb("h_hi", [HP, HC], BF16)
        lo = sb("h_lo", [HP, HC], BF16)
        iota_t = sb("h_iota", [P, P, HT], BF16)
        one_hi = sb("h_one_hi", [HP, 2, NB, HT], BF16)
        one_lo = sb("h_one_lo", [HP, 2, P, HT], BF16)
        apart = sb("h_apart", [HP, 2, NB + P, HT], BF16)
        one_apart = sb("h_one_apart", [HP, 2, NB + P, HT], BF16)
        count_rows = sb("h_rows", [NB, P])
        vec_rows = sb("h_vec", [NB, P])
        degree = sb("h_degree", [P, NB])
        root = sb("h_root", [P, NB])
        counts = ctx.enter_context(nc.psum_tensor("h_counts", [NB, 512], F32))
        turned = ctx.enter_context(nc.psum_tensor("h_turned", [P, 512], F32))
        src_landed, landed, x_landed, cleared, split, hot, hot_used, rows_ready, turned_ready = [
            sem("h_" + n) for n in ("src_landed", "landed", "x_landed", "cleared", "split", "hot", "hot_used",
                                    "rows_ready", "turned_ready")]
        dout_steps, dve_scaled, pool_scaled, act_scaled, stored = [
            sem("h_" + n) for n in ("dout_steps", "dve_scaled", "pool_scaled",
                                    "act_scaled", "stored")]
        apart_ready, size_ready, apart_hot, apart_used = [
            sem("h_" + n) for n in ("apart_ready", "size_ready", "apart_hot", "apart_used")]
        XP = NB // 4
        pieces = [(i * XP, min(XP, NB - 1 - i * XP)) for i in range(-(-(NB - 1) // XP))]
        by_dve, by_pool, by_act = (0, 1, 4), (2,), (3,)

        def rows(dram, b0, k):
            return dram[b0 * P:(b0 + k) * P, :].rearrange("(s p) d -> p s d", p=P)

        with nc.Block() as block:
            @block.sync
            def _(sp):
                sp.dma_start(src_i[:], src.rearrange("(p c) -> p c", p=HP)).then_inc(src_landed, 16)
                bounds.load(sp)
                consts.load(sp)
                sp.wait_ge(cleared, 2)
                sp.dma_start(vec_rows[0:NB - 1, :],
                             node_vec[0:(NB - 1) * P, :].rearrange("(b p) e -> b (p e)", p=P)).then_inc(landed, 16)
                sp.dma_start(vec_rows[NB - 1:NB, 0:TAIL],
                             node_vec[(NB - 1) * P:N, :].rearrange("(b p) e -> b (p e)", b=1)).then_inc(landed, 16)
                for b0, k in pieces:
                    sp.dma_start(xk[:, b0:b0 + k, :], rows(x, b0, k)).then_inc(x_landed, 16)
                sp.dma_start(xk[0:TAIL, NB - 1, :], x[(NB - 1) * P:N, :]).then_inc(x_landed, 16)
                for n, (b0, k) in enumerate(pieces):
                    for by, scaled in ((by_dve, dve_scaled), (by_pool, pool_scaled), (by_act, act_scaled)):
                        if n in by:
                            sp.wait_ge(scaled, by.index(n) + 1)
                    sp.dma_start(rows(table, b0, k), xk[:, b0:b0 + k, :]).then_inc(stored, 16)
                sp.dma_start(table[(NB - 1) * P:N, :], xk[0:TAIL, NB - 1, :]).then_inc(stored, 16)
                bounds.store(sp)
                sp.wait_ge(stored, 16 * (len(pieces) + 1))

            @block.gpsimd
            def _(pool):
                consts.make_iotas(pool)
                pool.wait_ge(consts.iotas, 4)
                pool.memset(vec_rows[96:NB, :], 0.0).then_inc(cleared, 1)
                pool.wait_ge(cleared, 1)
                pool.memset(xk[:, NB - 1, :], 0.0).then_inc(cleared, 1)
                pool.wait_ge(cleared, 2)
                pool.wait_ge(split, 4)

                def difference(r, b):
                    i = r * (BY_DVE + 1) + BY_DVE
                    if later(r, 1):
                        pool.wait_ge(apart_ready, r * 2)
                    if later(r, 2):
                        pool.wait_ge(apart_hot, r - 1)
                    pool.tensor_tensor(apart[:, b, 0:NB], hi[:, None, bass.ds(i * HT, HT)].to_broadcast([HP, NB, HT]),
                                       iota_t[0:HP, 0:NB, :], ALU.subtract).then_inc(apart_ready, 1)
                    pool.tensor_tensor(apart[:, b, NB:NB + P], lo[:, None, bass.ds(i * HT, HT)].to_broadcast([HP, P, HT]),
                                       iota_t[0:HP, :, :], ALU.subtract).then_inc(apart_ready, 1)

                difference(0, 0)
                difference(1, 1)
                with pool.Fori(1, HR // 2) as h:
                    for b in range(2):
                        difference(h * 2 + b, b)
                pool.wait_ge(apart_ready, HR * 2)
                pool.wait_ge(dout_steps, 3)
                pool.wait_ge(x_landed, 16 * (len(pieces) + 1))
                for n in by_pool:
                    b0, k = pieces[n]
                    pool.tensor_tensor(xk[:, b0:b0 + k, :], xk[:, b0:b0 + k, :],
                                       c.dout[:, b0:b0 + k, None].to_broadcast([P, k, D]), ALU.mult
                                       ).then_inc(pool_scaled, 1)

            @block.vector
            def _(dve):
                consts.make_masks(dve)
                dve.tensor_copy(iota_t[:], c.iota[:, :, None].to_broadcast([P, P, HT]))
                dve.wait_ge(src_landed, 16)
                dve.tensor_scalar(part_i[:], src_i[:], 7, None, ALU.arith_shift_right).then_inc(split, 1)
                dve.wait_ge(split, 1)
                dve.tensor_copy(hi[:], part_i[:]).then_inc(split, 1)
                dve.wait_ge(split, 2)
                dve.tensor_scalar(part_i[:], src_i[:], P - 1, None, ALU.bitwise_and).then_inc(split, 1)
                dve.wait_ge(split, 3)
                dve.tensor_copy(lo[:], part_i[:]).then_inc(split, 1)
                dve.wait_ge(split, 4)

                def chunk(r, j):
                    i, n, b = r * (BY_DVE + 1) + j, r * BY_DVE + j, j % 2
                    if later(n, 2):
                        dve.wait_ge(hot_used, n - 1)
                    dve.tensor_tensor(one_hi[:, b], hi[:, None, bass.ds(i * HT, HT)].to_broadcast([HP, NB, HT]),
                                      iota_t[0:HP, 0:NB, :], ALU.is_equal)
                    dve.tensor_tensor(one_lo[:, b], lo[:, None, bass.ds(i * HT, HT)].to_broadcast([HP, P, HT]),
                                      iota_t[0:HP, :, :], ALU.is_equal).then_inc(hot, 1)

                for j in range(BY_DVE):
                    chunk(0, j)
                with dve.Fori(1, HR) as r:
                    for j in range(BY_DVE):
                        chunk(r, j)
                dve.wait_ge(hot_used, HR * BY_DVE)
                dve.wait_ge(apart_used, HR)
                dve.tensor_copy(count_rows[:], counts[:, 0:P]).then_inc(rows_ready, 1)
                dve.wait_ge(turned_ready, 1)
                dve.tensor_scalar(degree[:], turned[:, 0:NB], 1.0, None, ALU.max).then_inc(dout_steps, 1)
                dve.tensor_copy(c.node_vec[:], turned[:, P:P + NB])
                dve.wait_ge(dout_steps, 2)
                dve.reciprocal(c.dout[:], root[:]).then_inc(dout_steps, 1)
                dve.wait_ge(dout_steps, 3)
                dve.wait_ge(x_landed, 16 * (len(pieces) + 1))
                for n in by_dve:
                    b0, k = pieces[n]
                    k += b0 + k == NB - 1
                    dve.tensor_tensor(xk[:, b0:b0 + k, :], xk[:, b0:b0 + k, :],
                                      c.dout[:, b0:b0 + k, None].to_broadcast([P, k, D]), ALU.mult
                                      ).then_inc(dve_scaled, 1)
                bounds.work_out(dve)
                consts.scale_weights(dve)

            @block.scalar
            def _(act):
                def one_hot(r, b):
                    act.wait_ge(apart_ready, r * 2 + 2)
                    act.activation(apart[:, b], apart[:, b], ACT.Abs).then_inc(size_ready, 1)
                    act.wait_ge(size_ready, r + 1)
                    if later(r, 2):
                        act.wait_ge(apart_used, r - 1)
                    act.activation(one_apart[:, b], apart[:, b], ACT.Relu, bias=c.one_row[0:HP, 0:1], scale=-1.0
                                   ).then_inc(apart_hot, 1)

                one_hot(0, 0)
                one_hot(1, 1)
                with act.Fori(1, HR // 2) as h:
                    for b in range(2):
                        one_hot(h * 2 + b, b)
                act.wait_ge(dout_steps, 1)
                act.activation(root[:], degree[:], ACT.Sqrt).then_inc(dout_steps, 1)
                act.wait_ge(dout_steps, 3)
                act.wait_ge(x_landed, 16 * (len(pieces) + 1))
                for n in by_act:
                    b0, k = pieces[n]
                    for b in range(b0, b0 + k):
                        last = act.activation(xk[:, b, :], xk[:, b, :], ACT.Copy, scale=c.dout[:, b:b + 1])
                    last.then_inc(act_scaled, 1)

            @block.tensor
            def _(pe):
                def round_of(r, b, first=False, last=False):
                    for j in range(BY_DVE):
                        pe.wait_ge(hot, r * BY_DVE + (j + 1))
                        for t in range(HT):
                            mm = pe.matmul(counts[:, 0:P], one_hi[:, j % 2, :, t], one_lo[:, j % 2, :, t],
                                           start=first and j == 0 and t == 0, stop=False)
                        mm.then_inc(hot_used, 1)
                    pe.wait_ge(apart_hot, r + 1)
                    for t in range(HT):
                        mm = pe.matmul(counts[:, 0:P], one_apart[:, b, 0:NB, t], one_apart[:, b, NB:NB + P, t],
                                       start=False, stop=last and t == HT - 1)
                    mm.then_inc(apart_used, 1)

                round_of(0, 0, first=True)
                round_of(1, 1)
                with pe.Fori(1, HR // 2 - 1) as h:
                    for b in range(2):
                        round_of(h * 2 + b, b)
                round_of(HR - 2, 0)
                round_of(HR - 1, 1, last=True)
                pe.wait_ge(rows_ready, 1)
                pe.wait_ge(landed, 32)
                pe.transpose(turned[:, 0:NB], count_rows[:], c.ident[0:NB, 0:NB])
                pe.transpose(turned[:, P:P + NB], vec_rows[:], c.ident[0:NB, 0:NB]).then_inc(turned_ready, 1)


def convolve_edges(nc, c, name, table, edges, acc, degree_row):
    ctx = ExitStack()
    with ctx:
        def sb(n, shape, dt=F32):
            return ctx.enter_context(nc.sbuf_tensor(f"{name}_{n}", shape, dt))

        def ps(n, sides=1):
            return ctx.enter_context(nc.psum_tensor(f"{name}_{n}", [P, sides, 512], F32))

        def sem(n):
            return ctx.enter_context(nc.semaphore(f"{name}_{n}"))

        ends = sb("ends", [P, SLOTS, 2 * T], I32)
        rows = sb("rows", [P, SLOTS, T, D])
        rel = sb("rel", [P, T])
        hot = sb("hot", [P, 2, T, P])
        iota = ps("iota")
        sums = ps("sums", 2)
        counts = ps("counts", 2)
        ends_landed = [sem(f"ends_landed{i}") for i in range(SLOTS)]
        rows_landed = [sem(f"rows_landed{i}") for i in range(SLOTS)]
        groups_past = sem("groups_past")
        cleared = sem("cleared")
        rel_ready = sem("rel_ready")
        hot_ready = sem("hot_ready")
        sums_ready = sem("sums_ready")
        sums_added = sem("sums_added")

        with nc.Block() as block:
            @block.sync
            def _(sp):
                past_reg, landed_reg = sp.alloc_register(f"{name}_sp_past"), sp.alloc_register(f"{name}_sp_landed")

                def body(g, slot, r):
                    if later(g, SLOTS):
                        past = worked_out(sp, past_reg, g - (SLOTS - 1))
                        landed = worked_out(sp, landed_reg, r * (16 * T))
                        sp.wait_ge(groups_past, past)
                        sp.wait_ge(rows_landed[slot], landed)
                    sp.dma_start(ends[:, slot, :], edges[bass.ds(g, 1)].rearrange("a p e -> p (a e)")
                                 ).then_inc(ends_landed[slot], 16)
                split_groups(sp, body)

            @block.gpsimd
            def _(pool):
                landed_reg, past_reg = pool.alloc_register(f"{name}_pool_landed"), pool.alloc_register(f"{name}_pool_past")

                def body(g, slot, r):
                    landed = worked_out(pool, landed_reg, r * 16 + 16)
                    past = worked_out(pool, past_reg, g - (SLOTS - 2))
                    pool.wait_ge(ends_landed[0], 16)
                    pool.wait_ge(ends_landed[slot], landed)
                    if later(g, SLOTS):
                        pool.wait_ge(groups_past, past)
                    for t in range(T):
                        pool.indirect_dma_start(
                            out=rows[:, slot, t, :], out_offset=None, in_=table,
                            in_offset=bass.IndirectOffsetOnAxis(ap=ends[:, slot, t:t + 1], axis=0),
                        ).then_inc(rows_landed[slot], 16)
                split_groups(pool, body)

            @block.vector
            def _(dve):
                dve.memset(acc[:], 0.0)
                if degree_row is not None:
                    dve.memset(degree_row[:], 0.0)
                dve.memset(sums[:], 0.0)
                dve.memset(counts[:], 0.0)
                dve.tensor_copy(iota[:, 0, 0:P], c.iota[:]).then_inc(cleared, 1)
                dve.wait_ge(cleared, 1)
                visits = dve.alloc_register(f"{name}_dve_visits")
                rels = dve.alloc_register(f"{name}_dve_rels")
                before = dve.alloc_register(f"{name}_dve_before")
                side = dve.alloc_register(f"{name}_dve_side")
                side_before = dve.alloc_register(f"{name}_dve_side_before")
                bounds = Bounds(dve, name + "_dve_bound", c)
                bounds.load(0, 0)
                dve.reg_mov(visits, 0)
                dve.reg_mov(rels, 0)
                dve.reg_mov(before, NB)
                dve.reg_mov(side, 0)
                dve.reg_mov(side_before, 1)

                def add_sums():
                    at = dve.snap(before, min_val=0, max_val=NB)
                    of = dve.snap(side_before, min_val=0, max_val=1)
                    dve.wait_ge(sums_ready, visits)
                    dve.wait_ge(sums_added, visits)
                    if degree_row is not None:
                        dve.tensor_tensor(degree_row[:, at, :], degree_row[:, at, :], counts[0:1, of, 0:P], ALU.add)
                    dve.tensor_tensor(acc[:, at, :], acc[:, at, :], sums[:, of, 0:P], ALU.add
                                      ).then_inc(sums_added, 1)

                def body(g, slot, r):
                    first, past = bounds.of(slot)
                    dve.wait_ge(ends_landed[slot], r * 16 + 16)
                    dve.wait_ge(rel_ready, rels)
                    dve.tensor_scalar(rel[:], ends[:, slot, T:2 * T], c.base[:, bass.ds(g, 1)], None,
                                      ALU.subtract).then_inc(rel_ready, 1)
                    dve.reg_add(rels, rels, 1)
                    bounds.load_next(g, slot)
                    with dve.Fori(first, past) as blk:
                        to = dve.snap(side, min_val=0, max_val=1)
                        dve.wait_ge(rel_ready, rels)
                        dve.tensor_tensor(hot[:, to], iota[:, 0, None, 0:P].to_broadcast([P, T, P]),
                                          rel[:, :, None].to_broadcast([P, T, P]), ALU.is_equal
                                          ).then_inc(hot_ready, 1)
                        add_sums()
                        dve.reg_add(visits, visits, 1)
                        dve.reg_add(rels, rels, 1)
                        dve.reg_mov(before, blk)
                        dve.reg_mov(side_before, side)
                        dve.reg_mod(side, visits, 2)
                        dve.wait_ge(hot_ready, visits)
                        dve.tensor_scalar(rel[:], rel[:], float(-P), None, ALU.add).then_inc(rel_ready, 1)
                    dve.sem_inc(groups_past, 1)
                split_groups(dve, body)
                add_sums()

            @block.tensor
            def _(pe):
                visits = pe.alloc_register(f"{name}_pe_visits")
                bounds = Bounds(pe, name + "_pe_bound", c)
                bounds.load(0, 0)
                side = pe.alloc_register(f"{name}_pe_side")
                pe.reg_mov(visits, 1)
                pe.reg_mov(side, 0)

                def body(g, slot, r):
                    first, past = bounds.of(slot)
                    bounds.load_next(g, slot)
                    rows_due = pe.snap(r * (16 * T) + 16 * T)
                    with pe.Fori(first, past):
                        of = pe.snap(side, min_val=0, max_val=1)
                        pe.wait_ge(rows_landed[slot], rows_due)
                        pe.wait_ge(hot_ready, visits)
                        for t in range(T):
                            mm = pe.matmul(sums[:, of, 0:P], rows[:, slot, t, :], hot[:, of, t, :],
                                           start=t == 0, stop=t == T - 1)
                            if degree_row is not None:
                                mm = pe.matmul(counts[0:1, of, 0:P], c.one_row[:], hot[:, of, t, :],
                                               start=t == 0, stop=t == T - 1)
                        mm.then_inc(sums_ready, 1)
                        pe.reg_mod(side, visits, 2)
                        pe.reg_add(visits, visits, 1)
                split_groups(pe, body)


def inward_degrees(nc, c, degree_row, degree_dram):
    ctx = ExitStack()
    with ctx:
        rows = ctx.enter_context(nc.sbuf_tensor("i_rows", [NB, P], F32))
        degree = ctx.enter_context(nc.sbuf_tensor("i_degree", [P, NB], F32))
        root = ctx.enter_context(nc.sbuf_tensor("i_root", [P, NB], F32))
        turned = ctx.enter_context(nc.psum_tensor("i_turned", [P, 512], F32))
        stored, landed, turned_ready, degree_ready, root_ready, din_ready = [
            ctx.enter_context(nc.semaphore("i_" + n))
            for n in ("stored", "landed", "turned_ready", "degree_ready", "root_ready", "din_ready")]

        with nc.Block() as block:
            @block.sync
            def _(sp):
                sp.dma_start(degree_dram.rearrange("(a b) p -> a (b p)", a=1),
                             degree_row[0:1, 0:NB, :].rearrange("a b p -> a (b p)")).then_inc(stored, 16)
                sp.wait_ge(stored, 16)
                sp.dma_start(rows[:], degree_dram).then_inc(landed, 16)

            @block.tensor
            def _(pe):
                pe.wait_ge(landed, 16)
                pe.transpose(turned[:, 0:NB], rows[:], c.ident[0:NB, 0:NB]).then_inc(turned_ready, 1)

            @block.scalar
            def _(act):
                act.wait_ge(degree_ready, 1)
                act.activation(root[:], degree[:], ACT.Sqrt).then_inc(root_ready, 1)

            @block.vector
            def _(dve):
                dve.wait_ge(turned_ready, 1)
                dve.tensor_scalar(degree[:], turned[:, 0:NB], 1.0, None, ALU.max).then_inc(degree_ready, 1)
                dve.wait_ge(root_ready, 1)
                dve.reciprocal(c.din[:], root[:]).then_inc(din_ready, 1)
                dve.wait_ge(din_ready, 1)
                dve.tensor_tensor(c.dinout[:], c.din[:], c.dout[:], ALU.mult)


def first_nodes(nc, c, acc, table):
    ctx = ExitStack()
    with ctx:
        agg = ctx.enter_context(nc.sbuf_tensor("n1_agg", [P, 2, QB, P], F32))
        bias = ctx.enter_context(nc.sbuf_tensor("n1_bias", [P, 2, QB, D], F32))
        out = ctx.enter_context(nc.sbuf_tensor("n1_out", [P, 2, QB, D], F32))
        prod = [ctx.enter_context(nc.psum_tensor(f"n1_prod{b}", [P, QB, D], F32)) for b in range(2)]
        agg_ready, prod_ready, bias_ready, made = [
            ctx.enter_context(nc.semaphore("n1_" + n)) for n in ("agg_ready", "prod_ready", "bias_ready", "made")]
        stored = [ctx.enter_context(nc.semaphore(f"n1_stored{i}")) for i in range(2)]

        with nc.Block() as block:
            @block.gpsimd
            def _(pool):
                def body(i, b, blocks):
                    if later(i, 2):
                        pool.wait_ge(made, i - 1)
                    k = len(blocks)
                    pool.tensor_tensor(bias[:, b, 0:k], c.b1[:, None, :].to_broadcast([P, k, D]),
                                       c.dout[:, bass.ds(i * QB, k), None].to_broadcast([P, k, D]),
                                       ALU.mult).then_inc(bias_ready, 1)
                node_steps(pool, body)

            @block.scalar
            def _(act):
                def body(i, b, blocks):
                    if later(i, 2):
                        act.wait_ge(prod_ready, i - 1)
                    act.activation(agg[:, b, 0:len(blocks)], acc[:, bass.ds(i * QB, len(blocks)), :],
                                   ACT.Copy).then_inc(agg_ready, 1)
                node_steps(act, body)

            @block.tensor
            def _(pe):
                def body(i, b, blocks):
                    pe.wait_ge(agg_ready, i + 1)
                    if later(i, 2):
                        pe.wait_ge(made, i - 1)
                    for j, n in enumerate(blocks):
                        mm = pe.matmul(prod[b][0:n, j, :], agg[:, b, j, 0:n], c.w1[:], start=True, stop=True)
                    mm.then_inc(prod_ready, 1)
                node_steps(pe, body)

            @block.vector
            def _(dve):
                def body(i, b, blocks):
                    if later(i, 2):
                        dve.wait_ge(stored[b], (i - b) * 8)
                    dve.wait_ge(bias_ready, i + 1)
                    dve.wait_ge(prod_ready, i + 1)
                    for j, n in enumerate(blocks):
                        last = dve.scalar_tensor_tensor(out[0:n, b, j], prod[b][0:n, j, :],
                                                        c.dinout[0:n, bass.ds(i * QB + j, 1)], bias[0:n, b, j],
                                                        ALU.mult, ALU.add)
                    last.then_inc(made, 1)
                node_steps(dve, body)

            @block.sync
            def _(sp):
                def body(i, b, blocks):
                    sp.wait_ge(made, i + 1)
                    for p, s, rows in rows_of(table, i, blocks):
                        sp.dma_start(rows, out[p, b, s]).then_inc(stored[b], 16)
                node_steps(sp, body)
                for b in range(2):
                    sp.wait_ge(stored[b], 16 * stores_of(b))


def stores_of(b):
    steps = (NQ - b + 1) // 2
    return steps + (NB - NQ * QB if NQ % 2 == b else 0)


class Norm:

    def __init__(self, nc, ctx, name):
        sb = lambda n, shape: ctx.enter_context(nc.sbuf_tensor(name + n, shape, F32))
        self.stats = sb("stats", [P, QB, 6])
        self.mean_var = sb("mean_var", [P, 2, QB, 2])
        self.root = sb("root", [P, 2, QB])
        self.rstd = sb("rstd", [P, 2, QB])
        self.shift = sb("shift", [P, 2, QB])
        self.eps = sb("eps", [P, 1])
        self.reg = nc.vector.alloc_register(name + "stats_due")

    def semaphores(self, sem):
        self.set_up, self.stats_ready, self.var_ready, self.root_ready, self.rstd_ready, self.shift_ready = [
            sem(n) for n in ("norm_set_up", "stats_ready", "var_ready", "root_ready", "rstd_ready", "shift_ready")]

    def clear(self, dve):
        dve.memset(self.eps[:], EPS)
        dve.memset(self.mean_var[:], 0.0).then_inc(self.set_up, 1)
        dve.wait_ge(self.set_up, 1)

    def statistics(self, dve, y, i, b, blocks):
        for j, n in enumerate(blocks):
            last = dve.bn_stats(self.stats[0:n, j, :], y[0:n, j])
        last.then_inc(self.stats_ready, 1)
        due = worked_out(dve, self.reg, i + 1)
        dve.wait_ge(self.set_up, 1)
        dve.wait_ge(self.stats_ready, due)
        for j, n in enumerate(blocks):
            last = dve.bn_aggr(self.mean_var[0:n, b, j, :], self.stats[0:n, j, :])
        last.then_inc(self.var_ready, 1)

    def take_root(self, act, i, b, blocks):
        act.wait_ge(self.var_ready, i + 1)
        if later(i, 2):
            act.wait_ge(self.rstd_ready, i - 1)
        act.activation(self.root[:, b, 0:len(blocks)], self.mean_var[:, b, 0:len(blocks), 1], ACT.Sqrt,
                       bias=self.eps[:, 0:1]).then_inc(self.root_ready, 1)

    def invert_root(self, dve, i, b, blocks):
        dve.wait_ge(self.root_ready, i + 1)
        dve.reciprocal(self.rstd[:, b, 0:len(blocks)], self.root[:, b, 0:len(blocks)]).then_inc(self.rstd_ready, 1)

    def invert_and_shift(self, dve, i, b, blocks):
        self.invert_root(dve, i, b, blocks)
        dve.wait_ge(self.rstd_ready, i + 1)
        k = len(blocks)
        dve.scalar_tensor_tensor(self.shift[:, b, 0:k], self.mean_var[:, b, 0:k, 0], -1.0, self.rstd[:, b, 0:k],
                                 ALU.mult, ALU.mult).then_inc(self.shift_ready, 1)

    def apply_scaled(self, act, y, out, i, b, blocks):
        act.wait_ge(self.shift_ready, i + 1)
        for j, n in enumerate(blocks):
            last = act.activation(out[0:n, j], y[0:n, j], ACT.Identity, bias=self.shift[0:n, b, j:j + 1],
                                  scale=self.rstd[0:n, b, j:j + 1])
        return last

    def apply(self, dve, y, out, i, b, blocks):
        dve.wait_ge(self.rstd_ready, i + 1)
        for j, n in enumerate(blocks):
            last = dve.tensor_scalar(out[0:n, j], y[0:n, j], self.mean_var[0:n, b, j, 0:1], self.rstd[0:n, b, j:j + 1],
                                     ALU.subtract, ALU.mult)
        return last


def second_nodes(nc, c, x, acc, x1_dram, table, skip_dram):
    ctx = ExitStack()
    with ctx:
        def sb(n, shape):
            return ctx.enter_context(nc.sbuf_tensor("n2_" + n, shape, F32))

        def sem(n):
            return ctx.enter_context(nc.semaphore("n2_" + n))

        agg = sb("agg", [P, 2, QB, P])
        xin = sb("xin", [P, AHEAD, QB, D])
        xb = sb("xb", [P, 2, QB, D])
        y = sb("y", [P, 2, QB, D])
        x1 = sb("x1", [P, 2, QB, D])
        x1t = sb("x1t", [P, 2, QB, P])
        feat = sb("feat", [P, 2, QB, 2 * D])
        s = Norm(nc, ctx, "n2_")
        prod = [ctx.enter_context(nc.psum_tensor(f"n2_prod{b}", [P, QB, D], F32)) for b in range(2)]
        turned = ctx.enter_context(nc.psum_tensor("n2_turned", [P, QB, P], F32))
        both = [ctx.enter_context(nc.psum_tensor(f"n2_both{b}", [P, QB, 2 * D], F32)) for b in range(2)]
        agg_ready, prod_ready, xb_ready, y_ready, x1_ready, turned_ready, x1t_ready, both_ready, feat_ready, tail = [
            sem(n) for n in ("agg_ready", "prod_ready", "xb_ready", "y_ready", "x1_ready", "turned_ready",
                             "x1t_ready", "both_ready", "feat_ready", "tail")]
        s.semaphores(sem)
        landed = [sem(f"landed{i}") for i in range(AHEAD)]
        x1_stored = [sem(f"x1_stored{i}") for i in range(2)]
        feat_stored = [sem(f"feat_stored{i}") for i in range(2)]

        with nc.Block() as block:
            @block.sync
            def _(sp):
                def load(i, slot, blocks):
                    if later(i, AHEAD):
                        sp.wait_ge(xb_ready, i - (AHEAD - 1))
                    for p, sl, rows in rows_of(x, i, blocks):
                        sp.dma_start(xin[p, slot, sl], rows).then_inc(tail if blocks[-1] < P else landed[slot], 16)

                def store_x1(i, slot, blocks):
                    b = slot % 2
                    sp.wait_ge(x1_ready, i + 1)
                    for p, sl, rows in rows_of(x1_dram, i, blocks):
                        sp.dma_start(rows, x1[p, b, sl]).then_inc(x1_stored[b], 16)

                def store_features(i, slot, blocks):
                    b = slot % 2
                    sp.wait_ge(feat_ready, i + 1)
                    for dram, cols in ((table, slice(0, D)), (skip_dram, slice(D, 2 * D))):
                        for p, sl, rows in rows_of(dram, i, blocks):
                            sp.dma_start(rows, feat[p, b, sl, cols]).then_inc(feat_stored[b], 16)

                staged_steps(sp, [load, None, None, None, store_x1, None, None, store_features], AHEAD)
                for b in range(2):
                    sp.wait_ge(x1_stored[b], 16 * stores_of(b))
                    sp.wait_ge(feat_stored[b], 32 * stores_of(b))

            @block.scalar
            def _(act):
                act.wait_ge(s.set_up, 1)

                def stage_sums(i, b, blocks):
                    if later(i, 2):
                        act.wait_ge(prod_ready, i - 1)
                    act.activation(agg[:, b, 0:len(blocks)], acc[:, bass.ds(i * QB, len(blocks)), :], ACT.Copy
                                   ).then_inc(agg_ready, 1)

                def turn(i, b, blocks):
                    act.wait_ge(turned_ready, i + 1)
                    if later(i, 2):
                        act.wait_ge(both_ready, i - 1)
                    act.activation(x1t[:, b, 0:len(blocks)], turned[:, 0:len(blocks)], ACT.Copy
                                   ).then_inc(x1t_ready, 1)

                def scale_features(i, b, blocks):
                    act.wait_ge(both_ready, i + 1)
                    if later(i, 2):
                        act.wait_ge(feat_stored[b], (i - b) * 16)
                    for j, n in enumerate(blocks):
                        last = act.activation(feat[0:n, b, j], both[b][0:n, j, :], ACT.Copy,
                                              scale=c.node_vec[0:n, bass.ds(i * QB + j, 1)])
                    last.then_inc(feat_ready, 1)

                staged_steps(act, [stage_sums, lambda i, b, blocks: s.take_root(act, i, b, blocks), turn, None,
                                   scale_features])

            @block.tensor
            def _(pe):
                def convolve(i, b, blocks):
                    pe.wait_ge(agg_ready, i + 1)
                    if later(i, 2):
                        pe.wait_ge(y_ready, i - 1)
                    for j, n in enumerate(blocks):
                        mm = pe.matmul(prod[b][0:n, j, :], agg[:, b, j, 0:n], c.w2[:], start=True, stop=True)
                    mm.then_inc(prod_ready, 1)

                def turn(i, b, blocks):
                    pe.wait_ge(x1_ready, i + 1)
                    if later(i, 1):
                        pe.wait_ge(x1t_ready, i)
                    for j, n in enumerate(blocks):
                        mm = pe.transpose(turned[:, j, 0:n], x1[0:n, b, j], c.ident[0:n, 0:n])
                    mm.then_inc(turned_ready, 1)

                def features(i, b, blocks):
                    pe.wait_ge(x1t_ready, i + 1)
                    if later(i, 2):
                        pe.wait_ge(feat_ready, i - 1)
                    for j, n in enumerate(blocks):
                        mm = pe.matmul(both[b][0:n, j, :], x1t[:, b, j, 0:n], c.w_node[:], start=True, stop=True)
                    mm.then_inc(both_ready, 1)

                pe.wait_ge(s.set_up, 1)
                staged_steps(pe, [convolve, None, turn, features])

            @block.gpsimd
            def _(pool):
                def add_bias(i, slot, blocks):
                    b = slot % 2
                    if blocks[-1] < P:
                        pool.wait_ge(tail, 16 * len(blocks))
                    else:
                        pool.wait_ge(landed[slot], (i - slot) * (16 // AHEAD) + 16)
                    if later(i, 2):
                        pool.wait_ge(y_ready, i - 1)
                    if blocks[-1] == P:
                        last = pool.tensor_tensor(xb[:, b], xin[:, slot], c.b2[:, None, :].to_broadcast([P, QB, D]),
                                                  ALU.add)
                    else:
                        for j, n in enumerate(blocks):
                            last = pool.tensor_tensor(xb[0:n, b, j], xin[0:n, slot, j], c.b2[0:n], ALU.add)
                    last.then_inc(xb_ready, 1)
                staged_steps(pool, [add_bias], AHEAD)

            @block.vector
            def _(dve):
                dve.memset(turned[:], 0.0)
                s.clear(dve)

                def residual(i, b, blocks):
                    dve.wait_ge(xb_ready, i + 1)
                    dve.wait_ge(prod_ready, i + 1)
                    if later(i, 2):
                        dve.wait_ge(x1_ready, i - 1)
                    for j, n in enumerate(blocks):
                        last = dve.scalar_tensor_tensor(y[0:n, b, j], prod[b][0:n, j, :],
                                                        c.din[0:n, bass.ds(i * QB + j, 1)], xb[0:n, b, j],
                                                        ALU.mult, ALU.add)
                    last.then_inc(y_ready, 1)
                    dve.wait_ge(s.set_up, 1)
                    dve.wait_ge(y_ready, i + 1)
                    s.statistics(dve, y[:, b], i, b, blocks)

                def normalise(i, b, blocks):
                    s.invert_root(dve, i, b, blocks)
                    if later(i, 2):
                        dve.wait_ge(turned_ready, i - 1)
                        dve.wait_ge(x1_stored[b], (i - b) * 8)
                    s.apply(dve, y[:, b], x1[:, b], i, b, blocks).then_inc(x1_ready, 1)

                staged_steps(dve, [residual, normalise])


def product_edges(nc, c, table, edges, attr, scalars, acc_ad, acc_bc):
    ctx = ExitStack()
    with ctx:
        def sb(n, shape, dt=F32):
            return ctx.enter_context(nc.sbuf_tensor("t_" + n, shape, dt))

        def ps(n, shape=(P, 512)):
            return ctx.enter_context(nc.psum_tensor("t_" + n, list(shape), F32))

        def sem(n):
            return ctx.enter_context(nc.semaphore("t_" + n))

        ends = sb("ends", [P, SLOTS, 2 * T], I32)
        attrs = sb("attrs", [P, SLOTS, T, 4])
        scal = sb("scal", [P, SLOTS, T * ES])
        rows = sb("rows", [P, SLOTS, T, D])
        scal_t = sb("scal_t", [P, T // 2 * P])
        hidden = sb("hidden", [P, T // 2 * P])
        ad = sb("ad", [P, 2, T, 2 * MUL])
        cg = sb("cg", [P, T, MUL])
        ge = sb("ge", [P, T, 3, MUL])
        dot = sb("dot", [P, T, MUL])
        dot3 = sb("dot3", [P, T, MUL])
        msg_ad = sb("msg_ad", [P, 2, T, D])
        msg_bc = sb("msg_bc", [P, 2, T, D])
        rel = sb("rel", [P, T])
        hot = sb("hot", [P, 2, T, P])
        sums = ps("sums", (P, 2, 512))
        turned = ps("turned")
        layer1 = ps("layer1")
        weight = [ps(f"weight{i}", (P, T, 4 * MUL)) for i in range(2)]
        loaded = [sem(f"loaded{i}") for i in range(SLOTS)]
        rows_landed = [sem(f"rows_landed{i}") for i in range(SLOTS)]
        groups_past, cleared, rel_ready, hot_ready, sums_ready, sums_added = [
            sem(n) for n in ("groups_past", "cleared", "rel_ready", "hot_ready", "sums_ready", "sums_added")]
        turned_ready, scal_t_ready, layer1_ready, hidden_ready, weight_ready, msg_ready, chain_sem = [
            sem(n) for n in ("turned_ready", "scal_t_ready", "layer1_ready", "hidden_ready", "weight_ready",
                             "msg_ready", "chain")]
        ad_ready = sem("ad_ready")

        with nc.Block() as block:
            @block.sync
            def _(sp):
                past_reg, landed_reg = sp.alloc_register("t_sp_past"), sp.alloc_register("t_sp_landed")

                def body(g, slot, r):
                    at = g * GE if not isinstance(g, int) else min(g * GE, E - GE)
                    if later(g, SLOTS):
                        past = worked_out(sp, past_reg, g - (SLOTS - 1))
                        landed = worked_out(sp, landed_reg, r * (16 * T))
                        sp.wait_ge(turned_ready, past)
                    sp.dma_start(scal[:, slot], scalars[bass.ds(at, GE), :].rearrange("(p t) e -> p (t e)", t=T)
                                 ).then_inc(loaded[slot], 16)
                    if later(g, SLOTS):
                        sp.wait_ge(groups_past, past)
                        sp.wait_ge(rows_landed[slot], landed)
                    sp.dma_start(ends[:, slot, :], edges[bass.ds(g, 1)].rearrange("a p e -> p (a e)")
                                 ).then_inc(loaded[slot], 16)
                    if later(g, SLOTS):
                        sp.wait_ge(msg_ready, past)
                    sp.dma_start(attrs[:, slot].rearrange("p t k -> p (t k)"),
                                 attr[bass.ds(at, GE), :].rearrange("(p t) e -> p (t e)", t=T)
                                 ).then_inc(loaded[slot], 16)
                split_groups(sp, body)

            @block.gpsimd
            def _(pool):
                landed_reg, past_reg = pool.alloc_register("t_pool_landed"), pool.alloc_register("t_pool_past")

                def body(g, slot, r):
                    landed = worked_out(pool, landed_reg, r * 48 + 48)
                    past = worked_out(pool, past_reg, g - (SLOTS - 1))
                    pool.wait_ge(loaded[0], 48)
                    pool.wait_ge(loaded[slot], landed)
                    if later(g, SLOTS):
                        pool.wait_ge(msg_ready, past)
                    for t in range(T):
                        pool.indirect_dma_start(
                            out=rows[:, slot, t, :], out_offset=None, in_=table,
                            in_offset=bass.IndirectOffsetOnAxis(ap=ends[:, slot, t:t + 1], axis=0),
                        ).then_inc(rows_landed[slot], 16)
                split_groups(pool, body)

            @block.scalar
            def _(act):
                def turn(g):
                    act.wait_ge(turned_ready, g + 1)
                    if later(g, 1):
                        act.wait_ge(layer1_ready, g)
                    act.activation(scal_t[:], turned[:], ACT.Copy).then_inc(scal_t_ready, 1)

                def hide(g):
                    act.wait_ge(layer1_ready, g + 1)
                    if later(g, 1):
                        act.wait_ge(weight_ready, g)
                    act.activation(hidden[:], layer1[:], ACT.Silu, scale=0.125).then_inc(hidden_ready, 1)

                def scale_ad(g, slot, r):
                    act.wait_ge(loaded[slot], r * 48 + 48)
                    if later(g, 2):
                        act.wait_ge(msg_ready, g - 1)
                    act.wait_ge(weight_ready, g + 1)
                    for t in range(T):
                        mul = act.activation(ad[:, slot % 2, t], weight[slot % 2][:, t, 0:2 * MUL], ACT.Copy,
                                             scale=attrs[:, slot, t, 0:1])
                    mul.then_inc(ad_ready, 1)

                turn(0)
                hide(0)
                turn(1)
                scale_ad(0, 0, 0)
                hide(1)

                def body(g, slot, r):
                    if not isinstance(g, int) or g + 2 < NG:
                        turn(g + 2)
                    if not isinstance(g, int) or g + 1 < NG:
                        scale_ad(g + 1, (slot + 1) % SLOTS, r + (slot + 1) // SLOTS)
                    if not isinstance(g, int) or g + 2 < NG:
                        hide(g + 2)
                split_groups(act, body)

            @block.tensor
            def _(pe):
                visits = pe.alloc_register("t_pe_visits")
                bounds = Bounds(pe, "t_pe_bound", c)
                bounds.load(0, 0)
                side = pe.alloc_register("t_pe_side")
                pe.reg_mov(visits, 1)
                pe.reg_mov(side, 0)

                def turn(g, slot, r):
                    pe.wait_ge(loaded[slot], r * 48 + 48)
                    if later(g, 1):
                        pe.wait_ge(scal_t_ready, g)
                    for j in range(T // 2):
                        mm = pe.transpose(turned[:, j * P:(j + 1) * P], scal[:, slot, j * P:(j + 1) * P],
                                          c.ident[:])
                    mm.then_inc(turned_ready, 1)

                def layer_1(g):
                    pe.wait_ge(scal_t_ready, g + 1)
                    if later(g, 1):
                        pe.wait_ge(hidden_ready, g)
                    pe.matmul(layer1[:], c.w_fc1[:], scal_t[:], start=True, stop=True).then_inc(layer1_ready, 1)

                def layer_2(g, b):
                    pe.wait_ge(hidden_ready, g + 1)
                    if later(g, 2):
                        pe.wait_ge(msg_ready, g - 1)
                    for j in range(T // 2):
                        mm = pe.matmul(weight[b][:, 2 * j:2 * j + 2, :], hidden[:, j * P:(j + 1) * P],
                                       c.w_fc2[:], start=True, stop=True)
                    mm.then_inc(weight_ready, 1)

                turn(0, 0, 0)
                layer_1(0)
                turn(1, 1, 0)
                layer_2(0, 0)
                layer_1(1)

                def body(g, slot, r):
                    first, past = bounds.of(slot)
                    if not isinstance(g, int) or g + 2 < NG:
                        turn(g + 2, (slot + 2) % SLOTS, r + (slot + 2) // SLOTS)
                    if not isinstance(g, int) or g + 1 < NG:
                        layer_2(g + 1, (slot + 1) % 2)
                    bounds.load_next(g, slot)
                    if not isinstance(g, int) or g + 2 < NG:
                        layer_1(g + 2)
                    msg_due = pe.snap(g + 1)
                    with pe.Fori(first, past):
                        of = pe.snap(side, min_val=0, max_val=1)
                        pe.wait_ge(msg_ready, msg_due)
                        pe.wait_ge(hot_ready, visits)
                        for t in range(T):
                            pe.matmul(sums[:, of, 0:P], msg_ad[:, slot % 2, t, :], hot[:, of, t, :],
                                      start=t == 0, stop=t == T - 1)
                        for t in range(T):
                            mm = pe.matmul(sums[:, of, P:2 * P], msg_bc[:, slot % 2, t, :], hot[:, of, t, :],
                                           start=t == 0, stop=t == T - 1)
                        mm.then_inc(sums_ready, 1)
                        pe.reg_mod(side, visits, 2)
                        pe.reg_add(visits, visits, 1)
                split_groups(pe, body)

            @block.vector
            def _(dve):
                dve.memset(acc_ad[:], 0.0)
                dve.memset(acc_bc[:], 0.0)
                dve.memset(sums[:], 0.0).then_inc(cleared, 1)
                dve.wait_ge(cleared, 1)
                visits = dve.alloc_register("t_dve_visits")
                rels = dve.alloc_register("t_dve_rels")
                before = dve.alloc_register("t_dve_before")
                side = dve.alloc_register("t_dve_side")
                side_before = dve.alloc_register("t_dve_side_before")
                bounds = Bounds(dve, "t_dve_bound", c)
                bounds.load(0, 0)
                dve.reg_mov(visits, 0)
                dve.reg_mov(rels, 0)
                dve.reg_mov(before, NB)
                dve.reg_mov(side, 0)
                dve.reg_mov(side_before, 1)
                LINKS = 5

                def add_sums():
                    at = dve.snap(before, min_val=0, max_val=NB)
                    of = dve.snap(side_before, min_val=0, max_val=1)
                    dve.wait_ge(sums_ready, visits)
                    dve.wait_ge(sums_added, visits)
                    dve.tensor_tensor(acc_ad[:, at, :], acc_ad[:, at, :], sums[:, of, 0:P], ALU.add)
                    dve.tensor_tensor(acc_bc[:, at, :], acc_bc[:, at, :], sums[:, of, P:2 * P], ALU.add
                                      ).then_inc(sums_added, 1)

                def messages(g, slot, r):
                    b = slot % 2
                    w = weight[b]
                    e0 = attrs[:, slot, :, 0:1]
                    e1 = attrs[:, slot, :, 1:4]
                    g0 = rows[:, slot, :, 0:MUL]
                    g1 = rows[:, slot, :, MUL:D].rearrange("p t (k u) -> p t k u", k=3)
                    base = g * LINKS
                    wide = [P, T, 3, MUL]
                    dve.wait_ge(loaded[slot], r * 48 + 48)
                    dve.wait_ge(rows_landed[slot], r * (16 * T) + 16 * T)
                    if later(g, 1):
                        dve.wait_ge(msg_ready, g)
                    dve.tensor_tensor(ge[:], g1, e1[:, :, :, None].to_broadcast(wide), ALU.mult
                                      ).then_inc(chain_sem, 1)
                    dve.wait_ge(ad_ready, g + 1)
                    dve.tensor_tensor(cg[:], w[:, :, 2 * MUL:3 * MUL], g0, ALU.mult).then_inc(chain_sem, 1)
                    dve.tensor_tensor(msg_ad[:, b, :, MUL:D].rearrange("p t (k u) -> p t k u", k=3),
                                      ad[:, b, :, None, MUL:2 * MUL].to_broadcast(wide), g1, ALU.mult)
                    dve.tensor_tensor(msg_ad[:, b, :, 0:MUL], ad[:, b, :, 0:MUL], g0, ALU.mult
                                      ).then_inc(chain_sem, 1)
                    bounds.load_next(g, slot)
                    dve.wait_ge(chain_sem, base + 3)
                    dve.tensor_tensor(dot[:], ge[:, :, 0], ge[:, :, 1], ALU.add).then_inc(chain_sem, 1)
                    dve.tensor_tensor(msg_bc[:, b, :, MUL:D].rearrange("p t (k u) -> p t k u", k=3),
                                      cg[:, :, None, :].to_broadcast(wide),
                                      e1[:, :, :, None].to_broadcast(wide), ALU.mult)
                    dve.wait_ge(chain_sem, base + 4)
                    dve.tensor_tensor(dot3[:], dot[:], ge[:, :, 2], ALU.add).then_inc(chain_sem, 1)
                    dve.wait_ge(chain_sem, base + 5)
                    dve.tensor_tensor(msg_bc[:, b, :, 0:MUL], w[:, :, 3 * MUL:4 * MUL], dot3[:], ALU.mult
                                      ).then_inc(msg_ready, 1)

                def body(g, slot, r):
                    first, past = bounds.of(slot)
                    messages(g, slot, r)
                    dve.wait_ge(loaded[slot], r * 48 + 48)
                    dve.wait_ge(rel_ready, rels)
                    dve.tensor_scalar(rel[:], ends[:, slot, T:2 * T], c.base[:, bass.ds(g, 1)], None,
                                      ALU.subtract).then_inc(rel_ready, 1)
                    dve.reg_add(rels, rels, 1)
                    with dve.Fori(first, past) as blk:
                        to = dve.snap(side, min_val=0, max_val=1)
                        dve.wait_ge(rel_ready, rels)
                        dve.tensor_tensor(hot[:, to], c.iota[:, None, 0:P].to_broadcast([P, T, P]),
                                          rel[:, :, None].to_broadcast([P, T, P]), ALU.is_equal
                                          ).then_inc(hot_ready, 1)
                        add_sums()
                        dve.reg_add(visits, visits, 1)
                        dve.reg_add(rels, rels, 1)
                        dve.reg_mov(before, blk)
                        dve.reg_mov(side_before, side)
                        dve.reg_mod(side, visits, 2)
                        dve.wait_ge(hot_ready, visits)
                        dve.tensor_scalar(rel[:], rel[:], float(-P), None, ALU.add).then_inc(rel_ready, 1)
                    dve.sem_inc(groups_past, 1)
                split_groups(dve, body)
                add_sums()


def last_nodes(nc, c, acc_ad, acc_bc, x1_dram, skip_dram, out_dram):
    ctx = ExitStack()
    with ctx:
        def sb(n, shape):
            return ctx.enter_context(nc.sbuf_tensor("n3_" + n, shape, F32))

        def sem(n):
            return ctx.enter_context(nc.semaphore("n3_" + n))

        W = D + 1
        agg = sb("agg", [P, 2, 2, QB, P])
        x1 = sb("x1", [P, AHEAD, QB, D])
        skip = sb("skip", [P, AHEAD, QB, D])
        turned_skip = sb("turned_skip", [P, QB, D])
        mix = sb("mix", [P, 2, QB, D])
        y = sb("y", [P, AHEAD, QB, D])
        out = sb("out", [P, 2, QB, D])
        raw, angle, turns, whole, r1, r2, r3, fold, cos_arg, sin_arg, cos, sin, sin_vec = [
            sb(n, [P, NB]) for n in ("raw", "angle", "turns", "whole", "r1", "r2", "r3", "fold", "cos_arg",
                                     "sin_arg", "cos", "sin", "sin_vec")]
        s = Norm(nc, ctx, "n3_")
        conv = [ctx.enter_context(nc.psum_tensor(f"n3_conv{b}", [P, 2, 512], F32)) for b in range(2)]
        agg_ready, conv_ready, conv_kept, angles, trig_ready, mix_ready, y_ready, out_ready, tail = [
            sem(n) for n in ("agg_ready", "conv_ready", "conv_kept", "angles", "trig_ready", "mix_ready",
                             "y_ready", "out_ready", "tail")]
        skip_turned = sem("skip_turned")
        s.semaphores(sem)
        landed = [sem(f"landed{i}") for i in range(AHEAD)]
        stored = [sem(f"stored{i}") for i in range(2)]

        with nc.Block() as block:
            @block.sync
            def _(sp):
                def load(i, slot, blocks):
                    if later(i, AHEAD):
                        sp.wait_ge(mix_ready, i - (AHEAD - 1))
                    for dst, src in ((x1, x1_dram), (skip, skip_dram)):
                        for p, sl, rows in rows_of(src, i, blocks):
                            sp.dma_start(dst[p, slot, sl], rows).then_inc(tail if blocks[-1] < P else landed[slot], 16)

                def store(i, slot, blocks):
                    b = slot % 2
                    sp.wait_ge(out_ready, i + 1)
                    for p, sl, rows in rows_of(out_dram, i, blocks):
                        sp.dma_start(rows, out[p, b, sl]).then_inc(stored[b], 16)

                staged_steps(sp, [load, None, None, None, None, store], AHEAD)
                for b in range(2):
                    sp.wait_ge(stored[b], 16 * stores_of(b))

            @block.scalar
            def _(act):
                def stage_sums(i, b, blocks):
                    k = len(blocks)
                    if later(i, 2):
                        act.wait_ge(conv_ready, i - 1)
                    act.activation(agg[:, b, 0, 0:k], acc_ad[:, bass.ds(i * QB, k), :], ACT.Copy)
                    act.activation(agg[:, b, 1, 0:k], acc_bc[:, bass.ds(i * QB, k), :], ACT.Copy
                                   ).then_inc(agg_ready, 1)

                node_steps(act, stage_sums)
                act.wait_ge(angles, 9)
                act.activation(cos[:], cos_arg[:], ACT.Sin).then_inc(trig_ready, 1)
                act.activation(sin[:], sin_arg[:], ACT.Sin).then_inc(trig_ready, 1)
                act.wait_ge(s.set_up, 1)

                def normalise(i, slot, blocks):
                    b = slot % 2
                    if later(i, 2):
                        act.wait_ge(stored[b], (i - b) * 8)
                    s.apply_scaled(act, y[:, slot], out[:, b], i, b, blocks).then_inc(out_ready, 1)

                staged_steps(act, [lambda i, slot, blocks: s.take_root(act, i, slot % 2, blocks), normalise], AHEAD)

            @block.gpsimd
            def _(pool):
                pool.wait_ge(trig_ready, 2)

                def mixed(i, slot, blocks):
                    b = slot % 2
                    if blocks[-1] < P:
                        pool.wait_ge(tail, 32 * len(blocks))
                        parts = [(slice(0, n), slice(j, j + 1)) for j, n in enumerate(blocks)]
                    else:
                        pool.wait_ge(landed[slot], (i - slot) * (32 // AHEAD) + 32)
                        parts = [(slice(0, P), slice(0, QB))]
                    if later(i, 1):
                        pool.wait_ge(mix_ready, i)
                    for p, sl in parts:
                        rows, k = p.stop, sl.stop - sl.start
                        last = pool.tensor_tensor(
                            turned_skip[p, sl], skip[p, slot, sl],
                            cos[p, bass.ds(i * QB + sl.start, k), None].to_broadcast([rows, k, D]), ALU.mult)
                    last.then_inc(skip_turned, 1)
                    pool.wait_ge(skip_turned, i + 1)
                    if later(i, 2):
                        pool.wait_ge(y_ready, i - 1)
                    for p, sl in parts:
                        last = pool.tensor_tensor(mix[p, b, sl], turned_skip[p, sl], x1[p, slot, sl], ALU.add)
                    last.then_inc(mix_ready, 1)
                staged_steps(pool, [mixed], AHEAD)

            @block.tensor
            def _(pe):
                def body(i, b, blocks):
                    pe.wait_ge(agg_ready, i + 1)
                    if later(i, 2):
                        pe.wait_ge(conv_kept, i - 1)
                    for j, n in enumerate(blocks):
                        to = conv[b][0:n, j // 2, (j % 2) * W:(j % 2 + 1) * W]
                        pe.matmul(to, agg[:, b, 0, j, 0:n], c.w_ad[:], start=True, stop=False)
                        mm = pe.matmul(to, agg[:, b, 1, j, 0:n], c.w_bc[:], start=False, stop=True)
                    mm.then_inc(conv_ready, 1)
                node_steps(pe, body)

            @block.vector
            def _(dve):
                dve.memset(raw[:], 0.0)
                s.clear(dve)

                def keep(i, b, blocks):
                    dve.wait_ge(conv_ready, i + 1)
                    pairs = [(j, 2, P) for j in range(0, QB, 2)] if blocks[-1] == P else [
                        (j, 1, n) for j, n in enumerate(blocks)]
                    for j, k, n in pairs:
                        both = conv[b][0:n, j // 2, (j % 2) * W:(j % 2 + k) * W].rearrange("p (k w) -> p k w", k=k)
                        dve.tensor_copy(acc_ad[0:n, bass.ds(i * QB + j, k), :], both[:, :, 0:D])
                        last = dve.tensor_copy(raw[0:n, bass.ds(i * QB + j, k)], both[:, :, D])
                    last.then_inc(conv_kept, 1)
                node_steps(dve, keep)
                dve.wait_ge(conv_kept, NQ + 1)

                def link(n, ins):
                    ins.then_inc(angles, 1)
                    dve.wait_ge(angles, n)

                link(1, dve.tensor_tensor(angle[:], raw[:], c.node_vec[:], ALU.mult))
                link(2, dve.tensor_scalar(turns[:], angle[:], 1.0 / (2 * PI), ROUND, ALU.mult, ALU.add))
                link(3, dve.tensor_scalar(whole[:], turns[:], -ROUND, None, ALU.add))
                link(4, dve.scalar_tensor_tensor(r1[:], whole[:], -TAU_A, angle[:], ALU.mult, ALU.add))
                link(5, dve.scalar_tensor_tensor(r2[:], whole[:], -TAU_B, r1[:], ALU.mult, ALU.add))
                link(6, dve.scalar_tensor_tensor(r3[:], whole[:], -TAU_C, r2[:], ALU.mult, ALU.add))
                link(7, dve.scalar_tensor_tensor(fold[:], r3[:], -1.0, r3[:], ALU.mult, ALU.max))
                link(8, dve.tensor_scalar(cos_arg[:], fold[:], -1.0, PI / 2, ALU.mult, ALU.add))
                link(9, dve.tensor_scalar(sin_arg[:], r3[:], SINE_END, -SINE_END, ALU.min, ALU.max))
                dve.wait_ge(trig_ready, 2)
                link(10, dve.tensor_tensor(sin_vec[:], sin[:], c.node_vec[:], ALU.mult))

                def residual(i, slot, blocks):
                    b = slot % 2
                    dve.wait_ge(mix_ready, i + 1)
                    if later(i, AHEAD):
                        dve.wait_ge(out_ready, i - (AHEAD - 1))
                    for j, n in enumerate(blocks):
                        at = bass.ds(i * QB + j, 1)
                        last = dve.scalar_tensor_tensor(y[0:n, slot, j], acc_ad[0:n, at, :].rearrange("p a d -> p (a d)"),
                                                        sin_vec[0:n, at], mix[0:n, b, j], ALU.mult, ALU.add)
                    last.then_inc(y_ready, 1)
                    dve.wait_ge(s.set_up, 1)
                    dve.wait_ge(y_ready, i + 1)
                    s.statistics(dve, y[:, slot], i, b, blocks)

                def normalise(i, slot, blocks):
                    if later(i, 2):
                        dve.wait_ge(out_ready, i - 1)
                    s.invert_and_shift(dve, i, slot % 2, blocks)

                staged_steps(dve, [residual, normalise], AHEAD)


def gnn_kernel(nc, x, edges, dst_groups, src, attr, scalars, node_vec, w, out):
    def dram(name, shape, dt=F32):
        return nc.dram_tensor(name, shape, dt, kind="Internal").ap()

    bounds_dram = dram("bounds_dram", [TC * P, 2], I32)
    base_dram = dram("base_dram", [TC * P])
    degree_dram = dram("degree_dram", [NB, P])
    table_0, table_1, table_2 = (dram(f"table_{i}", [N, D]) for i in range(3))
    x1_dram = dram("x1_dram", [N, D])
    skip_dram = dram("skip_dram", [N, D])

    class Kept:
        pass

    ctx = ExitStack()
    with ctx:
        def sb(name, shape, dt=F32):
            return ctx.enter_context(nc.sbuf_tensor(name, shape, dt))

        c = Kept()
        c.iota = sb("c_iota", [P, P])
        c.ident = sb("c_ident", [P, P])
        c.one_row = sb("c_one_row", [P, 1])
        c.w1, c.w2 = sb("c_w1", [D, D]), sb("c_w2", [D, D])
        c.b1, c.b2 = sb("c_b1", [P, D]), sb("c_b2", [P, D])
        c.w_node = sb("c_w_node", [D, 2 * D])
        c.w_ad, c.w_bc = sb("c_w_ad", [P, D + 1]), sb("c_w_bc", [P, D + 1])
        c.w_fc1 = sb("c_w_fc1", [2 * ES, 2 * ES])
        c.w_fc2 = sb("c_w_fc2", [2 * ES, 2 * P])
        c.bounds = sb("c_bounds", [1, TC * P * 2], I32)
        c.base = sb("c_base", [P, TC * P])
        c.node_vec = sb("c_node_vec", [P, NB])
        c.dout, c.din, c.dinout = sb("c_dout", [P, NB]), sb("c_din", [P, NB]), sb("c_dinout", [P, NB])

        first_table(nc, c, w, x, src, dst_groups, node_vec, table_0, bounds_dram, base_dram)
        with nc.sbuf_tensor("acc_0", [D, NB + 1, P], F32) as acc:
            with nc.sbuf_tensor("degree_row", [1, NB + 1, P], F32) as degree_row:
                convolve_edges(nc, c, "c1", table_0, edges, acc, degree_row)
                inward_degrees(nc, c, degree_row, degree_dram)
            first_nodes(nc, c, acc, table_1)
            convolve_edges(nc, c, "c2", table_1, edges, acc, None)
            second_nodes(nc, c, x, acc, x1_dram, table_2, skip_dram)
        with nc.sbuf_tensor("acc_ad", [D, NB + 1, P], F32) as acc_ad, \
                nc.sbuf_tensor("acc_bc", [D, NB + 1, P], F32) as acc_bc:
            product_edges(nc, c, table_2, edges, attr, scalars, acc_ad, acc_bc)
            last_nodes(nc, c, acc_ad, acc_bc, x1_dram, skip_dram, out)


WEIGHTS = ["L0_gnn_W1", "L0_gnn_b1", "L0_gnn_W2", "L0_gnn_b2", "L1_gnn_W_sc0", "L1_gnn_W_sc1", "L1_gnn_W_l1_0",
           "L1_gnn_W_l1_1", "L1_gnn_W_fc1", "L1_gnn_W_fc2", "L1_gnn_W_l2_A0", "L1_gnn_W_l2_B0", "L1_gnn_W_l2_C1",
           "L1_gnn_W_l2_D1", "L1_gnn_W_l3_A", "L1_gnn_W_l3_B"]


def kernel(**inputs):
    import concourse.bacc as bacc
    from concourse.bass_utils import run_bass_kernel_spmd

    src, dst = np.asarray(inputs["src"]), np.asarray(inputs["dst"])
    full = (NG - 1) * GE
    repeated = full - (E - GE)
    src_groups = np.concatenate([src[:full], src[E - GE:]]).reshape(NG, P, T)
    far = np.full(repeated, FAR, dst.dtype)
    dst_groups = np.concatenate([dst[:full], far, dst[full:]]).reshape(NG, GE)
    edges = np.concatenate([src_groups, dst_groups.reshape(NG, P, T)], axis=2)

    nc = bacc.Bacc("TRN2", target_bir_lowering=False, num_devices=1)
    arrays = {}

    def given(name, a):
        a = np.ascontiguousarray(a)
        arrays[f"in_{name}"] = a
        return nc.dram_tensor(f"in_{name}", a.shape, mybir.dt.from_np(a.dtype), kind="ExternalInput").ap()

    x = given("x", inputs["x"])
    edges_d = given("edges", edges)
    dst_d = given("dst_groups", dst_groups)
    src_d = given("src", src)
    attr = given("edge_attr_4", inputs["edge_attr_4"])
    scalars = given("edge_attr_64", inputs["edge_attr_64"])
    node_vec = given("node_vec1", inputs["node_vec1"])
    w = {name: given(name, inputs[name]) for name in WEIGHTS}
    out = nc.dram_tensor("out_0", [N, D], F32, kind="ExternalOutput").ap()
    gnn_kernel(nc, x, edges_d, dst_d, src_d, attr, scalars, node_vec, w, out)
    result = run_bass_kernel_spmd(nc, [arrays], core_ids=[0])
    return result.results[0]["out_0"]
```
